# Optimizing a Trainium2 kernel written in Bass

```python
import numpy as np
import jax
import jax.numpy as jnp

def _softmax(x, axis=-1):
    return jax.nn.softmax(x, axis=axis)

def _gelu(x):
    return jax.nn.gelu(x, approximate=True)

def _silu(x):
    return jax.nn.silu(x)

def _sigmoid(x):
    return jax.nn.sigmoid(x)

def _layernorm(x, axis=-1, eps=1e-05):
    m = jnp.mean(x, axis=axis, keepdims=True)
    v = jnp.var(x, axis=axis, keepdims=True)
    return (x - m) / jnp.sqrt(v + eps)

def _scatter_add(tgt, idx, src, axis=0):
    return tgt.at[idx].add(src)

def _segment_sum(src, seg, n):
    return jax.ops.segment_sum(src, seg, n)
kernel_name = 'mk_gnn_resnorm_d4_gnn_r16_e42ae9'

def setup_inputs(seed: int=0):
    np.random.seed(seed)
    _w = jnp.asarray

    def _rec_inputs():
        import jax
        import jax.numpy as jnp
        _gk = jax.random.key(seed)
        x = -8.776e-05 + 1 * jax.random.normal(jax.random.fold_in(_gk, 1), (6250, 128), jnp.float32)
        src = jax.random.randint(jax.random.fold_in(_gk, 2), (100000,), 0, 6250, jnp.int32)
        dst = jax.random.randint(jax.random.fold_in(_gk, 3), (100000,), 0, 6250, jnp.int32)
        _o = jnp.argsort(dst, stable=True)
        src = src[_o]
        dst = dst[_o]
        edge_attr_4 = 0.0012443 + 1.0001 * jax.random.normal(jax.random.fold_in(_gk, 12), (100000, 4), jnp.float32)
        edge_attr_8 = -0.000521468 + 0.999954 * jax.random.normal(jax.random.fold_in(_gk, 13), (100000, 8), jnp.float32)
        node_vec1 = jax.random.uniform(jax.random.fold_in(_gk, 15), (6250, 1), jnp.float32, 0.0, 1)
        return (x, src, dst, edge_attr_4, edge_attr_8, node_vec1)
    x, src, dst, edge_attr_4, edge_attr_8, node_vec1 = _rec_inputs()

    def _L0_gnn_setup():
        import jax, jax.numpy as jnp
        import numpy as np
        N_NODES = 2500
        N_EDGES = 40000
        MUL = 32
        NUM_NEIGHBORS = 16.0
        SILU_NORM = 1.6791767923989418
        SQRT3 = 3.0 ** 0.5
        key = jax.random.key(seed)
        ks = jax.random.split(key, 12)
        return {'node_input': jax.random.normal(ks[0], (N_NODES, 4 * MUL), dtype=jnp.float32), 'node_attr': jnp.ones((N_NODES, 1), dtype=jnp.float32), 'edge_src': jax.random.randint(ks[1], (N_EDGES,), 0, N_NODES, dtype=jnp.int32), 'edge_dst': jax.random.randint(ks[2], (N_EDGES,), 0, N_NODES, dtype=jnp.int32), 'edge_attr': jax.random.normal(ks[3], (N_EDGES, 4), dtype=jnp.float32), 'edge_scalars': jax.random.normal(ks[4], (N_EDGES, 8), dtype=jnp.float32), 'w_lin1_s': jax.random.normal(ks[5], (MUL, MUL), dtype=jnp.float32), 'w_lin1_v': jax.random.normal(ks[6], (MUL, MUL), dtype=jnp.float32), 'fc_w1': jax.random.normal(ks[7], (8, 64), dtype=jnp.float32), 'fc_w2': jax.random.normal(ks[8], (64, 4 * MUL), dtype=jnp.float32), 'w_lin2_s': jax.random.normal(ks[9], (2 * MUL, MUL), dtype=jnp.float32), 'w_lin2_v': jax.random.normal(ks[10], (2 * MUL, MUL), dtype=jnp.float32)}
    _L0_gnn_all = _L0_gnn_setup()
    _L0_gnn_in = {k: v for k, v in _L0_gnn_all.items() if k in ('w_lin1_s', 'w_lin1_v', 'fc_w1', 'fc_w2', 'w_lin2_s', 'w_lin2_v')}
    del _L0_gnn_all

    def _L1_gnn_setup():
        import jax, jax.numpy as jnp
        import numpy as np
        N, E = (6250, 100000)
        IN_DIM, HID, OUT_DIM = (128, 256, 128)
        LN_EPS = 1e-05

        def _gcn_norm(edge_index, n_nodes):
            loops = jnp.arange(n_nodes, dtype=edge_index.dtype)
            src = jnp.concatenate([edge_index[0], loops])
            dst = jnp.concatenate([edge_index[1], loops])
            deg = jax.ops.segment_sum(jnp.ones_like(dst, dtype=jnp.float32), dst, num_segments=n_nodes)
            dinv = jnp.where(deg > 0, jax.lax.rsqrt(deg), 0.0)
            norm = dinv[src] * dinv[dst]
            return (src, dst, norm)

        def _gcn_conv(x, W, b, src, dst, norm, n_nodes):
            h = x @ W
            msg = h[src] * norm[:, None]
            out = jax.ops.segment_sum(msg, dst, num_segments=n_nodes)
            return out + b

        def _layernorm(x, g, b):
            mu = jnp.mean(x, axis=-1, keepdims=True)
            var = jnp.mean(jnp.square(x - mu), axis=-1, keepdims=True)
            return (x - mu) * jax.lax.rsqrt(var + LN_EPS) * g + b
        key = jax.random.key(seed)
        ks = jax.random.split(key, 16)
        inp = {'x': jax.random.normal(ks[0], (N, IN_DIM), dtype=jnp.float32), 'edge_index': jax.random.randint(ks[1], (2, E), 0, N, dtype=jnp.int32), 'W0': jax.random.normal(ks[2], (IN_DIM, HID), dtype=jnp.float32) * 0.05, 'b0': jnp.zeros((HID,), dtype=jnp.float32), 'W1': jax.random.normal(ks[3], (HID, HID), dtype=jnp.float32) * 0.05, 'b1': jnp.zeros((HID,), dtype=jnp.float32), 'W2': jax.random.normal(ks[4], (HID, HID), dtype=jnp.float32) * 0.05, 'b2': jnp.zeros((HID,), dtype=jnp.float32), 'W3': jax.random.normal(ks[5], (HID, OUT_DIM), dtype=jnp.float32) * 0.05, 'b3': jnp.zeros((OUT_DIM,), dtype=jnp.float32), 'a0': jnp.ones((1,), dtype=jnp.float32), 'a1': jnp.ones((1,), dtype=jnp.float32), 'a2': jnp.ones((1,), dtype=jnp.float32), 'g0': jnp.ones((HID,), dtype=jnp.float32), 'beta0': jnp.zeros((HID,), dtype=jnp.float32), 'g1': jnp.ones((HID,), dtype=jnp.float32), 'beta1': jnp.zeros((HID,), dtype=jnp.float32), 'g2': jnp.ones((HID,), dtype=jnp.float32), 'beta2': jnp.zeros((HID,), dtype=jnp.float32)}
        return inp
    _L1_gnn_all = _L1_gnn_setup()
    _L1_gnn_in = {k: v for k, v in _L1_gnn_all.items() if k in ('W0', 'b0', 'W1', 'b1', 'W2', 'b2', 'W3', 'b3', 'a0', 'a1', 'a2', 'g0', 'beta0', 'g1', 'beta1', 'g2', 'beta2')}
    del _L1_gnn_all

    def _L2_gnn_setup():
        import jax, jax.numpy as jnp
        import numpy as np
        N_NODES = 6250
        N_EDGES = 100000
        HIDDEN = 128
        key = jax.random.key(seed)
        ks = jax.random.split(key, 7)
        s = 1.0 / np.sqrt(HIDDEN)
        user_states = jax.random.normal(ks[0], (N_NODES, HIDDEN), dtype=jnp.float32)
        edge_src = jax.random.randint(ks[1], (N_EDGES,), 0, N_NODES)
        edge_dst = jax.random.randint(ks[2], (N_EDGES,), 0, N_NODES)
        W_self = jax.random.uniform(ks[3], (HIDDEN, HIDDEN), minval=-s, maxval=s, dtype=jnp.float32)
        b_self = jax.random.uniform(ks[4], (HIDDEN,), minval=-s, maxval=s, dtype=jnp.float32)
        W_neigh = jax.random.uniform(ks[5], (HIDDEN, HIDDEN), minval=-s, maxval=s, dtype=jnp.float32)
        b_neigh = jax.random.uniform(ks[6], (HIDDEN,), minval=-s, maxval=s, dtype=jnp.float32)
        return {'user_states': user_states, 'edge_src': edge_src, 'edge_dst': edge_dst, 'W_self': W_self, 'b_self': b_self, 'W_neigh': W_neigh, 'b_neigh': b_neigh}
    _L2_gnn_all = _L2_gnn_setup()
    _L2_gnn_in = {k: v for k, v in _L2_gnn_all.items() if k in ('W_self', 'b_self', 'W_neigh', 'b_neigh')}
    del _L2_gnn_all

    def _L3_gnn_setup():
        import jax, jax.numpy as jnp
        import numpy as np
        N_NODES = 3125
        N_EDGES = 50000
        HEADS = 2
        HID = 64
        NEG_SLOPE = 0.2

        def gat_prelu(x, W_src, W_dst, att_src, att_dst, bias, prelu_w, edge_index):
            N = x.shape[0]
            src, dst = (edge_index[0], edge_index[1])
            xs = (x @ W_src).reshape(N, HEADS, HID)
            xd = (x @ W_dst).reshape(N, HEADS, HID)
            a_src = jnp.einsum('nhc,hc->nh', xs, att_src)
            a_dst = jnp.einsum('nhc,hc->nh', xd, att_dst)
            e = jax.nn.leaky_relu(a_src[src] + a_dst[dst], NEG_SLOPE)
            m = jax.ops.segment_max(e, dst, num_segments=N)
            ee = jnp.exp(e - m[dst])
            denom = jax.ops.segment_sum(ee, dst, num_segments=N)
            alpha = ee / (denom[dst] + 1e-16)
            msg = xs[src] * alpha[:, :, None]
            out = jax.ops.segment_sum(msg, dst, num_segments=N)
            out = out.reshape(N, HEADS * HID) + bias
            return jnp.where(out >= 0, out, prelu_w * out)
        key = jax.random.key(seed)
        ks = jax.random.split(key, 8)
        x = jax.random.normal(ks[0], (N_NODES, 128), dtype=jnp.float32)
        W_src = jax.random.normal(ks[1], (128, HEADS * HID), dtype=jnp.float32) * (1.0 / np.sqrt(128))
        W_dst = jax.random.normal(ks[2], (128, HEADS * HID), dtype=jnp.float32) * (1.0 / np.sqrt(128))
        att_src = jax.random.normal(ks[3], (HEADS, HID), dtype=jnp.float32) * 0.1
        att_dst = jax.random.normal(ks[4], (HEADS, HID), dtype=jnp.float32) * 0.1
        bias = jax.random.normal(ks[5], (HEADS * HID,), dtype=jnp.float32) * 0.01
        prelu_w = jnp.full((HEADS * HID,), 0.25, dtype=jnp.float32)
        edge_index = jax.random.randint(ks[6], (2, N_EDGES), 0, N_NODES, dtype=jnp.int64)
        return {'x': x, 'W_src': W_src, 'W_dst': W_dst, 'att_src': att_src, 'att_dst': att_dst, 'bias': bias, 'prelu_w': prelu_w, 'edge_index': edge_index}
    _L3_gnn_all = _L3_gnn_setup()
    _L3_gnn_in = {k: v for k, v in _L3_gnn_all.items() if k in ('W_src', 'W_dst', 'att_src', 'att_dst', 'bias', 'prelu_w')}
    del _L3_gnn_all
    return {'x': x, 'src': src, 'dst': dst, 'edge_attr_4': edge_attr_4, 'edge_attr_8': edge_attr_8, 'node_vec1': node_vec1, 'L0_gnn_w_lin1_s': _L0_gnn_in['w_lin1_s'], 'L0_gnn_w_lin1_v': _L0_gnn_in['w_lin1_v'], 'L0_gnn_fc_w1': _L0_gnn_in['fc_w1'], 'L0_gnn_fc_w2': _L0_gnn_in['fc_w2'], 'L0_gnn_w_lin2_s': _L0_gnn_in['w_lin2_s'], 'L0_gnn_w_lin2_v': _L0_gnn_in['w_lin2_v'], 'L1_gnn_W0': _L1_gnn_in['W0'], 'L1_gnn_b0': _L1_gnn_in['b0'], 'L1_gnn_W1': _L1_gnn_in['W1'], 'L1_gnn_b1': _L1_gnn_in['b1'], 'L1_gnn_W2': _L1_gnn_in['W2'], 'L1_gnn_b2': _L1_gnn_in['b2'], 'L1_gnn_W3': _L1_gnn_in['W3'], 'L1_gnn_b3': _L1_gnn_in['b3'], 'L1_gnn_a0': _L1_gnn_in['a0'], 'L1_gnn_a1': _L1_gnn_in['a1'], 'L1_gnn_a2': _L1_gnn_in['a2'], 'L1_gnn_g0': _L1_gnn_in['g0'], 'L1_gnn_beta0': _L1_gnn_in['beta0'], 'L1_gnn_g1': _L1_gnn_in['g1'], 'L1_gnn_beta1': _L1_gnn_in['beta1'], 'L1_gnn_g2': _L1_gnn_in['g2'], 'L1_gnn_beta2': _L1_gnn_in['beta2'], 'L2_gnn_W_self': _L2_gnn_in['W_self'], 'L2_gnn_b_self': _L2_gnn_in['b_self'], 'L2_gnn_W_neigh': _L2_gnn_in['W_neigh'], 'L2_gnn_b_neigh': _L2_gnn_in['b_neigh'], 'L3_gnn_W_src': _L3_gnn_in['W_src'], 'L3_gnn_W_dst': _L3_gnn_in['W_dst'], 'L3_gnn_att_src': _L3_gnn_in['att_src'], 'L3_gnn_att_dst': _L3_gnn_in['att_dst'], 'L3_gnn_bias': _L3_gnn_in['bias'], 'L3_gnn_prelu_w': _L3_gnn_in['prelu_w']}

def reference(x, src, dst, edge_attr_4, edge_attr_8, node_vec1, L0_gnn_w_lin1_s, L0_gnn_w_lin1_v, L0_gnn_fc_w1, L0_gnn_fc_w2, L0_gnn_w_lin2_s, L0_gnn_w_lin2_v, L1_gnn_W0, L1_gnn_b0, L1_gnn_W1, L1_gnn_b1, L1_gnn_W2, L1_gnn_b2, L1_gnn_W3, L1_gnn_b3, L1_gnn_a0, L1_gnn_a1, L1_gnn_a2, L1_gnn_g0, L1_gnn_beta0, L1_gnn_g1, L1_gnn_beta1, L1_gnn_g2, L1_gnn_beta2, L2_gnn_W_self, L2_gnn_b_self, L2_gnn_W_neigh, L2_gnn_b_neigh, L3_gnn_W_src, L3_gnn_W_dst, L3_gnn_att_src, L3_gnn_att_dst, L3_gnn_bias, L3_gnn_prelu_w):
    import jax
    import jax.numpy as jnp

    def _L0_gnn_ref(node_input, node_attr, edge_src, edge_dst, edge_attr, edge_scalars, w_lin1_s, w_lin1_v, fc_w1, fc_w2, w_lin2_s, w_lin2_v):
        import jax, jax.numpy as jnp
        import numpy as np
        N_NODES = 2500
        N_EDGES = 40000
        MUL = 32
        NUM_NEIGHBORS = 16.0
        SILU_NORM = 1.6791767923989418
        SQRT3 = 3.0 ** 0.5
        N = node_input.shape[0]
        s = node_input[:, :MUL]
        v = node_input[:, MUL:].reshape(N, MUL, 3)
        s = s @ (w_lin1_s / jnp.sqrt(jnp.float32(MUL)))
        v = jnp.einsum('nui,uw->nwi', v, w_lin1_v / jnp.sqrt(jnp.float32(MUL)))
        h = jax.nn.silu(edge_scalars @ (fc_w1 / jnp.sqrt(jnp.float32(fc_w1.shape[0])))) * SILU_NORM
        w = h @ (fc_w2 / jnp.sqrt(jnp.float32(fc_w2.shape[0])))
        w0 = w[:, 0 * MUL:1 * MUL]
        w1 = w[:, 1 * MUL:2 * MUL]
        w2 = w[:, 2 * MUL:3 * MUL]
        w3 = w[:, 3 * MUL:4 * MUL]
        se = s[edge_src]
        ve = v[edge_src]
        es = edge_attr[:, :1]
        ev = edge_attr[:, 1:4]
        mid_s0 = w0 * se * es
        mid_s1 = w3 * jnp.einsum('eui,ei->eu', ve, ev) / SQRT3
        mid_v0 = (w1 * se)[:, :, None] * ev[:, None, :]
        mid_v1 = (w2 * es)[:, :, None] * ve
        mid_scal = jnp.concatenate([mid_s0, mid_s1], axis=1)
        mid_vec = jnp.concatenate([mid_v0, mid_v1], axis=1)
        inv = 1.0 / jnp.sqrt(jnp.float32(NUM_NEIGHBORS))
        ns = jax.ops.segment_sum(mid_scal, edge_dst, num_segments=N) * inv
        nv = jax.ops.segment_sum(mid_vec, edge_dst, num_segments=N) * inv
        fan = jnp.sqrt(jnp.float32(2 * MUL))
        out_s = ns @ (w_lin2_s / fan)
        out_v = jnp.einsum('nui,uw->nwi', nv, w_lin2_v / fan)
        return jnp.concatenate([out_s, out_v.reshape(N, -1)], axis=1)

    def _L1_gnn_ref(x, edge_index, W0, b0, W1, b1, W2, b2, W3, b3, a0, a1, a2, g0, beta0, g1, beta1, g2, beta2):
        import jax, jax.numpy as jnp
        import numpy as np
        N, E = (6250, 100000)
        IN_DIM, HID, OUT_DIM = (128, 256, 128)
        LN_EPS = 1e-05

        def _gcn_norm(edge_index, n_nodes):
            loops = jnp.arange(n_nodes, dtype=edge_index.dtype)
            src = jnp.concatenate([edge_index[0], loops])
            dst = jnp.concatenate([edge_index[1], loops])
            deg = jax.ops.segment_sum(jnp.ones_like(dst, dtype=jnp.float32), dst, num_segments=n_nodes)
            dinv = jnp.where(deg > 0, jax.lax.rsqrt(deg), 0.0)
            norm = dinv[src] * dinv[dst]
            return (src, dst, norm)

        def _gcn_conv(x, W, b, src, dst, norm, n_nodes):
            h = x @ W
            msg = h[src] * norm[:, None]
            out = jax.ops.segment_sum(msg, dst, num_segments=n_nodes)
            return out + b

        def _layernorm(x, g, b):
            mu = jnp.mean(x, axis=-1, keepdims=True)
            var = jnp.mean(jnp.square(x - mu), axis=-1, keepdims=True)
            return (x - mu) * jax.lax.rsqrt(var + LN_EPS) * g + b
        n_nodes = x.shape[0]
        src, dst, norm = _gcn_norm(edge_index, n_nodes)
        layers = [(W0, b0, a0, g0, beta0), (W1, b1, a1, g1, beta1), (W2, b2, a2, g2, beta2)]
        h = x
        for W, b, a, g, beta in layers:
            c = _gcn_conv(h, W, b, src, dst, norm, n_nodes)
            c = c * jax.nn.sigmoid(a)
            c = _layernorm(c, g, beta)
            h = jax.nn.elu(c)
        return _gcn_conv(h, W3, b3, src, dst, norm, n_nodes)

    def _L2_gnn_ref(user_states, edge_src, edge_dst, W_self, b_self, W_neigh, b_neigh):
        import jax, jax.numpy as jnp
        import numpy as np
        N_NODES = 6250
        N_EDGES = 100000
        HIDDEN = 128
        n = user_states.shape[0]
        neigh_sum = jax.ops.segment_sum(user_states[edge_dst], edge_src, num_segments=n)
        counts = jax.ops.segment_sum(jnp.ones((edge_src.shape[0],), dtype=user_states.dtype), edge_src, num_segments=n)
        neigh_mean = neigh_sum / jnp.maximum(counts, 1.0)[:, None]
        neigh_msg = neigh_mean @ W_neigh.T + b_neigh
        neigh_msg = jnp.where(counts[:, None] > 0, neigh_msg, jnp.zeros_like(neigh_msg))
        self_msg = user_states @ W_self.T + b_self
        return jax.nn.relu(self_msg + neigh_msg)

    def _L3_gnn_ref(x, W_src, W_dst, att_src, att_dst, bias, prelu_w, edge_index):
        import jax, jax.numpy as jnp
        import numpy as np
        N_NODES = 3125
        N_EDGES = 50000
        HEADS = 2
        HID = 64
        NEG_SLOPE = 0.2

        def gat_prelu(x, W_src, W_dst, att_src, att_dst, bias, prelu_w, edge_index):
            N = x.shape[0]
            src, dst = (edge_index[0], edge_index[1])
            xs = (x @ W_src).reshape(N, HEADS, HID)
            xd = (x @ W_dst).reshape(N, HEADS, HID)
            a_src = jnp.einsum('nhc,hc->nh', xs, att_src)
            a_dst = jnp.einsum('nhc,hc->nh', xd, att_dst)
            e = jax.nn.leaky_relu(a_src[src] + a_dst[dst], NEG_SLOPE)
            m = jax.ops.segment_max(e, dst, num_segments=N)
            ee = jnp.exp(e - m[dst])
            denom = jax.ops.segment_sum(ee, dst, num_segments=N)
            alpha = ee / (denom[dst] + 1e-16)
            msg = xs[src] * alpha[:, :, None]
            out = jax.ops.segment_sum(msg, dst, num_segments=N)
            out = out.reshape(N, HEADS * HID) + bias
            return jnp.where(out >= 0, out, prelu_w * out)
        return gat_prelu(x, W_src, W_dst, att_src, att_dst, bias, prelu_w, edge_index)
    edge_index = jnp.stack([src, dst])
    x = _layernorm(x + _L0_gnn_ref(x, node_vec1, src, dst, edge_attr_4, edge_attr_8, L0_gnn_w_lin1_s, L0_gnn_w_lin1_v, L0_gnn_fc_w1, L0_gnn_fc_w2, L0_gnn_w_lin2_s, L0_gnn_w_lin2_v), axis=-1)
    x = _layernorm(x + _L1_gnn_ref(x, edge_index, L1_gnn_W0, L1_gnn_b0, L1_gnn_W1, L1_gnn_b1, L1_gnn_W2, L1_gnn_b2, L1_gnn_W3, L1_gnn_b3, L1_gnn_a0, L1_gnn_a1, L1_gnn_a2, L1_gnn_g0, L1_gnn_beta0, L1_gnn_g1, L1_gnn_beta1, L1_gnn_g2, L1_gnn_beta2), axis=-1)
    x = _layernorm(x + _L2_gnn_ref(x, src, dst, L2_gnn_W_self, L2_gnn_b_self, L2_gnn_W_neigh, L2_gnn_b_neigh), axis=-1)
    x = _layernorm(x + _L3_gnn_ref(x, L3_gnn_W_src, L3_gnn_W_dst, L3_gnn_att_src, L3_gnn_att_dst, L3_gnn_bias, L3_gnn_prelu_w, edge_index), axis=-1)
    return x

_drawn_inputs = setup_inputs


def setup_inputs(seed=0):
    import zlib

    import numpy as np

    out = dict(_drawn_inputs(seed))
    spreads = {'L1_gnn_b0': (0.0, 0.1),
     'L1_gnn_b1': (0.0, 0.1),
     'L1_gnn_b2': (0.0, 0.1),
     'L1_gnn_b3': (0.0, 0.1),
     'L1_gnn_g0': (1.0, 0.2),
     'L1_gnn_beta0': (0.0, 0.1),
     'L1_gnn_g1': (1.0, 0.2),
     'L1_gnn_beta1': (0.0, 0.1),
     'L1_gnn_g2': (1.0, 0.2),
     'L1_gnn_beta2': (0.0, 0.1),
     'L3_gnn_prelu_w': (0.25, 0.6)}
    factors = {'L3_gnn_bias': 8.0}
    for name, (base, spread) in spreads.items():
        noise = np.random.default_rng([zlib.crc32(name.encode()), seed]).standard_normal(out[name].shape)
        drawn = base * np.exp(spread * noise) if base else spread * noise
        out[name] = jnp.asarray(drawn.astype(out[name].dtype))
    for name, factor in factors.items():
        out[name] = (out[name] * factor).astype(out[name].dtype)
    return out
```

```python
import numpy as np
import concourse.bass as bass
from concourse import mybir
from contextlib import ExitStack

F32 = mybir.dt.float32
I32 = mybir.dt.int32
U32 = mybir.dt.uint32
ALU = mybir.AluOpType
ACT = mybir.ActivationFunctionType
AX = mybir.AxisListType

P = 128
N = 6250
E = 100000
D = 128
HID = 256
MUL = 32
NT = -(-N // P)
NB = NT + 1
LASTN = N - (NT - 1) * P
TC = -(-E // P)
TAIL = E - (TC - 1) * P
PADKEY = NT * P
G8 = 8
NG = 104
NCH = NG * G8
assert NCH >= (TC * P + NB * (P - 1)) // P
SCG = TC // G8
REST = TC - SCG * G8
PW = 136
EV, SRC, LO = 128, 131, 132
AW = 260
GW = 260
EPS = 1e-5
SILU_NORM = 1.6791767923989418
NEG = -3.0e38
SEGT = 5
NSEG = NB // SEGT
HEADS, CH = 2, 64
SLOPE = 0.2


class Count:

    def __init__(self, sem):
        self.sem, self.n = sem, 0


class Steps:

    def __init__(self, eng, count):
        self.eng, self.c, self.turn, self.per, self.k = eng, count, None, 0, 0

    def loop(self, turn, per):
        self.turn, self.per, self.k = turn, per, 0

    def end(self, turns):
        assert self.k == self.per, (self.k, self.per)
        self.c.n += turns * self.per
        self.turn = None

    def __call__(self, ins):
        ins.then_inc(self.c.sem, 1)
        if self.turn is None:
            self.c.n += 1
        else:
            self.k += 1
        return self

    def reached(self):
        return self.c.n if self.turn is None else self.turn * self.per + (self.c.n + self.k)

    def wait(self):
        self.eng.wait_ge(self.c.sem, self.reached())


class Chip:

    def __init__(self, nc, ctx):
        self.nc, self.ctx = nc, ctx
        sb = self.sb
        self.ps = ctx.enter_context(nc.psum_tensor("ps", [P, 8, 512], F32))
        self.ident = sb("ident", [P, P])
        self.ones = sb("ones", [P, P])
        self.upper = sb("upper", [P, P])
        self.iota = sb("iota", [P, P])
        self.iota_b = sb("iota_b", [P, NB])
        self.eps = sb("eps", [P, 1])
        self.x = sb("x", [P, NB, D])
        self.acc = sb("acc", [P, NB, AW])
        self.mv = sb("mv", [P, NB, 2])
        self.rstd = sb("rstd", [P, NB])
        self.dinv = sb("dinv", [P, NB])
        self.meta = {k: sb(f"meta_{k}", [P, NCH, 2]) for k in ("dst", "src")}
        self.bin_of = {k: sb(f"bin_of_{k}", [1, NCH], I32) for k in ("dst", "src")}
        self.idx = sb("idx", [P, 2, G8], I32)
        self.rows = sb("rows", [P, 2, G8, GW])
        self.hot = sb("hot", [P, 2, G8, P])
        self.pay = sb("pay", [P, 2, G8, PW])
        self.iota_c = self.hot[0:64, 0, :, :].rearrange("p j n -> p (j n)")[:, 0:NCH]
        sem = self.sem
        self.ready = sem("constants_ready")
        self.held = sem("held")
        self.dve = sem("dve_step")
        self.pool = sem("pool_step")
        self.act = sem("act_step")
        self.load = sem("load_done")
        self.store = sem("store_done")
        self.idx_ready = sem("indices_ready")
        self.gathered = [sem(f"gathered_{h}") for h in range(2)]
        self.scattered = [sem(f"scattered_{h}") for h in range(2)]
        self.hot_ready = sem("one_hot_ready")
        self.mm = sem("chunk_multiplied")
        self.added = sem("chunk_added")

    def sb(self, name, shape, dt=F32):
        return self.ctx.enter_context(self.nc.sbuf_tensor(name, shape, dt))

    def sem(self, name):
        return Count(self.ctx.enter_context(self.nc.semaphore(name)))

    def hold(self, eng, count, value):
        eng.wait_ge(count.sem, value)
        eng.sem_inc(self.held.sem, 1)


def tiles(ap, n, width):
    return ap.rearrange("(n p) f -> p n f", p=P)


def setup(c, A, s):
    nc = c.nc
    with nc.Block() as block:

        @block.gpsimd
        def _(pool):
            st = Steps(pool, c.pool)
            st(pool.memset(c.ident[:, :], 0.0))
            st(pool.memset(c.ones[:, :], 1.0))
            st(pool.memset(c.upper[:, :], 0.0))
            st.wait()
            pool.affine_select(out=c.ident[:, :], in_=c.ident[:, :], compare_op=ALU.not_equal, fill=1.0,
                               base=0, pattern=[[-1, P]], channel_multiplier=1)
            pool.affine_select(out=c.upper[:, :], in_=c.upper[:, :], compare_op=ALU.is_ge, fill=1.0,
                               base=0, pattern=[[-1, P]], channel_multiplier=1)
            pool.iota(c.iota[:, :], pattern=[[1, P]], base=0, channel_multiplier=0,
                      allow_small_or_imprecise_dtypes=True)
            pool.iota(c.iota_b[:, :], pattern=[[1, NB]], base=0, channel_multiplier=0,
                      allow_small_or_imprecise_dtypes=True)
            pool.iota(c.iota_c[:, :], pattern=[[1, NCH]], base=0, channel_multiplier=0,
                      allow_small_or_imprecise_dtypes=True)
            pool.memset(c.eps[:, :], EPS).then_inc(c.ready.sem, 1)

        @block.vector
        def _(dve):
            st = Steps(dve, c.dve)
            st(dve.memset(s.key["dst"][:, :], PADKEY))
            st(dve.memset(s.key["src"][:, :], PADKEY))
            st(dve.memset(s.attr[:, :, :], 0.0))
            st(dve.memset(c.x[:, NT - 1:NB, :], 0.0))
            st(dve.memset(s.lin1[:, :], 0.0))
            st(dve.memset(s.one_row[:, :], 1.0))
            st(dve.memset(s.pos["dst"][:, :], 0.0))
            st(dve.memset(s.pos["src"][:, :], 0.0))
            st(dve.memset(c.pay[:, :, :, :], 0.0))
            for k in ("dst", "src"):
                st(dve.memset(c.meta[k][:, :, 0], 0.0))
                st(dve.memset(c.meta[k][:, :, 1], -1.0))
            st(dve.memset(c.rows[:, :, :, :], 1.0))
            st.wait()
            st(dve.memset(c.pay[:, :, :, LO], -1.0))

        @block.sync
        def _(sp):
            sp.wait_ge(c.dve.sem, 15)
            n = 0
            for k in ("dst", "src"):
                sp.dma_start(s.key[k][:, 0:TC - 1], A[k + "_main"]).then_inc(c.load.sem, 16)
                sp.dma_start(s.key[k][0:TAIL, TC - 1:TC], A[k + "_tail"]).then_inc(c.load.sem, 16)
                n += 2
            sp.dma_start(s.attr[:, 0:TC - 1, :], A["ea4_main"]).then_inc(c.load.sem, 16)
            sp.dma_start(s.attr[0:TAIL, TC - 1, :], A["ea4_tail"]).then_inc(c.load.sem, 16)
            sp.dma_start(c.x[:, 0:NT - 1, :], tiles(A["x"][0:(NT - 1) * P, :], NT - 1, D)).then_inc(c.load.sem, 16)
            sp.dma_start(c.x[0:LASTN, NT - 1, :], A["x"][(NT - 1) * P:N, :]).then_inc(c.load.sem, 16)
            n += 4
            for dst, src in s.weights:
                sp.dma_start(dst, src).then_inc(c.load.sem, 16)
                n += 1
            sp.dma_start(s.src_rows.rearrange("(p j) w -> p j w", p=P), c.meta["src"][:, :, :]).then_inc(c.store.sem, 16)
            sp.wait_ge(c.load.sem, 16 * n)
            s.n_loads = n
            sp.wait_ge(c.store.sem, 16)

        @block.scalar
        def _(act):
            act.wait_ge(c.dve.sem, 15)
            width = 2 * G8 * PW
            view = s.dst_rows.rearrange("(p j) w -> p (j w)", p=P)
            src = c.pay[:, :, :, :].rearrange("p h g w -> p (h g w)")
            with act.Fori(0, NG // 2) as i:
                act.dma_start(view[:, bass.ds(i * width, width)], src).then_inc(s.prefilled.sem, 16)
    c.ready.n = 1
    c.pool.n = 3
    c.load.n = 16 * s.n_loads
    c.store.n = 16
    s.prefilled.n = 16 * (NG // 2)


def sort_key(c, s, k):
    nc = c.nc
    key, binf, lof, mask, run, pos = s.key[k], s.binf, s.lof[k], s.mask, s.run, s.pos[k]
    cnt, base = s.cnt, s.base[k]
    if k == "dst":
        s.lo_done = True
    with nc.Block() as block:

        @block.vector
        def _(dve):
            st = Steps(dve, c.dve)
            st(dve.tensor_scalar(s.ki[:, :], key[:, :], 7, None, ALU.arith_shift_right))
            st(dve.tensor_scalar(s.kl[:, :], key[:, :], P - 1, None, ALU.bitwise_and)).wait()
            st(dve.tensor_copy(binf[:, :], s.ki[:, :]))
            st(dve.tensor_copy(lof, s.kl[:, :])).wait()
            with dve.Fori(0, NB) as b:
                st.loop(b, 2)
                st(dve.tensor_scalar(mask[:, :], binf[:, :], c.iota_b[:, bass.ds(b, 1)], None, ALU.is_equal)).wait()
                st(dve.tensor_reduce(cnt[:, bass.ds(b, 1)], mask[:, :], AX.X, ALU.add)).wait()
            st.end(NB)
            dve.wait_ge(c.dve.sem, c.dve.n)
            dve.sem_inc(s.counted.sem, 1)
            dve.wait_ge(s.summed.sem, s.summed.n + 1)
            st(dve.tensor_scalar(s.ci[:, :], c.ps[:, 0, 0:NB], float(P - 1), None, ALU.add)).wait()
            st(dve.tensor_scalar(s.cj[:, :], s.ci[:, :], 7, None, ALU.arith_shift_right)).wait()
            st(dve.tensor_copy(s.nch[:, :], s.cj[:, :])).wait()
            st(dve.tensor_tensor_scan(s.inc[:, :], c.ones[:, 0:NB], s.nch[:, :], 0.0, ALU.mult, ALU.add)).wait()
            st(dve.tensor_tensor(s.exc[:, :], s.inc[:, :], s.nch[:, :], ALU.subtract)).wait()
            dve.sem_inc(s.ended.sem, 1)
            st(dve.tensor_scalar(s.exc[:, :], s.exc[:, :], float(P), -1.0, ALU.mult, ALU.add)).wait()
            st(dve.tensor_tensor(base[:, :], s.exc[:, :], c.ps[:, 1, 0:NB], ALU.add)).wait()
            dve.wait_ge(s.turned.sem, s.turned.n + 1)
            st(dve.tensor_copy(s.end_t[0:NB, :], c.ps[0:NB, 2, 0:1])).wait()
            st(dve.tensor_scalar(s.past[0:NT, :], c.iota_c[0:NT, :], s.end_t[0:NT, 0:1], None, ALU.is_ge)).wait()
            dve.sem_inc(s.passed.sem, 1)
            dve.wait_ge(s.binned.sem, s.binned.n + 1)
            half = NCH // 2
            st(dve.tensor_copy(c.bin_of[k][0:1, 0:half], c.ps[0:1, 3, 0:half]))
            st(dve.tensor_copy(c.bin_of[k][0:1, half:NCH], c.ps[0:1, 4, 0:half]))
            with dve.Fori(0, NB) as b:
                st.loop(b, 3)
                st(dve.tensor_scalar(mask[:, :], binf[:, :], c.iota_b[:, bass.ds(b, 1)], None, ALU.is_equal)).wait()
                st(dve.tensor_tensor_scan(run[:, :], s.one_row[:, :], mask[:, :], base[:, bass.ds(b, 1)], ALU.mult, ALU.add))
                c.hold(dve, c.dve, b * 3 + (c.dve.n + 2))
                st(dve.copy_predicated(pos[:, :], mask[:, :].bitcast(U32), run[:, :])).wait()
            st.end(NB)
            dve.wait_ge(c.dve.sem, c.dve.n)
            st(dve.tensor_copy(s.ki[:, :], pos[:, :])).wait()
            st(dve.tensor_scalar(s.kl[:, :], s.ki[:, :], P - 1, None, ALU.bitwise_and))
            st(dve.tensor_scalar(s.kh[:, :], s.ki[:, :], 7, None, ALU.arith_shift_right)).wait()
            st(dve.tensor_copy(run[:, :], s.kl[:, :]))
            st(dve.tensor_copy(mask[:, :], s.kh[:, :])).wait()
            st(dve.scalar_tensor_tensor(pos[:, :], run[:, :], float(NCH), mask[:, :], ALU.mult, ALU.add)).wait()

        @block.tensor
        def _(pe):
            pe.wait_ge(s.counted.sem, s.counted.n + 1)
            pe.matmul(c.ps[:, 0, 0:NB], c.ones[:, :], cnt[:, :], start=True, stop=True)
            pe.matmul(c.ps[:, 1, 0:NB], c.upper[:, :], cnt[:, :], start=True, stop=True).then_inc(s.summed.sem, 1)
            pe.wait_ge(s.ended.sem, s.ended.n + 1)
            pe.transpose(c.ps[0:NB, 2, 0:P], s.inc[:, :], c.ident[:, :]).then_inc(s.turned.sem, 1)
            pe.wait_ge(s.passed.sem, s.passed.n + 1)
            half = NCH // 2
            for i in range(2):
                last = pe.matmul(c.ps[0:1, 3 + i, 0:half], c.ones[0:NT, 0:1], s.past[0:NT, i * half:(i + 1) * half],
                                 start=True, stop=True)
            last.then_inc(s.binned.sem, 1)
    for x in (s.counted, s.summed, s.ended, s.turned, s.passed, s.binned):
        x.n += 1


def fields(c, s):
    nc = c.nc
    with nc.Block() as block:

        @block.vector
        def _(dve):
            st = Steps(dve, c.dve)
            for i, (k, out) in enumerate((("src", s.fld[:, :, 4]), ("dst", s.fsrc[:, :, 0]))):
                st(dve.tensor_copy(s.run[:, :], s.key[k][:, :])).wait()
                st(dve.scalar_tensor_tensor(out, s.run[:, :], float(PADKEY), s.run[:, :], ALU.is_lt, ALU.mult)).wait()
            st(dve.tensor_copy(s.fld[:, :, 5], s.lof["dst"]))
            st(dve.tensor_copy(s.fsrc[:, :, 1], s.lof["src"])).wait()


def groups(eng, total, body):
    body(0, 0)
    body(0, 1)
    with eng.Fori(1, total // 2) as i:
        body(i, 0)
        body(i, 1)


def first(i):
    return isinstance(i, int) and i == 0


def at(q, per, start, n):
    if isinstance(q, int):
        return slice(q * per + start, q * per + start + n)
    return bass.ds(q * per + start, n)


def scatter_dst(c, A, s):
    nc = c.nc
    m = s.m
    n0 = SCG // 2

    def all_groups(eng, body):
        groups(eng, SCG, lambda i, h: body(i, h, G8))
        body(n0, 0, G8)
        body(n0, 1, REST)

    with nc.Block() as block:

        @block.sync
        def _(sp):
            def load(i, h, n):
                q = 2 * i + h
                width = G8 * P if n == G8 else E - SCG * G8 * P
                if not first(i):
                    sp.wait_ge(m.h_mm.sem, q * 2 - 2 + m.h_mm.n)
                sp.dma_start(s.ea8[:, h, 0:width], A["ea8"][:, at(q, G8 * P, 0, width)]).then_inc(m.ea[h].sem, 16)
            all_groups(sp, load)

        @block.tensor
        def _(pe):
            def mlp(i, h, n):
                q = 2 * i + h
                pe.wait_ge(m.ea[h].sem, i * 16 + (m.ea[h].n + 16))
                for b in range(2):
                    w = min(512, n * P - 512 * b)
                    if not (first(i) and h == 0):
                        pe.wait_ge(m.silu.sem, q * 2 + (m.silu.n + b - 1))
                    pe.matmul(c.ps[0:64, b, 0:w], s.fc1[:, :], s.ea8[:, h, 512 * b:512 * b + w],
                              start=True, stop=True).then_inc(m.h_mm.sem, 1)
                for b in range(2):
                    pe.wait_ge(m.silu.sem, q * 2 + (m.silu.n + b + 1))
                    if not (first(i) and h == 0):
                        pe.wait_ge(m.copied.sem, q * 2 + (m.copied.n + b - 1))
                    for j in range(min(4, n - 4 * b)):
                        last = pe.matmul(c.ps[:, 2 + b, j * P:(j + 1) * P], s.hid[:, b, j * P:(j + 1) * P],
                                         s.fc2[:, :], start=True, stop=True)
                    last.then_inc(m.w_mm.sem, 1)
            all_groups(pe, mlp)

        @block.scalar
        def _(act):
            def payload(i, h, n):
                q = 2 * i + h
                for b in range(2):
                    w = min(512, n * P - 512 * b)
                    act.wait_ge(m.h_mm.sem, q * 2 + (m.h_mm.n + b + 1))
                    if not (first(i) and h == 0):
                        act.wait_ge(m.w_mm.sem, q * 2 + (m.w_mm.n + b - 1))
                    nc.scalar.activation(s.hid[:, b, 0:w], c.ps[0:64, b, 0:w], ACT.Silu).then_inc(m.silu.sem, 1)
                if not first(i):
                    act.wait_ge(m.sc[h].sem, i * (16 * G8) + m.sc[h].n)
                nc.scalar.activation(c.idx[:, h, 0:n], s.pos["dst"][:, at(q, G8, 0, n)], ACT.Copy)
                nc.scalar.activation(c.pay[:, h, 0:n, EV:EV + 5], s.fld[:, at(q, G8, 0, n), 1:6], ACT.Copy)
                for b in range(2):
                    k = min(4, n - 4 * b)
                    act.wait_ge(m.w_mm.sem, q * 2 + (m.w_mm.n + b + 1))
                    w4 = c.ps[:, 2 + b, :].rearrange("p (j a t u) -> p j a t u", j=4, a=2, t=2)
                    to = c.pay[:, h, 4 * b:4 * b + k, 0:P].rearrange("p j (a t u) -> p j a t u", a=2, t=2)
                    nc.scalar.activation(to[:, :, :, 1, :], w4[:, 0:k, :, 1, :], ACT.Copy)
                    for j in range(k):
                        last = nc.scalar.activation(to[:, j, :, 0, :], w4[:, j, :, 0, :], ACT.Copy,
                                                    scale=s.attr[:, at(q, G8, 4 * b + j, 1), 0])
                    last.then_inc(m.copied.sem, 1)
            act.wait_ge(s.prefilled.sem, s.prefilled.n)
            all_groups(act, payload)

        @block.gpsimd
        def _(pool):
            pool.wait_ge(s.prefilled.sem, s.prefilled.n)
            def send(i, h, n):
                c.hold(pool, m.copied, i * 4 + (h * 2 + m.copied.n + 2))
                for j in range(n):
                    pool.indirect_dma_start(s.dst_rows, bass.IndirectOffsetOnAxis(ap=c.idx[:, h, j:j + 1], axis=0),
                                            c.pay[:, h, j, :], None).then_inc(m.sc[h].sem, 16)
            all_groups(pool, send)
            pool.wait_ge(m.sc[0].sem, m.sc[0].n + 16 * G8 * (n0 + 1))
            pool.wait_ge(m.sc[1].sem, m.sc[1].n + 16 * (G8 * n0 + REST))
    for x in (m.h_mm, m.silu, m.w_mm, m.copied):
        x.n += 2 * (SCG + 1)
    m.ea[0].n += 16 * (n0 + 1)
    m.ea[1].n += 16 * (n0 + 1)
    m.sc[0].n += 16 * G8 * (n0 + 1)
    m.sc[1].n += 16 * (G8 * n0 + REST)


def scatter_src(c, s):
    nc = c.nc
    m = s.m
    n0 = SCG // 2

    def all_groups(eng, body):
        groups(eng, SCG, lambda i, h: body(i, h, G8))
        body(n0, 0, G8)
        body(n0, 1, REST)

    with nc.Block() as block:

        @block.scalar
        def _(act):
            def payload(i, h, n):
                q = 2 * i + h
                if not first(i):
                    act.wait_ge(m.ss[h].sem, i * (16 * G8) + m.ss[h].n)
                nc.scalar.activation(c.idx[:, h, 0:n], s.pos["src"][:, at(q, G8, 0, n)], ACT.Copy)
                nc.scalar.activation(s.small[:, h, 0:n, :], s.fsrc[:, at(q, G8, 0, n), :],
                                     ACT.Copy).then_inc(m.small.sem, 1)
            all_groups(act, payload)

        @block.gpsimd
        def _(pool):
            def send(i, h, n):
                c.hold(pool, m.small, i * 2 + (h + m.small.n + 1))
                for j in range(n):
                    pool.indirect_dma_start(s.src_rows, bass.IndirectOffsetOnAxis(ap=c.idx[:, h, j:j + 1], axis=0),
                                            s.small[:, h, j, :], None).then_inc(m.ss[h].sem, 16)
            all_groups(pool, send)

        @block.sync
        def _(sp):
            sp.wait_ge(m.ss[0].sem, m.ss[0].n + 16 * G8 * (n0 + 1))
            sp.wait_ge(m.ss[1].sem, m.ss[1].n + 16 * (G8 * n0 + REST))
            sp.dma_start(c.meta["src"][:, :, :], s.src_rows.rearrange("(p j) w -> p j w", p=P)).then_inc(c.load.sem, 16)
            sp.wait_ge(c.load.sem, c.load.n + 16)
    m.small.n += SCG + 1
    m.ss[0].n += 16 * G8 * (n0 + 1)
    m.ss[1].n += 16 * (G8 * n0 + REST)
    c.load.n += 16


def load_bins(c, eng, k, i, h):
    _, vals = c.nc.values_load_multi_w_load_instructions(
        c.bin_of[k][0:1, at(2 * i + h, G8, 0, G8)], engines=[eng], min_val=0, max_val=NB - 1,
        skip_runtime_bounds_check_because="the sort makes them from 0 to NB - 1")
    return vals


def one_hot(c, h, places):
    c.nc.vector.tensor_tensor(c.hot[:, h, :, :], c.iota[:, :].unsqueeze(1).broadcast_to([P, G8, P]),
                              places.broadcast_to([P, G8, P]), ALU.is_equal).then_inc(c.hot_ready.sem, 1)


def add_chunk(c, dve, i, h, j, bin_, width, product):
    q = 2 * i + h
    dve.wait_ge(c.mm.sem, q * G8 + (c.mm.n + j + 1))
    if not (first(i) and h == 0 and j == 0):
        dve.wait_ge(c.added.sem, q * G8 + (c.added.n + j))
    to = c.acc[:, bass.ds(bin_, 1), 0:width]
    c.nc.vector.tensor_tensor(to, to, product, ALU.add).then_inc(c.added.sem, 1)


def end_pass(c):
    c.mm.n += NCH
    c.added.n += NCH
    c.hot_ready.n += NG
    c.idx_ready.n += NG
    for g in c.gathered:
        g.n += 16 * G8 * (NG // 2)


def messages(c, s, table):
    nc = c.nc
    m = s.m
    rows3 = s.dst_rows.rearrange("(p j) w -> p j w", p=P)
    with nc.Block() as block:

        @block.sync
        def _(sp):
            def load(i, h):
                q = 2 * i + h
                if not first(i):
                    c.hold(sp, c.mm, q * G8 + (c.mm.n - G8))
                    sp.wait_ge(m.kept.sem, q + (m.kept.n - 1))
                sp.dma_start(c.pay[:, h, :, :], rows3[:, at(q, G8, 0, G8), :]).then_inc(m.pay[h].sem, 16)
            groups(sp, NG, load)

        @block.scalar
        def _(act):
            def scaled(i, h):
                q = 2 * i + h
                act.wait_ge(m.pay[h].sem, i * 16 + (m.pay[h].n + 16))
                if not first(i):
                    act.wait_ge(c.mm.sem, q * G8 + (c.mm.n - G8))
                nc.scalar.activation(c.idx[:, h, :], c.pay[:, h, :, SRC], ACT.Copy).then_inc(c.idx_ready.sem, 1)
                nc.scalar.activation(c.meta["dst"][:, at(q, G8, 0, G8), :], c.pay[:, h, :, SRC:SRC + 2],
                                     ACT.Copy).then_inc(m.kept.sem, 1)
                act.wait_ge(c.hot_ready.sem, q + (c.hot_ready.n + 1))
                for j in range(G8):
                    if not (first(i) and h == 0):
                        act.wait_ge(c.mm.sem, q * G8 + (c.mm.n + j - G8 + 1))
                    for a in range(3):
                        last = nc.scalar.activation(s.hot_v[:, j, a, :], c.hot[:, h, j, :], ACT.Copy,
                                                    scale=c.pay[:, h, j, EV + a:EV + a + 1])
                    last.then_inc(m.scaled.sem, 1)
            groups(act, NG, scaled)

        @block.gpsimd
        def _(pool):
            def gather(i, h):
                c.hold(pool, c.idx_ready, i * 2 + (h + c.idx_ready.n + 1))
                for j in range(G8):
                    pool.indirect_dma_start(c.rows[:, h, j, 0:D], None, table,
                                            bass.IndirectOffsetOnAxis(ap=c.idx[:, h, j:j + 1], axis=0)
                                            ).then_inc(c.gathered[h].sem, 16)
            groups(pool, NG, gather)

        @block.vector
        def _(dve):
            def reduce(i, h):
                q = 2 * i + h
                dve.wait_ge(m.pay[h].sem, i * 16 + (m.pay[h].n + 16))
                if not first(i):
                    dve.wait_ge(c.mm.sem, q * G8 + (c.mm.n - G8))
                one_hot(c, h, c.pay[:, h, :, LO:LO + 1])
                bins = load_bins(c, mybir.EngineType.DVE, "dst", i, h)
                dve.wait_ge(c.gathered[h].sem, i * (16 * G8) + (c.gathered[h].n + 16 * G8))
                for j in range(G8 + 2):
                    if j < G8:
                        if not (first(i) and h == 0):
                            dve.wait_ge(c.mm.sem, q * G8 + (c.mm.n + j - G8 + 1))
                        w = c.pay[:, h, j, 0:P].rearrange("p (t u) -> p t u", t=4)
                        g = c.rows[:, h, j, 0:D].rearrange("p (t u) -> p t u", t=4)
                        nc.vector.tensor_tensor(s.prod[:, j, 0:8:7, 0:MUL], w[:, 0:2, :],
                                                g[:, 0:1, :].broadcast_to([P, 2, MUL]), ALU.mult)
                        nc.vector.tensor_tensor(s.prod[:, j, 1:7, 0:MUL].rearrange("p (a t) u -> p a t u", a=2),
                                                w[:, 2:4, :].unsqueeze(2).broadcast_to([P, 2, 3, MUL]),
                                                g[:, 1:4, :].unsqueeze(1).broadcast_to([P, 2, 3, MUL]),
                                                ALU.mult).then_inc(m.prod.sem, 1)
                    if j >= 2:
                        add_chunk(c, dve, i, h, j - 2, bins[j - 2], AW, c.ps[:, j - 2:j - 1, 0:AW])
            groups(dve, NG, reduce)

        @block.tensor
        def _(pe):
            def product(i, h):
                q = 2 * i + h
                for j in range(G8):
                    pe.wait_ge(m.prod.sem, q * G8 + (m.prod.n + j + 1))
                    pe.wait_ge(m.scaled.sem, q * G8 + (m.scaled.n + j + 1))
                    if not (first(i) and h == 0):
                        pe.wait_ge(c.added.sem, q * G8 + (c.added.n + j - G8 + 1))
                    out = c.ps[:, j, 0:AW].rearrange("p (g u) -> p g u", g=4)
                    pe.matmul(out[:, :, MUL:2 * MUL + 1], c.hot[:, h, j, :], s.prod[:, j, 0:4, :],
                              start=True, stop=False, skip_group_check=True)
                    for a in range(3):
                        last = pe.matmul(out[:, 0:a + 2:a + 1, 0:MUL], s.hot_v[:, j, a, :],
                                         s.prod[:, j, 4 + a:8:3 - a, 0:MUL], start=False, stop=(a == 2),
                                         skip_group_check=True)
                    last.then_inc(c.mm.sem, 1)
            groups(pe, NG, product)
    end_pass(c)
    m.pay[0].n += 16 * (NG // 2)
    m.pay[1].n += 16 * (NG // 2)
    m.kept.n += NG
    m.prod.n += NCH
    m.scaled.n += NCH


def copy_indices(c, act, k):
    def body(i, h):
        q = 2 * i + h
        if not first(i):
            act.wait_ge(c.mm.sem, q * G8 + (c.mm.n - G8))
        c.nc.scalar.activation(c.idx[:, h, :], c.meta[k][:, at(q, G8, 0, G8), 0], ACT.Copy).then_inc(c.idx_ready.sem, 1)
    return body


def gather_rows(c, pool, table, to):
    def body(i, h):
        c.hold(pool, c.idx_ready, i * 2 + (h + c.idx_ready.n + 1))
        for j in range(G8):
            pool.indirect_dma_start(to(h, j), None, table,
                                    bass.IndirectOffsetOnAxis(ap=c.idx[:, h, j:j + 1], axis=0)
                                    ).then_inc(c.gathered[h].sem, 16)
    return body


def aggregate(c, k, table, width, used):
    nc = c.nc
    with nc.Block() as block:

        @block.scalar
        def _(act):
            groups(act, NG, copy_indices(c, act, k))

        @block.gpsimd
        def _(pool):
            groups(pool, NG, gather_rows(c, pool, table, lambda h, j: c.rows[:, h, j, 0:width]))

        @block.vector
        def _(dve):
            def reduce(i, h):
                q = 2 * i + h
                if not first(i):
                    dve.wait_ge(c.mm.sem, q * G8 + (c.mm.n - G8))
                one_hot(c, h, c.meta[k][:, at(q, G8, 0, G8), 1:2])
                bins = load_bins(c, mybir.EngineType.DVE, k, i, h)
                for j in range(G8):
                    add_chunk(c, dve, i, h, j, bins[j], used, c.ps[:, j:j + 1, 0:used])
            groups(dve, NG, reduce)

        @block.tensor
        def _(pe):
            def product(i, h):
                q = 2 * i + h
                pe.wait_ge(c.gathered[h].sem, i * (16 * G8) + (c.gathered[h].n + 16 * G8))
                pe.wait_ge(c.hot_ready.sem, q + (c.hot_ready.n + 1))
                for j in range(G8):
                    if not (first(i) and h == 0):
                        pe.wait_ge(c.added.sem, q * G8 + (c.added.n + j - G8 + 1))
                    pe.matmul(c.ps[:, j, 0:used], c.hot[:, h, j, :], c.rows[:, h, j, 0:used],
                              start=True, stop=True).then_inc(c.mm.sem, 1)
            groups(pe, NG, product)
    end_pass(c)


def node_product(c, s, feed, parts, part_width, products, steps, take):
    nc = c.nc
    m = s.m

    def tiles_of(eng, body):
        body(0)
        with eng.Fori(1, NB // 2 - 1) as i:
            body(i)
        body(NB // 2 - 1)

    last_ = lambda i: isinstance(i, int) and i == NB // 2 - 1

    with nc.Block() as block:

        @block.scalar
        def _(act):
            def fill(k, slot, free):
                if free:
                    act.wait_ge(m.turned.sem, k + (m.turned.n - 1))
                feed(k, slot).then_inc(m.fed.sem, 1)

            def body(i):
                if first(i):
                    fill(0, 0, False)
                    fill(1, 1, False)
                for slot in range(2):
                    k = 2 * i + slot
                    act.wait_ge(m.turned.sem, k + (m.turned.n + 1))
                    if not first(i):
                        act.wait_ge(m.multiplied.sem, k + (m.multiplied.n - 1))
                    nc.scalar.activation(s.ut[0:part_width, slot, 0:parts * P], c.ps[0:part_width, slot, 0:parts * P],
                                         ACT.Copy).then_inc(m.back.sem, 1)
                    if not last_(i):
                        fill(k + 2, slot, True)
            tiles_of(act, body)

        @block.tensor
        def _(pe):
            def turn(k, slot, free):
                if free:
                    pe.wait_ge(m.back.sem, k + (m.back.n - 1))
                c.hold(pe, m.fed, k + (m.fed.n + 1))
                for a in range(parts):
                    last = pe.transpose(c.ps[0:part_width, slot, a * P:(a + 1) * P],
                                        s.u[:, slot, a * part_width:(a + 1) * part_width], c.ident[:, :])
                last.then_inc(m.turned.sem, 1)

            def body(i):
                if first(i):
                    turn(0, 0, False)
                for slot in range(2):
                    k = 2 * i + slot
                    if not (last_(i) and slot == 1):
                        turn(k + 1, 1 - slot, not (first(i) and slot == 0))
                    pe.wait_ge(m.back.sem, k + (m.back.n + 1))
                    if not first(i):
                        pe.wait_ge(m.taken.sem, k + (m.taken.n - 1))
                    for a, w, lo, hi, start, stop in products:
                        last = pe.matmul(c.ps[:, 4 + slot, lo:hi], s.ut[0:part_width, slot, a * P:(a + 1) * P], w,
                                         start=start, stop=stop)
                    last.then_inc(m.multiplied.sem, 1)
            tiles_of(pe, body)

        @block.vector
        def _(dve):
            st = Steps(dve, c.dve)

            def body(i):
                st.loop(i, 2 * steps)
                for slot in range(2):
                    k = 2 * i + slot
                    dve.wait_ge(m.multiplied.sem, k + (m.multiplied.n + 1))
                    take(st, k, 4 + slot).then_inc(m.taken.sem, 1)
                assert st.k == st.per, (st.k, st.per)
            tiles_of(dve, body)
            st.end(NB // 2)
    for x in (m.fed, m.turned, m.back, m.multiplied, m.taken):
        x.n += NB


def one(k):
    return slice(k, k + 1) if isinstance(k, int) else bass.ds(k, 1)


def stats(c, s, st, k, ap):
    c.hold(st.eng, st.c, st.reached())
    st(c.nc.vector.bn_stats(s.st6[:, :], ap))
    c.hold(st.eng, st.c, st.reached())
    st(c.nc.vector.bn_aggr(s.mv1[:, 0, :], s.st6[:, :])).wait()
    return c.nc.vector.tensor_scalar(c.mv[:, one(k), :], s.mv1[:, :, :], 0.0, None, ALU.add)


def seg(ap, g):
    return ap[:, g * SEGT:(g + 1) * SEGT]


def spread(col, width):
    return col.unsqueeze(2).broadcast_to([P, col.shape[1], width])


def over(row, n):
    return row.unsqueeze(1).broadcast_to([P, n, row.shape[1]])


def root(c, s, to, src, bias):
    nc = c.nc
    with nc.Block() as block:

        @block.scalar
        def _(act):
            nc.scalar.activation(to, src, ACT.Sqrt, bias=bias).then_inc(s.m.rooted.sem, 1)

        @block.vector
        def _(dve):
            dve.wait_ge(s.m.rooted.sem, s.m.rooted.n + 1)
            Steps(dve, c.dve)(nc.vector.reciprocal(to, to))
    s.m.rooted.n += 1


def normalise(c, s, self_term=False, clear=False, table=None, out=None):
    nc = c.nc
    root(c, s, c.rstd[:, :], c.mv[:, :, 1], c.eps[:, 0:1])
    with nc.Block() as block:

        @block.vector
        def _(dve):
            st = Steps(dve, c.dve)
            for g in range(NSEG):
                x = seg(c.x, g)
                st(nc.vector.tensor_tensor(x, x, spread(seg(c.mv, g)[:, :, 0], D), ALU.subtract)).wait()
                last = nc.vector.tensor_tensor(x, x, spread(seg(c.rstd, g), D), ALU.mult)
                if self_term:
                    st(last).wait()
                    last = nc.vector.tensor_tensor(seg(c.acc, g)[:, :, 0:D], x, spread(seg(c.dinv, g), D), ALU.mult)
                last.then_inc(s.m.part.sem, 1)
            if clear:
                nc.vector.memset(c.acc[:, :, :], 0.0)

        @block.sync
        def _(sp):
            for g in range(NSEG):
                sp.wait_ge(s.m.part.sem, s.m.part.n + g + 1)
                src = seg(c.acc, g)[:, :, 0:D] if self_term else seg(c.x, g)
                if out is None:
                    sp.dma_start(tiles(table, NB, D)[:, g * SEGT:(g + 1) * SEGT, :], src).then_inc(c.store.sem, 16)
                elif g < NSEG - 1:
                    sp.dma_start(tiles(out[0:(NSEG - 1) * SEGT * P, :], 0, 0)[:, g * SEGT:(g + 1) * SEGT, :], src
                                 ).then_inc(c.store.sem, 16)
                else:
                    full = NT - 1 - g * SEGT
                    sp.dma_start(tiles(out[g * SEGT * P:(NT - 1) * P, :], 0, 0), src[:, 0:full, :]).then_inc(c.store.sem, 16)
                    sp.dma_start(out[(NT - 1) * P:N, :], c.x[0:LASTN, NT - 1, :]).then_inc(c.store.sem, 16)
            sp.wait_ge(c.store.sem, c.store.n + 16 * (NSEG + (out is not None)))
    s.m.part.n += NSEG
    c.store.n += 16 * (NSEG + (out is not None))


def write_table(c, src, table, width):
    nc = c.nc
    with nc.Block() as block:

        @block.sync
        def _(sp):
            for g in range(NSEG):
                sp.dma_start(tiles(table, NB, width)[:, g * SEGT:(g + 1) * SEGT, :], seg(src, g)).then_inc(c.store.sem, 16)
            sp.wait_ge(c.store.sem, c.store.n + 16 * NSEG)
    c.store.n += 16 * NSEG


def clear_acc(c, value=0.0):
    nc = c.nc
    with nc.Block() as block:

        @block.vector
        def _(dve):
            Steps(dve, c.dve)(nc.vector.memset(c.acc[:, :, :], value))


def conv_norm(c, s, l, table):
    nc = c.nc
    root(c, s, c.rstd[:, :], c.mv[:, :, 1], c.eps[:, 0:1])
    m = s.m
    gain, shift = s.gain[l], s.shift[l]
    with nc.Block() as block:

        @block.vector
        def _(dve):
            st = Steps(dve, c.dve)

            def finish(g):
                a = seg(c.acc, g)[:, :, 0:HID]
                dve.wait_ge(m.powered.sem, m.powered.n + g + 1)
                st(nc.vector.scalar_tensor_tensor(a, a, 0.0, s.ex[:, g % 2, :, :], ALU.max, ALU.add)).wait()
                nc.vector.scalar_tensor_tensor(a, a, -1.0, spread(seg(c.dinv, g), HID), ALU.add,
                                               ALU.mult).then_inc(m.part.sem, 1)

            for g in range(NSEG):
                a = seg(c.acc, g)[:, :, 0:HID]
                st(nc.vector.tensor_tensor(a, a, spread(seg(c.mv, g)[:, :, 0], HID), ALU.subtract)).wait()
                nc.vector.tensor_tensor(a, a, spread(seg(c.rstd, g), HID), ALU.mult).then_inc(m.centred.sem, 1)
                if g:
                    dve.wait_ge(m.shifted.sem, m.shifted.n + g)
                    b = seg(c.acc, g - 1)[:, :, 0:HID]
                    nc.vector.tensor_scalar(s.ex[:, (g - 1) % 2, :, :], b, 0.0, None, ALU.min).then_inc(m.cut.sem, 1)
                if g >= 2:
                    finish(g - 2)
            dve.wait_ge(m.shifted.sem, m.shifted.n + NSEG)
            b = seg(c.acc, NSEG - 1)[:, :, 0:HID]
            nc.vector.tensor_scalar(s.ex[:, (NSEG - 1) % 2, :, :], b, 0.0, None, ALU.min).then_inc(m.cut.sem, 1)
            finish(NSEG - 2)
            finish(NSEG - 1)

        @block.gpsimd
        def _(pool):
            for g in range(NSEG):
                a = seg(c.acc, g)[:, :, 0:HID]
                pool.wait_ge(m.centred.sem, m.centred.n + g + 1)
                pool.tensor_tensor(a, a, over(gain[:, :], SEGT), ALU.mult).then_inc(c.pool.sem, 1)
                pool.wait_ge(c.pool.sem, c.pool.n + g + 1)
                pool.tensor_tensor(a, a, over(shift[:, :], SEGT), ALU.add).then_inc(m.shifted.sem, 1)

        @block.scalar
        def _(act):
            for g in range(NSEG):
                act.wait_ge(m.cut.sem, m.cut.n + g + 1)
                e = s.ex[:, g % 2, :, :]
                nc.scalar.activation(e, e, ACT.Exp).then_inc(m.powered.sem, 1)

        @block.sync
        def _(sp):
            if table is not None:
                for g in range(NSEG):
                    sp.wait_ge(m.part.sem, m.part.n + g + 1)
                    sp.dma_start(tiles(table, NB, HID)[:, g * SEGT:(g + 1) * SEGT, :],
                                 seg(c.acc, g)[:, :, 0:HID]).then_inc(c.store.sem, 16)
                sp.wait_ge(c.store.sem, c.store.n + 16 * NSEG)
    if table is not None:
        c.store.n += 16 * NSEG
    for x in (m.centred, m.shifted, m.cut, m.powered, m.part):
        x.n += NSEG
    c.pool.n += NSEG


def tile_stats(c, s, dve, st):
    with dve.Fori(0, NB) as k:
        st.loop(k, 3)
        stx = stats(c, s, st, k, c.x[:, one(k), :].rearrange("p a b -> p (a b)"))
        st(stx).wait()
    st.end(NB)


def add_gcn(c, s):
    nc = c.nc
    with nc.Block() as block:

        @block.vector
        def _(dve):
            st = Steps(dve, c.dve)
            for g in range(NSEG):
                a, x = seg(c.acc, g)[:, :, 0:D], seg(c.x, g)
                st(nc.vector.tensor_tensor(a, a, spread(seg(c.dinv, g), D), ALU.mult))
                st(nc.vector.tensor_tensor(x, x, over(s.b3[:, :], SEGT), ALU.add)).wait()
                st(nc.vector.tensor_tensor(x, x, a, ALU.add))
            st.wait()
            tile_stats(c, s, dve, st)


def add_gat(c, s):
    nc = c.nc
    with nc.Block() as block:

        @block.vector
        def _(dve):
            st = Steps(dve, c.dve)
            den = c.acc[:, :, D:D + HEADS]
            st(nc.vector.tensor_scalar(den, den, 1e-16, None, ALU.add)).wait()
            st(nc.vector.reciprocal(den, den)).wait()
            for g in range(NSEG):
                a, x, t = seg(c.acc, g)[:, :, 0:D], seg(c.x, g), s.ex[:, 0, :, 0:D]
                a4 = a.rearrange("p n (h c) -> p n h c", h=HEADS)
                r4 = seg(den, g).unsqueeze(3).broadcast_to([P, SEGT, HEADS, CH])
                st(nc.vector.tensor_tensor(a4, a4, r4, ALU.mult)).wait()
                st(nc.vector.tensor_tensor(a, a, over(s.bias[:, :], SEGT), ALU.add)).wait()
                st(nc.vector.scalar_tensor_tensor(t, a, 0.0, over(s.prelu[:, :], SEGT), ALU.min, ALU.mult)).wait()
                st(nc.vector.scalar_tensor_tensor(a, a, 0.0, t, ALU.max, ALU.add)).wait()
                st(nc.vector.tensor_tensor(x, x, a, ALU.add))
            st.wait()
            tile_stats(c, s, dve, st)


def scores_max(c, s, table):
    nc = c.nc
    m = s.m
    with nc.Block() as block:

        @block.scalar
        def _(act):
            copy = copy_indices(c, act, "dst")
            def body(i, h):
                copy(i, h)
                q = 2 * i + h
                act.wait_ge(c.hot_ready.sem, q + (c.hot_ready.n + 1))
                act.wait_ge(c.gathered[h].sem, i * (16 * G8) + (c.gathered[h].n + 16 * G8))
                for j in range(G8):
                    if not (first(i) and h == 0):
                        act.wait_ge(c.mm.sem, q * G8 + (c.mm.n + j - G8 + 1))
                    for a in range(HEADS):
                        last = nc.scalar.activation(s.hot_v[:, j, a, :], c.hot[:, h, j, :], ACT.Identity,
                                                    bias=c.rows[:, h, j, a:a + 1])
                    last.then_inc(m.scaled.sem, 1)
            groups(act, NG, body)

        @block.gpsimd
        def _(pool):
            groups(pool, NG, gather_rows(c, pool, table, lambda h, j: c.rows[:, h, j, 0:HEADS]))

        @block.vector
        def _(dve):
            def reduce(i, h):
                q = 2 * i + h
                if not first(i):
                    dve.wait_ge(c.mm.sem, q * G8 + (c.mm.n - G8))
                for j in range(G8):
                    last = nc.vector.tensor_scalar(c.hot[:, h, j, :], c.iota[:, :],
                                                   c.meta["dst"][:, at(q, G8, j, 1), 1], NEG,
                                                   ALU.not_equal, ALU.mult)
                last.then_inc(c.hot_ready.sem, 1)
                bins = load_bins(c, mybir.EngineType.DVE, "dst", i, h)
                for j in range(G8 + 1):
                    if j < G8:
                        dve.wait_ge(c.mm.sem, q * G8 + (c.mm.n + j + 1))
                        nc.vector.tensor_reduce(s.mx8[:, j, :], c.ps[:, j, 0:HEADS * P].rearrange("p (a e) -> p a e", a=HEADS),
                                                AX.X, ALU.max).then_inc(m.reduced.sem, 1)
                    if j:
                        dve.wait_ge(m.reduced.sem, q * G8 + (m.reduced.n + j))
                        if not (first(i) and h == 0 and j == 1):
                            dve.wait_ge(c.added.sem, q * G8 + (c.added.n + j - 1))
                        to = s.mx[:, bass.ds(bins[j - 1], 1), :]
                        nc.vector.tensor_tensor(to, to, s.mx8[:, j - 1:j, :], ALU.max).then_inc(c.added.sem, 1)
            groups(dve, NG, reduce)

        @block.tensor
        def _(pe):
            def turn(i, h):
                q = 2 * i + h
                for j in range(G8):
                    pe.wait_ge(m.scaled.sem, q * G8 + (m.scaled.n + j + 1))
                    if not (first(i) and h == 0):
                        pe.wait_ge(m.reduced.sem, q * G8 + (m.reduced.n + j - G8 + 1))
                    for a in range(HEADS):
                        last = pe.transpose(c.ps[:, j, a * P:(a + 1) * P], s.hot_v[:, j, a, :], c.ident[:, :])
                    last.then_inc(c.mm.sem, 1)
            groups(pe, NG, turn)
    end_pass(c)
    m.scaled.n += NCH
    m.reduced.n += NCH


def node_max(c, s):
    nc = c.nc
    with nc.Block() as block:

        @block.vector
        def _(dve):
            st = Steps(dve, c.dve)
            st(nc.vector.tensor_tensor(s.mx[:, :, :], s.mx[:, :, :], s.nt[:, :, 0:2], ALU.add)).wait()
            st(nc.vector.scalar_tensor_tensor(s.nt[:, :, 2:4], s.mx[:, :, :], SLOPE, s.mx[:, :, :], ALU.mult, ALU.max))
            nc.vector.memset(c.acc[:, :, :], 0.0)


def attend(c, s, table):
    nc = c.nc
    m = s.m
    width = D + HEADS
    with nc.Block() as block:

        @block.scalar
        def _(act):
            copy = copy_indices(c, act, "dst")
            def body(i, h):
                copy(i, h)
                q = 2 * i + h
                for b in range(2):
                    act.wait_ge(m.turned.sem, q * 2 + (m.turned.n + b + 1))
                    nc.scalar.activation(s.hot_t[:, 4 * b:4 * b + 4, :].rearrange("p j n -> p (j n)"), c.ps[:, b, :],
                                         ACT.Copy).then_inc(m.back.sem, 1)
                act.wait_ge(m.scored.sem, q + (m.scored.n + 1))
                nc.scalar.activation(s.wt[:, :, D:width], s.z[:, :, :], ACT.Exp).then_inc(m.powered.sem, 1)
            groups(act, NG, body)

        @block.gpsimd
        def _(pool):
            groups(pool, NG, gather_rows(c, pool, table, lambda h, j: c.rows[:, h, j, 0:width]))

        @block.vector
        def _(dve):
            st = Steps(dve, c.dve)
            def reduce(i, h):
                q = 2 * i + h
                if h == 0:
                    st.loop(i, 6)
                if not first(i):
                    dve.wait_ge(c.mm.sem, q * G8 + (c.mm.n - G8))
                one_hot(c, h, c.meta["dst"][:, at(q, G8, 0, G8), 1:2])
                bins = load_bins(c, mybir.EngineType.DVE, "dst", i, h)
                dve.wait_ge(c.gathered[h].sem, i * (16 * G8) + (c.gathered[h].n + 16 * G8))
                dve.wait_ge(m.looked.sem, q + (m.looked.n + 1))
                e8 = c.ps[:, 2, 0:4 * G8].rearrange("p (j k) -> p j k", j=G8)
                z = s.z[:, :, :]
                if not (first(i) and h == 0):
                    dve.wait_ge(m.powered.sem, q + m.powered.n)
                st(nc.vector.tensor_tensor(z, c.rows[:, h, :, D:width], e8[:, :, 0:2], ALU.add)).wait()
                st(nc.vector.scalar_tensor_tensor(z, z, SLOPE, z, ALU.mult, ALU.max)).wait()
                st(nc.vector.tensor_tensor(z, z, e8[:, :, 2:4], ALU.subtract)).wait()
                nc.vector.tensor_scalar(z, z, 0.0, None, ALU.min).then_inc(m.scored.sem, 1)
                dve.wait_ge(m.powered.sem, q + (m.powered.n + 1))
                nc.vector.tensor_tensor(
                    s.wt[:, :, 0:D].rearrange("p j (a u) -> p j a u", a=HEADS),
                    c.rows[:, h, :, 0:D].rearrange("p j (a u) -> p j a u", a=HEADS),
                    s.wt[:, :, D:width].unsqueeze(3).broadcast_to([P, G8, HEADS, CH]),
                    ALU.mult).then_inc(m.weighted.sem, 1)
                for j in range(G8):
                    bank = 3 + j % 5
                    add_chunk(c, dve, i, h, j, bins[j], width, c.ps[:, bank:bank + 1, 0:width])
            groups(dve, NG, reduce)
            st.end(NG // 2)

        @block.tensor
        def _(pe):
            def product(i, h):
                q = 2 * i + h
                bins = load_bins(c, mybir.EngineType.PE, "dst", i, h)
                pe.wait_ge(c.hot_ready.sem, q + (c.hot_ready.n + 1))
                for j in range(G8):
                    last = pe.transpose(c.ps[:, j // 4, (j % 4) * P:(j % 4 + 1) * P], c.hot[:, h, j, :], c.ident[:, :])
                    if j % 4 == 3:
                        last.then_inc(m.turned.sem, 1)
                for b in range(2):
                    pe.wait_ge(m.back.sem, q * 2 + (m.back.n + b + 1))
                    for j in range(4 * b, 4 * b + 4):
                        last = pe.matmul(c.ps[:, 2, 4 * j:4 * j + 4], s.hot_t[:, j, :],
                                         s.nt[:, bass.ds(bins[j], 1), :].rearrange("p a b -> p (a b)"),
                                         start=True, stop=True)
                last.then_inc(m.looked.sem, 1)
                pe.wait_ge(m.weighted.sem, q + (m.weighted.n + 1))
                for j in range(G8):
                    before = j - 5 if j >= 5 else j - 3 if j < 3 else j - G8
                    if not (first(i) and h == 0 and before < 0):
                        pe.wait_ge(c.added.sem, q * G8 + (c.added.n + before + 1))
                    pe.matmul(c.ps[:, 3 + j % 5, 0:width], c.hot[:, h, j, :], s.wt[:, j, :],
                              start=True, stop=True).then_inc(c.mm.sem, 1)
            groups(pe, NG, product)
    end_pass(c)
    m.turned.n += 2 * NG
    m.back.n += 2 * NG
    for x in (m.looked, m.scored, m.powered, m.weighted):
        x.n += NG


def prepare_weights(c, s):
    nc = c.nc
    v = nc.vector
    with nc.Block() as block:

        @block.scalar
        def _(act):
            nc.scalar.activation(s.sig[:, :], s.sig[:, :], ACT.Exp, scale=-1.0).then_inc(s.m.rooted.sem, 1)

        @block.vector
        def _(dve):
            st = Steps(dve, c.dve)
            st(v.tensor_scalar(s.lin1[:, :], s.lin1[:, :], MUL ** -0.5, None, ALU.mult))
            st(v.tensor_scalar(s.fc1[:, :], s.fc1[:, :], 8 ** -0.5, None, ALU.mult))
            st(v.tensor_scalar(s.fc2[:, :], s.fc2[:, :], SILU_NORM * 64 ** -0.5, None, ALU.mult))
            scale = 0.25 * (2 * MUL) ** -0.5
            st(v.tensor_scalar(s.lin2s[0:MUL, :], s.lin2s[0:MUL, :], scale * 3 ** -0.5, None, ALU.mult))
            st(v.tensor_scalar(s.lin2s[MUL:2 * MUL, :], s.lin2s[MUL:2 * MUL, :], scale, None, ALU.mult))
            st(v.tensor_scalar(s.lin2v[:, :], s.lin2v[:, :], scale, None, ALU.mult))
            st(v.tensor_tensor(s.attw[:, 0, :], s.wg[:, 0:D], s.att[:, 0, :], ALU.mult))
            st(v.tensor_tensor(s.attw[:, 1, :], s.wdst[:, :], s.att[:, 1, :], ALU.mult)).wait()
            st(v.tensor_reduce(s.wg[:, D:D + 4], s.attw[:, :, :].rearrange("p a (h u) -> p (a h) u", h=HEADS),
                               AX.X, ALU.add))
            dve.wait_ge(s.m.rooted.sem, s.m.rooted.n + 1)
            st(v.tensor_scalar(s.sig[:, :], s.sig[:, :], 1.0, None, ALU.add)).wait()
            st(v.reciprocal(s.sig[:, :], s.sig[:, :])).wait()
            for l in range(3):
                w, a = s.w[l][:, :], s.sig[:, l:l + 1]
                st(v.tensor_scalar(w, w, a, None, ALU.mult))
                st(v.tensor_scalar(s.b[l][:, :], s.b[l][:, :], a, None, ALU.mult))
    s.m.rooted.n += 1


def degrees(c, s):
    root(c, s, c.dinv[:, :], c.acc[:, :, 2 * MUL], c.ones[:, 0:1])


class Scratch:
    pass


def gnn(nc, A, out, upto=None):
    with ExitStack() as ctx:
        c = Chip(nc, ctx)
        s = Scratch()
        sb = c.sb
        flat = c.acc[:, :, :].rearrange("p n w -> p (n w)")
        at_ = [0]

        def lay(width, dt=F32):
            a = flat[:, at_[0]:at_[0] + width]
            at_[0] += width
            return a if dt is F32 else a.bitcast(dt)
        s.key = {k: lay(TC, I32) for k in ("dst", "src")}
        s.lof = {k: lay(TC) for k in ("dst", "src")}
        s.pos = {k: lay(TC) for k in ("dst", "src")}
        s.binf, s.mask, s.run, s.one_row = (lay(TC) for _ in range(4))
        s.ki, s.kl, s.kh = (lay(TC, I32) for _ in range(3))
        s.fsrc = lay(2 * TC).rearrange("p (t w) -> p t w", w=2)
        s.fld = sb("fld", [P, TC, 6])
        s.attr = s.fld[:, :, 0:4]
        s.cnt, s.nch, s.inc, s.exc = (sb(n, [P, NB]) for n in ("bin_count", "bin_chunks", "bin_end", "bin_start"))
        s.ci, s.cj = (sb(n, [P, NB], I32) for n in ("bin_count_i", "bin_chunks_i"))
        s.base = {k: sb(f"base_{k}", [P, NB]) for k in ("dst", "src")}
        s.end_t = sb("end_t", [64, 1])
        s.past = c.hot[0:64, 1, :, :].rearrange("p j n -> p (j n)")[:, 0:NCH]
        s.small = sb("small", [P, 2, G8, 2])
        s.hot_v = sb("hot_v", [P, G8, 3, P])
        s.prod = sb("prod", [P, G8, 8, MUL + 1])
        s.ex = s.hot_v[:, :, :, :].rearrange("p j a n -> p (j a n)")[:, 0:2 * SEGT * HID].rearrange(
            "p (g n w) -> p g n w", g=2, n=SEGT)
        s.hot_t = s.prod[:, :, :, :].rearrange("p j a n -> p (j a n)")[:, 0:G8 * P].rearrange("p (j n) -> p j n", j=G8)
        s.ea8 = s.hot_v[0:8, :, :, :].rearrange("p j a n -> p (j a n)")[:, 0:2 * G8 * P].rearrange(
            "p (h n) -> p h n", h=2)
        s.hid = s.prod[0:64, :, :, :].rearrange("p j a n -> p (j a n)")[:, 0:1024].rearrange("p (b n) -> p b n", b=2)
        s.wt = c.pay[:, 0, :, 0:D + HEADS]
        s.z = c.pay[:, 1, :, 0:HEADS]
        s.u = s.hid_u = sb("u", [P, 2, HID])
        s.ut = sb("ut", [P, 2, 4 * P])
        s.st6 = sb("st6", [P, 6])
        s.mv1 = sb("mv1", [P, 1, 2])
        s.mx = sb("mx", [P, NB, HEADS])
        s.mx8 = sb("mx8", [P, G8, HEADS])
        s.nt = sb("nt", [P, NB, 4])
        s.rcnt = sb("rcnt", [P, NB])
        s.has = sb("has", [P, NB])
        s.lin1 = sb("lin1", [P, P])
        s.fc1 = sb("fc1", [8, 64])
        s.fc2 = sb("fc2", [64, P])
        s.lin2s = sb("lin2s", [2 * MUL, MUL])
        s.lin2v = sb("lin2v", [2 * MUL, MUL])
        s.w = [sb("w0", [P, HID]), sb("w1", [P, 2 * HID]), sb("w2", [P, 2 * HID])]
        s.w3 = sb("w3", [P, 2 * D])
        s.b = [sb(f"b{l}", [P, HID]) for l in range(3)]
        s.gain = [sb(f"gain{l}", [P, HID]) for l in range(3)]
        s.shift = [sb(f"shift{l}", [P, HID]) for l in range(3)]
        s.b3 = sb("b3", [P, D])
        s.sig = sb("sig", [P, 3])
        s.wself, s.wneigh = sb("wself", [P, D]), sb("wneigh", [P, D])
        s.bself, s.bneigh = sb("bself", [P, D]), sb("bneigh", [P, D])
        s.wg, s.wdst = sb("wg", [P, D + 4]), sb("wdst", [P, D])
        s.att, s.attw = sb("att", [P, 2, D]), sb("attw", [P, 2, D])
        s.bias, s.prelu = sb("bias", [P, D]), sb("prelu", [P, D])
        two = lambda ap: ap.rearrange("(a p) n -> p a n", p=P)
        each = lambda ap: ap.partition_broadcast(P)
        halves = lambda t: t[:, :].rearrange("p (a n) -> p a n", a=2)
        s.weights = [(s.lin1[0:MUL, 0:MUL], A["L0_gnn_w_lin1_s"]),
                     (s.fc1[:, :], A["L0_gnn_fc_w1"]), (s.fc2[:, :], A["L0_gnn_fc_w2"]),
                     (s.lin2s[0:MUL, :], A["L0_gnn_w_lin2_s"][MUL:2 * MUL, :]),
                     (s.lin2s[MUL:2 * MUL, :], A["L0_gnn_w_lin2_s"][0:MUL, :]),
                     (s.lin2v[:, :], A["L0_gnn_w_lin2_v"]),
                     (s.w[0][:, :], A["L1_gnn_W0"]), (halves(s.w[1]), two(A["L1_gnn_W1"])),
                     (halves(s.w[2]), two(A["L1_gnn_W2"])), (halves(s.w3), two(A["L1_gnn_W3"])),
                     (s.b3[:, :], each(A["L1_gnn_b3"])),
                     (s.wself[:, :], A["WsT"]), (s.wneigh[:, :], A["WnT"]),
                     (s.bself[:, :], each(A["L2_gnn_b_self"])), (s.bneigh[:, :], each(A["L2_gnn_b_neigh"])),
                     (s.wg[:, 0:D], A["L3_gnn_W_src"]), (s.wdst[:, :], A["L3_gnn_W_dst"]),
                     (s.att[:, 0, :], each(A["L3_gnn_att_src"].rearrange("h u -> (h u)"))),
                     (s.att[:, 1, :], each(A["L3_gnn_att_dst"].rearrange("h u -> (h u)"))),
                     (s.bias[:, :], each(A["L3_gnn_bias"])), (s.prelu[:, :], each(A["L3_gnn_prelu_w"]))]
        for i in range(3):
            s.weights += [(s.lin1[MUL + i:P:3, MUL * (i + 1):MUL * (i + 2)], A["L0_gnn_w_lin1_v"]),
                          (s.b[i][:, :], each(A[f"L1_gnn_b{i}"])), (s.gain[i][:, :], each(A[f"L1_gnn_g{i}"])),
                          (s.shift[i][:, :], each(A[f"L1_gnn_beta{i}"])), (s.sig[:, i:i + 1], each(A[f"L1_gnn_a{i}"]))]
        dram = lambda name, shape: nc.dram_tensor(name, shape, F32, kind="Internal").ap()
        s.dst_rows = dram("dst_rows", (NCH * P, PW))
        s.src_rows = dram("src_rows", (NCH * P, 2))
        t0, t1 = dram("table_lin1", (NB * P, D)), dram("table_gcn0", (NB * P, D))
        t2, t3 = dram("table_gcn1", (NB * P, HID)), dram("table_gcn2", (NB * P, HID))
        t4, t5 = dram("table_gcn3", (NB * P, D)), dram("table_mean", (NB * P, D))
        t6, t7 = dram("table_gat", (NB * P, D + HEADS)), dram("table_score", (NB * P, HEADS))
        s.prefilled = c.sem("rows_prefilled")
        s.counted, s.summed, s.ended = c.sem("bins_counted"), c.sem("bins_summed"), c.sem("bins_ended")
        s.turned, s.passed, s.binned = c.sem("ends_turned"), c.sem("ends_passed"), c.sem("chunks_binned")
        m = s.m = Scratch()
        m.h_mm = c.sem("mlp_hidden_multiplied")
        m.silu = c.sem("mlp_hidden_ready")
        m.w_mm = c.sem("mlp_weights_multiplied")
        m.copied = c.sem("payload_ready")
        m.small = c.sem("small_rows_ready")
        m.kept = c.sem("small_fields_kept")
        m.prod = c.sem("tensor_products_ready")
        m.scaled = c.sem("scaled_one_hots_ready")
        m.fed = c.sem("tile_fed")
        m.turned = c.sem("tile_turned")
        m.back = c.sem("turned_tile_back")
        m.multiplied = c.sem("tile_multiplied")
        m.taken = c.sem("tile_taken")
        m.rooted = c.sem("root_taken")
        m.part = c.sem("segment_ready")
        m.centred = c.sem("segment_centred")
        m.shifted = c.sem("segment_shifted")
        m.cut = c.sem("segment_cut")
        m.powered = c.sem("exponential_taken")
        m.reduced = c.sem("scores_reduced")
        m.looked = c.sem("node_scores_looked_up")
        m.scored = c.sem("edge_scores_ready")
        m.weighted = c.sem("rows_weighted")
        m.ea = [c.sem(f"edge_scalars_loaded_{h}") for h in range(2)]
        m.sc = [c.sem(f"rows_scattered_{h}") for h in range(2)]
        m.ss = [c.sem(f"small_rows_scattered_{h}") for h in range(2)]
        m.pay = [c.sem(f"payload_loaded_{h}") for h in range(2)]
        run(c, A, s, out, (t0, t1, t2, t3, t4, t5, t6, t7), upto)


def run(c, A, s, out, tables, upto):
    nc = c.nc
    t0, t1, t2, t3, t4, t5, t6, t7 = tables
    ps, acc, x = c.ps, c.acc, c.x
    v = nc.vector

    def flat(ap):
        return ap.rearrange("p a b -> p (a b)")

    def dump():
        with nc.Block() as block:
            @block.sync
            def _(sp):
                sp.dma_start(tiles(out[0:(NT - 1) * P, :], 0, 0), x[:, 0:NT - 1, :]).then_inc(c.store.sem, 16)
                sp.dma_start(out[(NT - 1) * P:N, :], x[0:LASTN, NT - 1, :]).then_inc(c.store.sem, 16)
                sp.wait_ge(c.store.sem, c.store.n + 32)

    setup(c, A, s)
    prepare_weights(c, s)
    sort_key(c, s, "dst")
    sort_key(c, s, "src")
    fields(c, s)
    scatter_dst(c, A, s)
    scatter_src(c, s)

    def feed_x(k, slot):
        return nc.scalar.activation(s.u[:, slot, 0:D], flat(x[:, one(k), :]), ACT.Copy)

    def take_rows(st, k, bank):
        return v.tensor_copy(flat(acc[:, one(k), 0:D]), ps[:, bank, 0:D])
    node_product(c, s, feed_x, 1, P, [(0, s.lin1[:, :], 0, D, True, True)], 0, take_rows)
    write_table(c, acc[:, :, 0:D], t0, D)
    with nc.Block() as block:
        @block.vector
        def _(dve):
            v.memset(acc[:, :, :], 0.0)
            Steps(dve, c.dve)(v.memset(s.prod[:, :, :, :], 1.0))
    messages(c, s, t0)
    degrees(c, s)

    def feed_msg(k, slot):
        return nc.scalar.activation(s.u[:, slot, :].rearrange("p (g w) -> p g w", g=4),
                                    flat(acc[:, one(k), :]).rearrange("p (g w) -> p g w", g=4)[:, :, 0:2 * MUL], ACT.Copy)

    def take_msg(st, k, bank):
        xs = flat(x[:, one(k), 0:MUL])
        xv = flat(x[:, one(k), MUL:D]).rearrange("p (u i) -> p i u", i=3)
        st(v.tensor_tensor(xs, xs, ps[:, bank, 0:MUL], ALU.add))
        st(v.tensor_tensor(xv, xv, ps[:, bank, MUL:D].rearrange("p (i u) -> p i u", i=3), ALU.add))
        return stats(c, s, st, k, flat(x[:, one(k), :]))
    node_product(c, s, feed_msg, 4, 2 * MUL,
                 [(g, (s.lin2v if g else s.lin2s)[:, :], MUL * g, MUL * g + MUL, True, True) for g in range(4)],
                 4, take_msg)
    normalise(c, s, self_term=True, table=t1)
    if upto == 0:
        return dump()

    def feed_scaled(width):
        def feed(k, slot):
            return nc.scalar.activation(s.u[:, slot, 0:width], flat(acc[:, one(k), 0:width]), ACT.Copy,
                                        scale=c.dinv[:, one(k)])
        return feed

    def take_conv(l):
        def take(st, k, bank):
            y = flat(acc[:, one(k), 0:HID])
            st(v.tensor_tensor(y, ps[:, bank, 0:HID], s.b[l][:, :], ALU.add))
            return stats(c, s, st, k, y)
        return take
    aggregate(c, "dst", t1, D, D)
    node_product(c, s, feed_scaled(D), 1, P, [(0, s.w[0][:, :], 0, HID, True, True)], 3, take_conv(0))
    conv_norm(c, s, 0, t2)
    for l, tin, tout in ((1, t2, t3), (2, t3, None)):
        aggregate(c, "dst", tin, HID, HID)
        node_product(c, s, feed_scaled(HID), 2, P,
                     [(a, s.w[l][:, a * HID:(a + 1) * HID], 0, HID, a == 0, a == 1) for a in range(2)], 3, take_conv(l))
        conv_norm(c, s, l, tout)

    def feed_acc(k, slot):
        return nc.scalar.activation(s.u[:, slot, :], flat(acc[:, one(k), 0:HID]), ACT.Copy)
    node_product(c, s, feed_acc, 2, P, [(a, s.w3[:, a * D:(a + 1) * D], 0, D, a == 0, a == 1) for a in range(2)],
                 0, take_rows)
    write_table(c, acc[:, :, 0:D], t4, D)
    aggregate(c, "dst", t4, D, D)
    add_gcn(c, s)
    normalise(c, s, table=t5, clear=True)
    if upto == 1:
        return dump()

    with nc.Block() as block:
        @block.vector
        def _(dve):
            Steps(dve, c.dve)(v.memset(c.rows[:, :, :, D:D + 1], 1.0))
    aggregate(c, "src", t5, D, D + 1)
    with nc.Block() as block:
        @block.vector
        def _(dve):
            st = Steps(dve, c.dve)
            st(v.tensor_scalar(s.has[:, :], acc[:, :, D], 0.0, None, ALU.is_gt))
            st(v.tensor_scalar(s.rcnt[:, :], acc[:, :, D], 1.0, None, ALU.max)).wait()
            st(v.reciprocal(s.rcnt[:, :], s.rcnt[:, :]))

    def feed_mean(k, slot):
        nc.scalar.activation(s.u[:, slot, 0:D], flat(acc[:, one(k), 0:D]), ACT.Copy, scale=s.rcnt[:, one(k)])
        return nc.scalar.activation(s.u[:, slot, D:2 * D], flat(x[:, one(k), :]), ACT.Copy)

    def take_mean(st, k, bank):
        t, y = s.ex[:, 0, 0, 0:D], flat(x[:, one(k), :])
        st(v.scalar_tensor_tensor(t, s.bneigh[:, :], s.has[:, one(k)], ps[:, bank, 0:D], ALU.mult, ALU.add)).wait()
        st(v.tensor_tensor(t, t, s.bself[:, :], ALU.add)).wait()
        st(v.scalar_tensor_tensor(y, t, 0.0, y, ALU.max, ALU.add))
        return stats(c, s, st, k, y)
    node_product(c, s, feed_mean, 2, P, [(0, s.wneigh[:, :], 0, D, True, False), (1, s.wself[:, :], 0, D, False, True)],
                 5, take_mean)
    normalise(c, s, table=t5)
    if upto == 2:
        return dump()

    def take_gat(st, k, bank):
        st(v.tensor_copy(flat(acc[:, one(k), 0:D + HEADS]), ps[:, bank, 0:D + HEADS]))
        return v.tensor_copy(flat(s.nt[:, one(k), 0:HEADS]), ps[:, bank, D + HEADS:D + 2 * HEADS])
    node_product(c, s, feed_x, 1, P, [(0, s.wg[:, :], 0, D + 4, True, True)], 1, take_gat)
    write_table(c, acc[:, :, 0:D + HEADS], t6, D + HEADS)
    write_table(c, acc[:, :, D:D + HEADS], t7, HEADS)
    with nc.Block() as block:
        @block.vector
        def _(dve):
            Steps(dve, c.dve)(v.memset(s.mx[:, :, :], NEG))
    scores_max(c, s, t7)
    node_max(c, s)
    attend(c, s, t6)
    add_gat(c, s)
    normalise(c, s, out=out)


_PLAIN = ["x", "L0_gnn_w_lin1_s", "L0_gnn_w_lin1_v", "L0_gnn_fc_w1", "L0_gnn_fc_w2", "L0_gnn_w_lin2_s",
          "L0_gnn_w_lin2_v", "L1_gnn_W0", "L1_gnn_b0", "L1_gnn_W1", "L1_gnn_b1", "L1_gnn_W2", "L1_gnn_b2",
          "L1_gnn_W3", "L1_gnn_b3", "L1_gnn_a0", "L1_gnn_a1", "L1_gnn_a2", "L1_gnn_g0", "L1_gnn_beta0",
          "L1_gnn_g1", "L1_gnn_beta1", "L1_gnn_g2", "L1_gnn_beta2", "L2_gnn_b_self", "L2_gnn_b_neigh",
          "L3_gnn_W_src", "L3_gnn_W_dst", "L3_gnn_att_src", "L3_gnn_att_dst", "L3_gnn_bias", "L3_gnn_prelu_w"]
UPTO = None


def kernel(**inputs):
    import concourse.bacc as _bacc
    from concourse.bass_utils import run_bass_kernel_spmd as _run

    whole = (TC - 1) * P
    arrays = {n: np.ascontiguousarray(inputs[n]) for n in _PLAIN}
    for k in ("dst", "src"):
        e = np.ascontiguousarray(inputs[k])
        arrays[k + "_main"] = np.ascontiguousarray(e[:whole].reshape(TC - 1, P).T)
        arrays[k + "_tail"] = np.ascontiguousarray(e[whole:].reshape(TAIL, 1))
    a = np.ascontiguousarray(inputs["edge_attr_4"])
    arrays["ea4_main"] = np.ascontiguousarray(a[:whole].reshape(TC - 1, P, 4).transpose(1, 0, 2))
    arrays["ea4_tail"] = np.ascontiguousarray(a[whole:])
    arrays["ea8"] = np.ascontiguousarray(np.ascontiguousarray(inputs["edge_attr_8"]).T)
    arrays["WsT"] = np.ascontiguousarray(np.ascontiguousarray(inputs["L2_gnn_W_self"]).T)
    arrays["WnT"] = np.ascontiguousarray(np.ascontiguousarray(inputs["L2_gnn_W_neigh"]).T)
    nc = _bacc.Bacc("TRN2", target_bir_lowering=False, num_devices=1)
    aps = {n: nc.dram_tensor("in_" + n, a.shape, mybir.dt.from_np(a.dtype), kind="ExternalInput").ap()
           for n, a in arrays.items()}
    out = nc.dram_tensor("out_x", (N, D), F32, kind="ExternalOutput").ap()
    gnn(nc, aps, out, UPTO)
    r = _run(nc, [{"in_" + n: a for n, a in arrays.items()}], core_ids=[0])
    return r.results[0]["out_x"]
```

```python
import numpy as np
import concourse.bass as bass
from concourse import mybir
from contextlib import ExitStack

F32 = mybir.dt.float32
I32 = mybir.dt.int32
U32 = mybir.dt.uint32
ALU = mybir.AluOpType
ACT = mybir.ActivationFunctionType
AX = mybir.AxisListType

P = 128
N = 6250
E = 100000
D = 128
HID = 256
MUL = 32
NT = -(-N // P)
NB = NT + 1
LASTN = N - (NT - 1) * P
TC = -(-E // P)
TAIL = E - (TC - 1) * P
PADKEY = NT * P
G8 = 8
NG = 104
NCH = NG * G8
assert NCH >= (TC * P + NB * (P - 1)) // P
SCG = TC // G8
REST = TC - SCG * G8
PW = 136
EV, SRC, LO = 128, 131, 132
AW = 260
GW = 260
EPS = 1e-5
SILU_NORM = 1.6791767923989418
NEG = -3.0e38
SEGT = 5
NSEG = NB // SEGT
HEADS, CH = 2, 64
SLOPE = 0.2


class Count:

    def __init__(self, sem):
        self.sem, self.n = sem, 0


class Steps:

    def __init__(self, eng, count):
        self.eng, self.c, self.turn, self.per, self.k = eng, count, None, 0, 0

    def loop(self, turn, per):
        self.turn, self.per, self.k = turn, per, 0

    def end(self, turns):
        assert self.k == self.per, (self.k, self.per)
        self.c.n += turns * self.per
        self.turn = None

    def __call__(self, ins):
        ins.then_inc(self.c.sem, 1)
        if self.turn is None:
            self.c.n += 1
        else:
            self.k += 1
        return self

    def reached(self):
        return self.c.n if self.turn is None else self.turn * self.per + (self.c.n + self.k)

    def wait(self):
        self.eng.wait_ge(self.c.sem, self.reached())


class Chip:

    def __init__(self, nc, ctx):
        self.nc, self.ctx = nc, ctx
        sb = self.sb
        self.ps = ctx.enter_context(nc.psum_tensor("ps", [P, 8, 512], F32))
        self.ident = sb("ident", [P, P])
        self.ones = sb("ones", [P, P])
        self.upper = sb("upper", [P, P])
        self.iota = sb("iota", [P, P])
        self.iota_b = sb("iota_b", [P, NB])
        self.eps = sb("eps", [P, 1])
        self.x = sb("x", [P, NB, D])
        self.acc = sb("acc", [P, NB, AW])
        self.mv = sb("mv", [P, NB, 2])
        self.rstd = sb("rstd", [P, NB])
        self.dinv = sb("dinv", [P, NB])
        self.meta = {k: sb(f"meta_{k}", [P, NCH, 2]) for k in ("dst", "src")}
        self.bin_of = {k: sb(f"bin_of_{k}", [1, NCH], I32) for k in ("dst", "src")}
        self.idx = sb("idx", [P, 4, G8], I32)
        self.rows = sb("rows", [P, 2, G8, GW])
        self.hot = sb("hot", [P, 2, G8, P])
        self.pay = sb("pay", [P, 2, G8, PW])
        self.iota_c = self.hot[0:64, 0, :, :].rearrange("p j n -> p (j n)")[:, 0:NCH]
        sem = self.sem
        self.ready = sem("constants_ready")
        self.held = sem("held")
        self.dve = sem("dve_step")
        self.pool = sem("pool_step")
        self.act = sem("act_step")
        self.load = sem("load_done")
        self.store = sem("store_done")
        self.idx_ready = sem("indices_ready")
        self.gathered = [sem(f"gathered_{h}") for h in range(4)]
        self.scattered = [sem(f"scattered_{h}") for h in range(2)]
        self.hot_ready = sem("one_hot_ready")
        self.mm = sem("chunk_multiplied")
        self.added = sem("chunk_added")

    def sb(self, name, shape, dt=F32):
        return self.ctx.enter_context(self.nc.sbuf_tensor(name, shape, dt))

    def sem(self, name):
        return Count(self.ctx.enter_context(self.nc.semaphore(name)))

    def hold(self, eng, count, value):
        eng.wait_ge(count.sem, value)
        eng.sem_inc(self.held.sem, 1)


def tiles(ap, n, width):
    return ap.rearrange("(n p) f -> p n f", p=P)


def setup(c, A, s):
    nc = c.nc
    with nc.Block() as block:

        @block.gpsimd
        def _(pool):
            st = Steps(pool, c.pool)
            st(pool.memset(c.ident[:, :], 0.0))
            st(pool.memset(c.ones[:, :], 1.0))
            st(pool.memset(c.upper[:, :], 0.0))
            st.wait()
            pool.affine_select(out=c.ident[:, :], in_=c.ident[:, :], compare_op=ALU.not_equal, fill=1.0,
                               base=0, pattern=[[-1, P]], channel_multiplier=1)
            pool.affine_select(out=c.upper[:, :], in_=c.upper[:, :], compare_op=ALU.is_ge, fill=1.0,
                               base=0, pattern=[[-1, P]], channel_multiplier=1)
            pool.iota(c.iota[:, :], pattern=[[1, P]], base=0, channel_multiplier=0,
                      allow_small_or_imprecise_dtypes=True)
            pool.iota(c.iota_b[:, :], pattern=[[1, NB]], base=0, channel_multiplier=0,
                      allow_small_or_imprecise_dtypes=True)
            pool.iota(c.iota_c[:, :], pattern=[[1, NCH]], base=0, channel_multiplier=0,
                      allow_small_or_imprecise_dtypes=True)
            pool.memset(c.eps[:, :], EPS).then_inc(c.ready.sem, 1)

        @block.vector
        def _(dve):
            st = Steps(dve, c.dve)
            st(dve.memset(s.key["dst"][:, :], PADKEY))
            st(dve.memset(s.key["src"][:, :], PADKEY))
            st(dve.memset(s.attr[:, :, :], 0.0))
            st(dve.memset(c.x[:, NT - 1:NB, :], 0.0))
            st(dve.memset(s.lin1[:, :], 0.0))
            st(dve.memset(s.one_row[:, :], 1.0))
            st(dve.memset(s.pos["dst"][:, :], 0.0))
            st(dve.memset(s.pos["src"][:, :], 0.0))
            st(dve.memset(c.pay[:, :, :, :], 0.0))
            for k in ("dst", "src"):
                st(dve.memset(c.meta[k][:, :, 0], 0.0))
                st(dve.memset(c.meta[k][:, :, 1], -1.0))
            st(dve.memset(c.rows[:, :, :, :], 1.0))
            st.wait()
            st(dve.memset(c.pay[:, :, :, LO], -1.0))

        @block.sync
        def _(sp):
            sp.wait_ge(c.dve.sem, 15)
            n = 0
            for k in ("dst", "src"):
                sp.dma_start(s.key[k][:, 0:TC - 1], A[k + "_main"]).then_inc(c.load.sem, 16)
                sp.dma_start(s.key[k][0:TAIL, TC - 1:TC], A[k + "_tail"]).then_inc(c.load.sem, 16)
                n += 2
            sp.dma_start(s.attr[:, 0:TC - 1, :], A["ea4_main"]).then_inc(c.load.sem, 16)
            sp.dma_start(s.attr[0:TAIL, TC - 1, :], A["ea4_tail"]).then_inc(c.load.sem, 16)
            sp.dma_start(c.x[:, 0:NT - 1, :], tiles(A["x"][0:(NT - 1) * P, :], NT - 1, D)).then_inc(c.load.sem, 16)
            sp.dma_start(c.x[0:LASTN, NT - 1, :], A["x"][(NT - 1) * P:N, :]).then_inc(c.load.sem, 16)
            n += 4
            for dst, src in s.weights:
                sp.dma_start(dst, src).then_inc(c.load.sem, 16)
                n += 1
            sp.dma_start(s.src_rows.rearrange("(p j) w -> p j w", p=P), c.meta["src"][:, :, :]).then_inc(c.store.sem, 16)
            sp.wait_ge(c.load.sem, 16 * n)
            s.n_loads = n
            sp.wait_ge(c.store.sem, 16)

        @block.scalar
        def _(act):
            act.wait_ge(c.dve.sem, 15)
            width = 2 * G8 * PW
            view = s.dst_rows.rearrange("(p j) w -> p (j w)", p=P)
            src = c.pay[:, :, :, :].rearrange("p h g w -> p (h g w)")
            with act.Fori(0, NG // 2) as i:
                act.dma_start(view[:, bass.ds(i * width, width)], src).then_inc(s.prefilled.sem, 16)
    c.ready.n = 1
    c.pool.n = 3
    c.load.n = 16 * s.n_loads
    c.store.n = 16
    s.prefilled.n = 16 * (NG // 2)


def sort_key(c, s, k):
    nc = c.nc
    key, binf, lof, mask, run, pos = s.key[k], s.binf, s.lof[k], s.mask, s.run, s.pos[k]
    cnt, base = s.cnt, s.base[k]
    if k == "dst":
        s.lo_done = True
    with nc.Block() as block:

        @block.vector
        def _(dve):
            st = Steps(dve, c.dve)
            st(dve.tensor_scalar(s.ki[:, :], key[:, :], 7, None, ALU.arith_shift_right))
            st(dve.tensor_scalar(s.kl[:, :], key[:, :], P - 1, None, ALU.bitwise_and)).wait()
            st(dve.tensor_copy(binf[:, :], s.ki[:, :]))
            st(dve.tensor_copy(lof, s.kl[:, :])).wait()
            with dve.Fori(0, NB) as b:
                st.loop(b, 2)
                st(dve.tensor_scalar(mask[:, :], binf[:, :], c.iota_b[:, bass.ds(b, 1)], None, ALU.is_equal)).wait()
                st(dve.tensor_reduce(cnt[:, bass.ds(b, 1)], mask[:, :], AX.X, ALU.add)).wait()
            st.end(NB)
            dve.wait_ge(c.dve.sem, c.dve.n)
            dve.sem_inc(s.counted.sem, 1)
            dve.wait_ge(s.summed.sem, s.summed.n + 1)
            st(dve.tensor_scalar(s.ci[:, :], c.ps[:, 0, 0:NB], float(P - 1), None, ALU.add)).wait()
            st(dve.tensor_scalar(s.cj[:, :], s.ci[:, :], 7, None, ALU.arith_shift_right)).wait()
            st(dve.tensor_copy(s.nch[:, :], s.cj[:, :])).wait()
            st(dve.tensor_tensor_scan(s.inc[:, :], c.ones[:, 0:NB], s.nch[:, :], 0.0, ALU.mult, ALU.add)).wait()
            st(dve.tensor_tensor(s.exc[:, :], s.inc[:, :], s.nch[:, :], ALU.subtract)).wait()
            dve.sem_inc(s.ended.sem, 1)
            st(dve.tensor_scalar(s.exc[:, :], s.exc[:, :], float(P), -1.0, ALU.mult, ALU.add)).wait()
            st(dve.tensor_tensor(base[:, :], s.exc[:, :], c.ps[:, 1, 0:NB], ALU.add)).wait()
            dve.wait_ge(s.turned.sem, s.turned.n + 1)
            st(dve.tensor_copy(s.end_t[0:NB, :], c.ps[0:NB, 2, 0:1])).wait()
            st(dve.tensor_scalar(s.past[0:NT, :], c.iota_c[0:NT, :], s.end_t[0:NT, 0:1], None, ALU.is_ge)).wait()
            dve.sem_inc(s.passed.sem, 1)
            dve.wait_ge(s.binned.sem, s.binned.n + 1)
            half = NCH // 2
            st(dve.tensor_copy(c.bin_of[k][0:1, 0:half], c.ps[0:1, 3, 0:half]))
            st(dve.tensor_copy(c.bin_of[k][0:1, half:NCH], c.ps[0:1, 4, 0:half]))
            with dve.Fori(0, NB) as b:
                st.loop(b, 3)
                st(dve.tensor_scalar(mask[:, :], binf[:, :], c.iota_b[:, bass.ds(b, 1)], None, ALU.is_equal)).wait()
                st(dve.tensor_tensor_scan(run[:, :], s.one_row[:, :], mask[:, :], base[:, bass.ds(b, 1)], ALU.mult, ALU.add))
                c.hold(dve, c.dve, b * 3 + (c.dve.n + 2))
                st(dve.copy_predicated(pos[:, :], mask[:, :].bitcast(U32), run[:, :])).wait()
            st.end(NB)
            dve.wait_ge(c.dve.sem, c.dve.n)
            st(dve.tensor_copy(s.ki[:, :], pos[:, :])).wait()
            st(dve.tensor_scalar(s.kl[:, :], s.ki[:, :], P - 1, None, ALU.bitwise_and))
            st(dve.tensor_scalar(s.kh[:, :], s.ki[:, :], 7, None, ALU.arith_shift_right)).wait()
            st(dve.tensor_copy(run[:, :], s.kl[:, :]))
            st(dve.tensor_copy(mask[:, :], s.kh[:, :])).wait()
            st(dve.scalar_tensor_tensor(pos[:, :], run[:, :], float(NCH), mask[:, :], ALU.mult, ALU.add)).wait()

        @block.tensor
        def _(pe):
            pe.wait_ge(s.counted.sem, s.counted.n + 1)
            pe.matmul(c.ps[:, 0, 0:NB], c.ones[:, :], cnt[:, :], start=True, stop=True)
            pe.matmul(c.ps[:, 1, 0:NB], c.upper[:, :], cnt[:, :], start=True, stop=True).then_inc(s.summed.sem, 1)
            pe.wait_ge(s.ended.sem, s.ended.n + 1)
            pe.transpose(c.ps[0:NB, 2, 0:P], s.inc[:, :], c.ident[:, :]).then_inc(s.turned.sem, 1)
            pe.wait_ge(s.passed.sem, s.passed.n + 1)
            half = NCH // 2
            for i in range(2):
                last = pe.matmul(c.ps[0:1, 3 + i, 0:half], c.ones[0:NT, 0:1], s.past[0:NT, i * half:(i + 1) * half],
                                 start=True, stop=True)
            last.then_inc(s.binned.sem, 1)
    for x in (s.counted, s.summed, s.ended, s.turned, s.passed, s.binned):
        x.n += 1


def fields(c, s):
    nc = c.nc
    with nc.Block() as block:

        @block.vector
        def _(dve):
            st = Steps(dve, c.dve)
            for i, (k, out) in enumerate((("src", s.fld[:, :, 4]), ("dst", s.fsrc[:, :, 0]))):
                st(dve.tensor_copy(s.run[:, :], s.key[k][:, :])).wait()
                st(dve.scalar_tensor_tensor(out, s.run[:, :], float(PADKEY), s.run[:, :], ALU.is_lt, ALU.mult)).wait()
            st(dve.tensor_copy(s.fld[:, :, 5], s.lof["dst"]))
            st(dve.tensor_copy(s.fsrc[:, :, 1], s.lof["src"])).wait()


def groups(eng, total, body, ahead=0, per=2):
    turns = total // per
    for h in range(per):
        body(0, h)
    with eng.Fori(1, turns - (ahead > 0)) as i:
        for h in range(per):
            body(i, h)
    if ahead:
        for h in range(per):
            body(turns - 1, h)


def after(i, h, by=1, per=2):
    if h + by < per:
        return i, h + by
    return None if isinstance(i, int) and i == NG // per - 1 else (i + 1, h + by - per)


def first(i):
    return isinstance(i, int) and i == 0


def at(q, per, start, n):
    if isinstance(q, int):
        return slice(q * per + start, q * per + start + n)
    return bass.ds(q * per + start, n)


def scatter_dst(c, A, s):
    nc = c.nc
    m = s.m
    n0 = SCG // 2

    def all_groups(eng, body):
        groups(eng, SCG, lambda i, h: body(i, h, G8))
        body(n0, 0, G8)
        body(n0, 1, REST)

    with nc.Block() as block:

        @block.sync
        def _(sp):
            def load(i, h, n):
                q = 2 * i + h
                width = G8 * P if n == G8 else E - SCG * G8 * P
                if not first(i):
                    sp.wait_ge(m.h_mm.sem, q * 2 - 2 + m.h_mm.n)
                sp.dma_start(s.ea8[:, h, 0:width], A["ea8"][:, at(q, G8 * P, 0, width)]).then_inc(m.ea[h].sem, 16)
            all_groups(sp, load)

        @block.tensor
        def _(pe):
            def mlp(i, h, n):
                q = 2 * i + h
                pe.wait_ge(m.ea[h].sem, i * 16 + (m.ea[h].n + 16))
                for b in range(2):
                    w = min(512, n * P - 512 * b)
                    if not (first(i) and h == 0):
                        pe.wait_ge(m.silu.sem, q * 2 + (m.silu.n + b - 1))
                    pe.matmul(c.ps[0:64, b, 0:w], s.fc1[:, :], s.ea8[:, h, 512 * b:512 * b + w],
                              start=True, stop=True).then_inc(m.h_mm.sem, 1)
                for b in range(2):
                    pe.wait_ge(m.silu.sem, q * 2 + (m.silu.n + b + 1))
                    if not (first(i) and h == 0):
                        pe.wait_ge(m.copied.sem, q * 2 + (m.copied.n + b - 1))
                    for j in range(min(4, n - 4 * b)):
                        last = pe.matmul(c.ps[:, 2 + b, j * P:(j + 1) * P], s.hid[:, b, j * P:(j + 1) * P],
                                         s.fc2[:, :], start=True, stop=True)
                    last.then_inc(m.w_mm.sem, 1)
            all_groups(pe, mlp)

        @block.scalar
        def _(act):
            def payload(i, h, n):
                q = 2 * i + h
                for b in range(2):
                    w = min(512, n * P - 512 * b)
                    act.wait_ge(m.h_mm.sem, q * 2 + (m.h_mm.n + b + 1))
                    if not (first(i) and h == 0):
                        act.wait_ge(m.w_mm.sem, q * 2 + (m.w_mm.n + b - 1))
                    nc.scalar.activation(s.hid[:, b, 0:w], c.ps[0:64, b, 0:w], ACT.Silu).then_inc(m.silu.sem, 1)
                if not first(i):
                    act.wait_ge(m.sc[h].sem, i * (16 * G8) + m.sc[h].n)
                nc.scalar.activation(c.idx[:, h, 0:n], s.pos["dst"][:, at(q, G8, 0, n)], ACT.Copy)
                nc.scalar.activation(c.pay[:, h, 0:n, EV:EV + 5], s.fld[:, at(q, G8, 0, n), 1:6], ACT.Copy)
                for b in range(2):
                    k = min(4, n - 4 * b)
                    act.wait_ge(m.w_mm.sem, q * 2 + (m.w_mm.n + b + 1))
                    w4 = c.ps[:, 2 + b, :].rearrange("p (j a t u) -> p j a t u", j=4, a=2, t=2)
                    to = c.pay[:, h, 4 * b:4 * b + k, 0:P].rearrange("p j (a t u) -> p j a t u", a=2, t=2)
                    nc.scalar.activation(to[:, :, :, 1, :], w4[:, 0:k, :, 1, :], ACT.Copy)
                    for j in range(k):
                        last = nc.scalar.activation(to[:, j, :, 0, :], w4[:, j, :, 0, :], ACT.Copy,
                                                    scale=s.attr[:, at(q, G8, 4 * b + j, 1), 0])
                    last.then_inc(m.copied.sem, 1)
            act.wait_ge(s.prefilled.sem, s.prefilled.n)
            all_groups(act, payload)

        @block.gpsimd
        def _(pool):
            pool.wait_ge(s.prefilled.sem, s.prefilled.n)
            def send(i, h, n):
                c.hold(pool, m.copied, i * 4 + (h * 2 + m.copied.n + 2))
                for j in range(n):
                    pool.indirect_dma_start(s.dst_rows, bass.IndirectOffsetOnAxis(ap=c.idx[:, h, j:j + 1], axis=0),
                                            c.pay[:, h, j, :], None).then_inc(m.sc[h].sem, 16)
            all_groups(pool, send)
            pool.wait_ge(m.sc[0].sem, m.sc[0].n + 16 * G8 * (n0 + 1))
            pool.wait_ge(m.sc[1].sem, m.sc[1].n + 16 * (G8 * n0 + REST))
    for x in (m.h_mm, m.silu, m.w_mm, m.copied):
        x.n += 2 * (SCG + 1)
    m.ea[0].n += 16 * (n0 + 1)
    m.ea[1].n += 16 * (n0 + 1)
    m.sc[0].n += 16 * G8 * (n0 + 1)
    m.sc[1].n += 16 * (G8 * n0 + REST)


def scatter_src(c, s):
    nc = c.nc
    m = s.m
    n0 = SCG // 2

    def all_groups(eng, body):
        groups(eng, SCG, lambda i, h: body(i, h, G8))
        body(n0, 0, G8)
        body(n0, 1, REST)

    with nc.Block() as block:

        @block.scalar
        def _(act):
            def payload(i, h, n):
                q = 2 * i + h
                if not first(i):
                    act.wait_ge(m.ss[h].sem, i * (16 * G8) + m.ss[h].n)
                nc.scalar.activation(c.idx[:, h, 0:n], s.pos["src"][:, at(q, G8, 0, n)], ACT.Copy)
                nc.scalar.activation(s.small[:, h, 0:n, :], s.fsrc[:, at(q, G8, 0, n), :],
                                     ACT.Copy).then_inc(m.small.sem, 1)
            all_groups(act, payload)

        @block.gpsimd
        def _(pool):
            def send(i, h, n):
                c.hold(pool, m.small, i * 2 + (h + m.small.n + 1))
                for j in range(n):
                    pool.indirect_dma_start(s.src_rows, bass.IndirectOffsetOnAxis(ap=c.idx[:, h, j:j + 1], axis=0),
                                            s.small[:, h, j, :], None).then_inc(m.ss[h].sem, 16)
            all_groups(pool, send)

        @block.sync
        def _(sp):
            sp.wait_ge(m.ss[0].sem, m.ss[0].n + 16 * G8 * (n0 + 1))
            sp.wait_ge(m.ss[1].sem, m.ss[1].n + 16 * (G8 * n0 + REST))
            sp.dma_start(c.meta["src"][:, :, :], s.src_rows.rearrange("(p j) w -> p j w", p=P)).then_inc(c.load.sem, 16)
            sp.wait_ge(c.load.sem, c.load.n + 16)
    m.small.n += SCG + 1
    m.ss[0].n += 16 * G8 * (n0 + 1)
    m.ss[1].n += 16 * (G8 * n0 + REST)
    c.load.n += 16


def load_bins(c, eng, k, q):
    _, vals = c.nc.values_load_multi_w_load_instructions(
        c.bin_of[k][0:1, at(q, G8, 0, G8)], engines=[eng], min_val=0, max_val=NB - 1,
        skip_runtime_bounds_check_because="the sort makes them from 0 to NB - 1")
    return vals


def one_hot(c, h, places):
    c.nc.vector.tensor_tensor(c.hot[:, h, :, :], c.iota[:, :].unsqueeze(1).broadcast_to([P, G8, P]),
                              places.broadcast_to([P, G8, P]), ALU.is_equal).then_inc(c.hot_ready.sem, 1)


def add_chunk(c, dve, q, j, bin_, width, product):
    dve.wait_ge(c.mm.sem, q * G8 + (c.mm.n + j + 1))
    if not (first(q) and j == 0):
        dve.wait_ge(c.added.sem, q * G8 + (c.added.n + j))
    to = c.acc[:, bass.ds(bin_, 1), 0:width]
    c.nc.vector.tensor_tensor(to, to, product, ALU.add).then_inc(c.added.sem, 1)


def end_pass(c, per=2):
    c.mm.n += NCH
    c.added.n += NCH
    c.hot_ready.n += NG
    c.idx_ready.n += NG
    for g in c.gathered[0:per]:
        g.n += 16 * G8 * (NG // per)


def messages(c, s, table):
    nc = c.nc
    m = s.m
    RING = 4
    rows3 = s.dst_rows.rearrange("(p j) w -> p j w", p=P)
    rows_of = lambda r: c.rows[:, r % 2, :, (r // 2) * D:(r // 2 + 1) * D]

    with nc.Block() as block:

        @block.sync
        def _(sp):
            def load(i, r):
                q = RING * i + r
                if not first(i):
                    c.hold(sp, c.mm, q * G8 + (c.mm.n - (RING - 1) * G8))
                    sp.wait_ge(m.kept.sem, q + (m.kept.n - RING + 1))
                sp.dma_start(s.pay4[:, r, :, :], rows3[:, at(q, G8, 0, G8), :]).then_inc(m.pay[r].sem, 16)
            groups(sp, NG, load, per=RING)

        @block.scalar
        def _(act):
            def indices(i, r):
                q = RING * i + r
                act.wait_ge(m.pay[r].sem, i * 16 + (m.pay[r].n + 16))
                if not first(i):
                    act.wait_ge(m.prod.sem, q * 2 + (m.prod.n - 2 * (RING - 1)))
                nc.scalar.activation(c.idx[:, r, :], s.pay4[:, r, :, SRC], ACT.Copy).then_inc(c.idx_ready.sem, 1)
                nc.scalar.activation(c.meta["dst"][:, at(q, G8, 0, G8), :], s.pay4[:, r, :, SRC:SRC + 2],
                                     ACT.Copy).then_inc(m.kept.sem, 1)

            def scaled(i, r):
                q = RING * i + r
                if after(i, r, 2, RING):
                    indices(*after(i, r, 2, RING))
                act.wait_ge(m.pay[r].sem, i * 16 + (m.pay[r].n + 16))
                if not (first(i) and r < 2):
                    act.wait_ge(m.prod.sem, q * 2 + (m.prod.n - 2))
                for j in range(G8):
                    w13 = s.pay4[:, r, j, 0:P].rearrange("p (t u) -> p t u", t=4)[:, 1:4:2, :]
                    for a in range(3):
                        last = nc.scalar.activation(s.wev[:, r % 2, j, a, :, :], w13, ACT.Copy,
                                                    scale=s.pay4[:, r, j, EV + a:EV + a + 1])
                    if j % 4 == 3:
                        last.then_inc(m.scaled.sem, 1)
            indices(0, 0)
            indices(0, 1)
            groups(act, NG, scaled, ahead=2, per=RING)

        @block.gpsimd
        def _(pool):
            def gather(i, r):
                c.hold(pool, c.idx_ready, i * RING + (r + c.idx_ready.n + 1))
                for j in range(G8):
                    pool.indirect_dma_start(rows_of(r)[:, j, :], None, table,
                                            bass.IndirectOffsetOnAxis(ap=c.idx[:, r, j:j + 1], axis=0)
                                            ).then_inc(c.gathered[r].sem, 16)
            groups(pool, NG, gather, per=RING)

        @block.vector
        def _(dve):
            def hot(i, r):
                q = RING * i + r
                dve.wait_ge(m.pay[r].sem, i * 16 + (m.pay[r].n + 16))
                if not (first(i) and r < 2):
                    dve.wait_ge(c.mm.sem, q * G8 + (c.mm.n - G8))
                one_hot(c, r % 2, s.pay4[:, r, :, LO:LO + 1])

            def products(i, r, b):
                q = RING * i + r
                js = slice(4 * b, 4 * b + 4)
                if b == 0:
                    dve.wait_ge(c.gathered[r].sem, i * (16 * G8) + (c.gathered[r].n + 16 * G8))
                if not (first(i) and r == 0):
                    dve.wait_ge(c.mm.sem, q * G8 + (c.mm.n + 4 * b + 4 - G8))
                dve.wait_ge(m.scaled.sem, q * 2 + (m.scaled.n + b + 1))
                w = s.pay4[:, r, js, 0:P].rearrange("p j (t u) -> p j t u", t=4)
                wev = s.wev[:, r % 2, js, :, :, :]
                g = rows_of(r)[:, js, :].rearrange("p j (t u) -> p j t u", t=4)
                scalar = g[:, :, 0:1, :].broadcast_to([P, 4, 3, MUL])
                if not (first(q) and b == 0):
                    dve.wait_ge(m.prod.sem, q * 2 + (m.prod.n + b))
                nc.vector.tensor_tensor(s.dot, wev[:, :, :, 1, :], g[:, :, 1:4, :], ALU.mult).then_inc(m.dotted.sem, 1)
                nc.vector.tensor_tensor(s.prod[:, js, 0, MUL:2 * MUL], w[:, :, 0, :], g[:, :, 0, :], ALU.mult)
                nc.vector.tensor_tensor(s.prod[:, js, 1:4, 0:MUL], wev[:, :, :, 0, :], scalar, ALU.mult)
                nc.vector.tensor_tensor(s.prod[:, js, 1:4, MUL:2 * MUL],
                                        w[:, :, 2:3, :].broadcast_to([P, 4, 3, MUL]), g[:, :, 1:4, :], ALU.mult)
                dve.wait_ge(m.dotted.sem, q * 2 + (m.dotted.n + b + 1))
                nc.vector.tensor_reduce(s.prod[:, js, 0, 0:MUL], s.dot.rearrange("p j a u -> p j u a"),
                                        AX.X, ALU.add).then_inc(m.prod.sem, 1)

            def reduce(i, r):
                q = RING * i + r
                bins = load_bins(c, mybir.EngineType.DVE, "dst", q)
                products(i, r, 1)
                if after(i, r, 1, RING):
                    hot(*after(i, r, 1, RING))
                for j in range(G8):
                    if j == 4 and after(i, r, 1, RING):
                        products(*after(i, r, 1, RING), 0)
                    add_chunk(c, dve, q, j, bins[j], AW, c.ps[:, j:j + 1, 0:AW])
            hot(0, 0)
            products(0, 0, 0)
            groups(dve, NG, reduce, ahead=1, per=RING)

        @block.tensor
        def _(pe):
            def product(i, r):
                q = RING * i + r
                pe.wait_ge(c.hot_ready.sem, q + (c.hot_ready.n + 1))
                for j in range(G8):
                    if j % 4 == 0:
                        pe.wait_ge(m.prod.sem, q * 2 + (m.prod.n + j // 4 + 1))
                    if not (first(i) and r == 0):
                        pe.wait_ge(c.added.sem, q * G8 + (c.added.n + j - G8 + 1))
                    pe.matmul(c.ps[:, j, 0:AW], c.hot[:, r % 2, j, :],
                              s.prod[:, j, :, :].rearrange("p g u -> p (g u)"),
                              start=True, stop=True).then_inc(c.mm.sem, 1)
            groups(pe, NG, product, per=RING)
    end_pass(c, RING)
    for p in m.pay:
        p.n += 16 * (NG // RING)
    m.kept.n += NG
    for x in (m.prod, m.scaled, m.dotted):
        x.n += 2 * NG


def copy_indices(c, act, k):
    def body(i, h):
        q = 2 * i + h
        if not first(i):
            act.wait_ge(c.mm.sem, q * G8 + (c.mm.n - G8))
        c.nc.scalar.activation(c.idx[:, h, :], c.meta[k][:, at(q, G8, 0, G8), 0], ACT.Copy).then_inc(c.idx_ready.sem, 1)
    return body


def gather_rows(c, pool, table, to):
    def body(i, h):
        c.hold(pool, c.idx_ready, i * 2 + (h + c.idx_ready.n + 1))
        for j in range(G8):
            pool.indirect_dma_start(to(h, j), None, table,
                                    bass.IndirectOffsetOnAxis(ap=c.idx[:, h, j:j + 1], axis=0)
                                    ).then_inc(c.gathered[h].sem, 16)
    return body


def aggregate(c, k, table, width, used):
    nc = c.nc
    with nc.Block() as block:

        @block.scalar
        def _(act):
            groups(act, NG, copy_indices(c, act, k))

        @block.gpsimd
        def _(pool):
            groups(pool, NG, gather_rows(c, pool, table, lambda h, j: c.rows[:, h, j, 0:width]))

        @block.vector
        def _(dve):
            def reduce(i, h):
                q = 2 * i + h
                if not first(i):
                    dve.wait_ge(c.mm.sem, q * G8 + (c.mm.n - G8))
                one_hot(c, h, c.meta[k][:, at(q, G8, 0, G8), 1:2])
                bins = load_bins(c, mybir.EngineType.DVE, k, q)
                for j in range(G8):
                    add_chunk(c, dve, q, j, bins[j], used, c.ps[:, j:j + 1, 0:used])
            groups(dve, NG, reduce)

        @block.tensor
        def _(pe):
            def product(i, h):
                q = 2 * i + h
                pe.wait_ge(c.gathered[h].sem, i * (16 * G8) + (c.gathered[h].n + 16 * G8))
                pe.wait_ge(c.hot_ready.sem, q + (c.hot_ready.n + 1))
                for j in range(G8):
                    if not (first(i) and h == 0):
                        pe.wait_ge(c.added.sem, q * G8 + (c.added.n + j - G8 + 1))
                    pe.matmul(c.ps[:, j, 0:used], c.hot[:, h, j, :], c.rows[:, h, j, 0:used],
                              start=True, stop=True).then_inc(c.mm.sem, 1)
            groups(pe, NG, product)
    end_pass(c)


def node_product(c, s, feed, parts, part_width, products, steps, take):
    nc = c.nc
    m = s.m

    def tiles_of(eng, body):
        body(0)
        with eng.Fori(1, NB // 2 - 1) as i:
            body(i)
        body(NB // 2 - 1)

    last_ = lambda i: isinstance(i, int) and i == NB // 2 - 1

    with nc.Block() as block:

        @block.scalar
        def _(act):
            def fill(k, slot, free):
                if free:
                    act.wait_ge(m.turned.sem, k + (m.turned.n - 1))
                feed(k, slot).then_inc(m.fed.sem, 1)

            def body(i):
                if first(i):
                    fill(0, 0, False)
                    fill(1, 1, False)
                for slot in range(2):
                    k = 2 * i + slot
                    act.wait_ge(m.turned.sem, k + (m.turned.n + 1))
                    if not first(i):
                        act.wait_ge(m.multiplied.sem, k + (m.multiplied.n - 1))
                    nc.scalar.activation(s.ut[0:part_width, slot, 0:parts * P], c.ps[0:part_width, slot, 0:parts * P],
                                         ACT.Copy).then_inc(m.back.sem, 1)
                    if not last_(i):
                        fill(k + 2, slot, True)
            tiles_of(act, body)

        @block.tensor
        def _(pe):
            def turn(k, slot, free):
                if free:
                    pe.wait_ge(m.back.sem, k + (m.back.n - 1))
                c.hold(pe, m.fed, k + (m.fed.n + 1))
                for a in range(parts):
                    last = pe.transpose(c.ps[0:part_width, slot, a * P:(a + 1) * P],
                                        s.u[:, slot, a * part_width:(a + 1) * part_width], c.ident[:, :])
                last.then_inc(m.turned.sem, 1)

            def body(i):
                if first(i):
                    turn(0, 0, False)
                for slot in range(2):
                    k = 2 * i + slot
                    if not (last_(i) and slot == 1):
                        turn(k + 1, 1 - slot, not (first(i) and slot == 0))
                    pe.wait_ge(m.back.sem, k + (m.back.n + 1))
                    if not first(i):
                        pe.wait_ge(m.taken.sem, k + (m.taken.n - 1))
                    for a, w, lo, hi, start, stop in products:
                        last = pe.matmul(c.ps[:, 4 + slot, lo:hi], s.ut[0:part_width, slot, a * P:(a + 1) * P], w,
                                         start=start, stop=stop)
                    last.then_inc(m.multiplied.sem, 1)
            tiles_of(pe, body)

        @block.vector
        def _(dve):
            st = Steps(dve, c.dve)

            def body(i):
                st.loop(i, 2 * steps)
                for slot in range(2):
                    k = 2 * i + slot
                    dve.wait_ge(m.multiplied.sem, k + (m.multiplied.n + 1))
                    take(st, k, 4 + slot).then_inc(m.taken.sem, 1)
                assert st.k == st.per, (st.k, st.per)
            tiles_of(dve, body)
            st.end(NB // 2)
    for x in (m.fed, m.turned, m.back, m.multiplied, m.taken):
        x.n += NB


def one(k):
    return slice(k, k + 1) if isinstance(k, int) else bass.ds(k, 1)


def stats(c, s, st, k, ap):
    c.hold(st.eng, st.c, st.reached())
    return c.nc.vector.bn_stats(s.st6[:, one(k), :].rearrange("p a b -> p (a b)"), ap)


def moments(c, s, dve, width):
    v, st = c.nc.vector, Steps(dve, c.dve)
    me, ve, mo, vo = (s.st6[:, :, i] for i in (1, 2, 4, 5))
    mean, var = c.mv[:, :, 0], c.mv[:, :, 1]
    st(v.tensor_tensor(mean, me, mo, ALU.add))
    st(v.tensor_tensor(mo, me, mo, ALU.subtract))
    st(v.tensor_tensor(var, ve, vo, ALU.add)).wait()
    st(v.tensor_scalar(mean, mean, 0.5, None, ALU.mult))
    st(v.tensor_tensor(mo, mo, mo, ALU.mult))
    st(v.tensor_scalar(var, var, 1.0 / width, None, ALU.mult)).wait()
    st(v.scalar_tensor_tensor(var, mo, 0.25, var, ALU.mult, ALU.add))


def seg(ap, g):
    return ap[:, g * SEGT:(g + 1) * SEGT]


def spread(col, width):
    return col.unsqueeze(2).broadcast_to([P, col.shape[1], width])


def over(row, n):
    return row.unsqueeze(1).broadcast_to([P, n, row.shape[1]])


def root(c, s, to, src, bias, width=None):
    nc = c.nc
    m = s.m
    with nc.Block() as block:

        @block.scalar
        def _(act):
            if width:
                act.wait_ge(m.moments.sem, m.moments.n + 1)
            nc.scalar.activation(to, src, ACT.Sqrt, bias=bias).then_inc(m.rooted.sem, 1)

        @block.vector
        def _(dve):
            if width:
                moments(c, s, dve, width)
                dve.wait_ge(c.dve.sem, c.dve.n)
                dve.sem_inc(m.moments.sem, 1)
            dve.wait_ge(m.rooted.sem, m.rooted.n + 1)
            Steps(dve, c.dve)(nc.vector.reciprocal(to, to))
    m.rooted.n += 1
    m.moments.n += bool(width)


def normalise(c, s, self_term=False, clear=False, table=None, out=None):
    nc = c.nc
    root(c, s, c.rstd[:, :], c.mv[:, :, 1], c.eps[:, 0:1], D)
    with nc.Block() as block:

        @block.vector
        def _(dve):
            st = Steps(dve, c.dve)
            for g in range(NSEG):
                x = seg(c.x, g)
                st(nc.vector.tensor_tensor(x, x, spread(seg(c.mv, g)[:, :, 0], D), ALU.subtract)).wait()
                last = nc.vector.tensor_tensor(x, x, spread(seg(c.rstd, g), D), ALU.mult)
                if self_term:
                    st(last).wait()
                    last = nc.vector.tensor_tensor(seg(c.acc, g)[:, :, 0:D], x, spread(seg(c.dinv, g), D), ALU.mult)
                last.then_inc(s.m.part.sem, 1)
            if clear:
                nc.vector.memset(c.acc[:, :, :], 0.0)

        @block.sync
        def _(sp):
            for g in range(NSEG):
                sp.wait_ge(s.m.part.sem, s.m.part.n + g + 1)
                src = seg(c.acc, g)[:, :, 0:D] if self_term else seg(c.x, g)
                if out is None:
                    sp.dma_start(tiles(table, NB, D)[:, g * SEGT:(g + 1) * SEGT, :], src).then_inc(c.store.sem, 16)
                elif g < NSEG - 1:
                    sp.dma_start(tiles(out[0:(NSEG - 1) * SEGT * P, :], 0, 0)[:, g * SEGT:(g + 1) * SEGT, :], src
                                 ).then_inc(c.store.sem, 16)
                else:
                    full = NT - 1 - g * SEGT
                    sp.dma_start(tiles(out[g * SEGT * P:(NT - 1) * P, :], 0, 0), src[:, 0:full, :]).then_inc(c.store.sem, 16)
                    sp.dma_start(out[(NT - 1) * P:N, :], c.x[0:LASTN, NT - 1, :]).then_inc(c.store.sem, 16)
            sp.wait_ge(c.store.sem, c.store.n + 16 * (NSEG + (out is not None)))
    s.m.part.n += NSEG
    c.store.n += 16 * (NSEG + (out is not None))


def write_table(c, src, table, width):
    nc = c.nc
    with nc.Block() as block:

        @block.sync
        def _(sp):
            for g in range(NSEG):
                sp.dma_start(tiles(table, NB, width)[:, g * SEGT:(g + 1) * SEGT, :], seg(src, g)).then_inc(c.store.sem, 16)
            sp.wait_ge(c.store.sem, c.store.n + 16 * NSEG)
    c.store.n += 16 * NSEG


def clear_acc(c, value=0.0):
    nc = c.nc
    with nc.Block() as block:

        @block.vector
        def _(dve):
            Steps(dve, c.dve)(nc.vector.memset(c.acc[:, :, :], value))


def conv_norm(c, s, l, table):
    nc = c.nc
    root(c, s, c.rstd[:, :], c.mv[:, :, 1], c.eps[:, 0:1], HID)
    m = s.m
    gain, shift = s.gain[l], s.shift[l]
    with nc.Block() as block:

        @block.vector
        def _(dve):
            st = Steps(dve, c.dve)

            def finish(g):
                a = seg(c.acc, g)[:, :, 0:HID]
                dve.wait_ge(m.powered.sem, m.powered.n + g + 1)
                st(nc.vector.scalar_tensor_tensor(a, a, 0.0, s.ex[:, g % 2, :, :], ALU.max, ALU.add)).wait()
                nc.vector.scalar_tensor_tensor(a, a, -1.0, spread(seg(c.dinv, g), HID), ALU.add,
                                               ALU.mult).then_inc(m.part.sem, 1)

            for g in range(NSEG):
                a = seg(c.acc, g)[:, :, 0:HID]
                st(nc.vector.tensor_tensor(a, a, spread(seg(c.mv, g)[:, :, 0], HID), ALU.subtract)).wait()
                nc.vector.tensor_tensor(a, a, spread(seg(c.rstd, g), HID), ALU.mult).then_inc(m.centred.sem, 1)
                if g:
                    dve.wait_ge(m.shifted.sem, m.shifted.n + g)
                    b = seg(c.acc, g - 1)[:, :, 0:HID]
                    nc.vector.tensor_scalar(s.ex[:, (g - 1) % 2, :, :], b, 0.0, None, ALU.min).then_inc(m.cut.sem, 1)
                if g >= 2:
                    finish(g - 2)
            dve.wait_ge(m.shifted.sem, m.shifted.n + NSEG)
            b = seg(c.acc, NSEG - 1)[:, :, 0:HID]
            nc.vector.tensor_scalar(s.ex[:, (NSEG - 1) % 2, :, :], b, 0.0, None, ALU.min).then_inc(m.cut.sem, 1)
            finish(NSEG - 2)
            finish(NSEG - 1)

        @block.gpsimd
        def _(pool):
            for g in range(NSEG):
                a = seg(c.acc, g)[:, :, 0:HID]
                pool.wait_ge(m.centred.sem, m.centred.n + g + 1)
                pool.tensor_tensor(a, a, over(gain[:, :], SEGT), ALU.mult).then_inc(c.pool.sem, 1)
                pool.wait_ge(c.pool.sem, c.pool.n + g + 1)
                pool.tensor_tensor(a, a, over(shift[:, :], SEGT), ALU.add).then_inc(m.shifted.sem, 1)

        @block.scalar
        def _(act):
            for g in range(NSEG):
                act.wait_ge(m.cut.sem, m.cut.n + g + 1)
                e = s.ex[:, g % 2, :, :]
                nc.scalar.activation(e, e, ACT.Exp).then_inc(m.powered.sem, 1)

        @block.sync
        def _(sp):
            if table is not None:
                for g in range(NSEG):
                    sp.wait_ge(m.part.sem, m.part.n + g + 1)
                    sp.dma_start(tiles(table, NB, HID)[:, g * SEGT:(g + 1) * SEGT, :],
                                 seg(c.acc, g)[:, :, 0:HID]).then_inc(c.store.sem, 16)
                sp.wait_ge(c.store.sem, c.store.n + 16 * NSEG)
    if table is not None:
        c.store.n += 16 * NSEG
    for x in (m.centred, m.shifted, m.cut, m.powered, m.part):
        x.n += NSEG
    c.pool.n += NSEG


def tile_stats(c, s, dve, st):
    with dve.Fori(0, NB) as k:
        st.loop(k, 1)
        st(c.nc.vector.bn_stats(s.st6[:, one(k), :].rearrange("p a b -> p (a b)"),
                                c.x[:, one(k), :].rearrange("p a b -> p (a b)")))
    st.end(NB)
    st.wait()


def add_gcn(c, s):
    nc = c.nc
    with nc.Block() as block:

        @block.vector
        def _(dve):
            st = Steps(dve, c.dve)
            for g in range(NSEG):
                a, x = seg(c.acc, g)[:, :, 0:D], seg(c.x, g)
                st(nc.vector.tensor_tensor(a, a, spread(seg(c.dinv, g), D), ALU.mult))
                st(nc.vector.tensor_tensor(x, x, over(s.b3[:, :], SEGT), ALU.add)).wait()
                st(nc.vector.tensor_tensor(x, x, a, ALU.add))
            st.wait()
            tile_stats(c, s, dve, st)


def add_gat(c, s):
    nc = c.nc
    with nc.Block() as block:

        @block.vector
        def _(dve):
            st = Steps(dve, c.dve)
            den = c.acc[:, :, D:D + HEADS]
            st(nc.vector.tensor_scalar(den, den, 1e-16, None, ALU.add)).wait()
            st(nc.vector.reciprocal(den, den)).wait()
            for g in range(NSEG):
                a, x, t = seg(c.acc, g)[:, :, 0:D], seg(c.x, g), s.ex[:, 0, :, 0:D]
                a4 = a.rearrange("p n (h c) -> p n h c", h=HEADS)
                r4 = seg(den, g).unsqueeze(3).broadcast_to([P, SEGT, HEADS, CH])
                st(nc.vector.tensor_tensor(a4, a4, r4, ALU.mult)).wait()
                st(nc.vector.tensor_tensor(a, a, over(s.bias[:, :], SEGT), ALU.add)).wait()
                st(nc.vector.scalar_tensor_tensor(t, a, 0.0, over(s.prelu[:, :], SEGT), ALU.min, ALU.mult)).wait()
                st(nc.vector.scalar_tensor_tensor(a, a, 0.0, t, ALU.max, ALU.add)).wait()
                st(nc.vector.tensor_tensor(x, x, a, ALU.add))
            st.wait()
            tile_stats(c, s, dve, st)


def scores_max(c, s, table):
    nc = c.nc
    m = s.m
    with nc.Block() as block:

        @block.scalar
        def _(act):
            copy = copy_indices(c, act, "dst")

            def body(i, h):
                if after(i, h):
                    copy(*after(i, h))
                q = 2 * i + h
                act.wait_ge(c.hot_ready.sem, q + (c.hot_ready.n + 1))
                act.wait_ge(c.gathered[h].sem, i * (16 * G8) + (c.gathered[h].n + 16 * G8))
                for j in range(G8):
                    if not (first(i) and h == 0):
                        act.wait_ge(c.mm.sem, q * G8 + (c.mm.n + j - G8 + 1))
                    for a in range(HEADS):
                        last = nc.scalar.activation(s.hot_v[:, j, a, :], c.hot[:, h, j, :], ACT.Identity,
                                                    bias=c.rows[:, h, j, a:a + 1])
                    last.then_inc(m.scaled.sem, 1)
            copy(0, 0)
            groups(act, NG, body, ahead=1)

        @block.gpsimd
        def _(pool):
            groups(pool, NG, gather_rows(c, pool, table, lambda h, j: c.rows[:, h, j, 0:HEADS]))

        @block.vector
        def _(dve):
            def reduce(i, h):
                q = 2 * i + h
                if not first(i):
                    dve.wait_ge(c.mm.sem, q * G8 + (c.mm.n - G8))
                for j in range(G8):
                    last = nc.vector.tensor_scalar(c.hot[:, h, j, :], c.iota[:, :],
                                                   c.meta["dst"][:, at(q, G8, j, 1), 1], NEG,
                                                   ALU.not_equal, ALU.mult)
                last.then_inc(c.hot_ready.sem, 1)
                bins = load_bins(c, mybir.EngineType.DVE, "dst", q)
                for j in range(G8 + 1):
                    if j < G8:
                        dve.wait_ge(c.mm.sem, q * G8 + (c.mm.n + j + 1))
                        nc.vector.tensor_reduce(s.mx8[:, j, :], c.ps[:, j, 0:HEADS * P].rearrange("p (a e) -> p a e", a=HEADS),
                                                AX.X, ALU.max).then_inc(m.reduced.sem, 1)
                    if j:
                        dve.wait_ge(m.reduced.sem, q * G8 + (m.reduced.n + j))
                        if not (first(i) and h == 0 and j == 1):
                            dve.wait_ge(c.added.sem, q * G8 + (c.added.n + j - 1))
                        to = s.mx[:, bass.ds(bins[j - 1], 1), :]
                        nc.vector.tensor_tensor(to, to, s.mx8[:, j - 1:j, :], ALU.max).then_inc(c.added.sem, 1)
            groups(dve, NG, reduce)

        @block.tensor
        def _(pe):
            def turn(i, h):
                q = 2 * i + h
                for j in range(G8):
                    pe.wait_ge(m.scaled.sem, q * G8 + (m.scaled.n + j + 1))
                    if not (first(i) and h == 0):
                        pe.wait_ge(m.reduced.sem, q * G8 + (m.reduced.n + j - G8 + 1))
                    for a in range(HEADS):
                        last = pe.transpose(c.ps[:, j, a * P:(a + 1) * P], s.hot_v[:, j, a, :], c.ident[:, :])
                    last.then_inc(c.mm.sem, 1)
            groups(pe, NG, turn)
    end_pass(c)
    m.scaled.n += NCH
    m.reduced.n += NCH


def node_max(c, s):
    nc = c.nc
    with nc.Block() as block:

        @block.vector
        def _(dve):
            st = Steps(dve, c.dve)
            st(nc.vector.tensor_tensor(s.mx[:, :, :], s.mx[:, :, :], s.nt[:, :, 0:2], ALU.add)).wait()
            st(nc.vector.scalar_tensor_tensor(s.nt[:, :, 2:4], s.mx[:, :, :], SLOPE, s.mx[:, :, :], ALU.mult, ALU.max))
            nc.vector.memset(c.acc[:, :, :], 0.0)


def attend(c, s, table):
    nc = c.nc
    m = s.m
    width = D + HEADS
    with nc.Block() as block:

        @block.scalar
        def _(act):
            copy = copy_indices(c, act, "dst")

            def turned(i, h):
                q = 2 * i + h
                for b in range(2):
                    act.wait_ge(m.turned.sem, q * 2 + (m.turned.n + b + 1))
                    nc.scalar.activation(s.hot_t[:, 4 * b:4 * b + 4, :].rearrange("p j n -> p (j n)"), c.ps[:, b, :],
                                         ACT.Copy).then_inc(m.back.sem, 1)

            def body(i, h):
                q = 2 * i + h
                if after(i, h):
                    copy(*after(i, h))
                act.wait_ge(m.scored.sem, q + (m.scored.n + 1))
                nc.scalar.activation(s.wt[:, :, D:width], s.z[:, :, :], ACT.Exp).then_inc(m.powered.sem, 1)
                if after(i, h):
                    turned(*after(i, h))
            copy(0, 0)
            turned(0, 0)
            groups(act, NG, body, ahead=1)

        @block.gpsimd
        def _(pool):
            groups(pool, NG, gather_rows(c, pool, table, lambda h, j: c.rows[:, h, j, 0:width]))

        @block.vector
        def _(dve):
            st = Steps(dve, c.dve)

            def hot(i, h):
                q = 2 * i + h
                if not first(i):
                    dve.wait_ge(c.mm.sem, q * G8 + (c.mm.n - G8))
                one_hot(c, h, c.meta["dst"][:, at(q, G8, 0, G8), 1:2])

            def reduce(i, h):
                q = 2 * i + h
                if h == 0:
                    st.loop(i, 6)
                bins = load_bins(c, mybir.EngineType.DVE, "dst", q)
                dve.wait_ge(c.gathered[h].sem, i * (16 * G8) + (c.gathered[h].n + 16 * G8))
                dve.wait_ge(m.looked.sem, q + (m.looked.n + 1))
                e8 = c.ps[:, 2, 0:4 * G8].rearrange("p (j k) -> p j k", j=G8)
                z = s.z[:, :, :]
                st(nc.vector.tensor_tensor(z, c.rows[:, h, :, D:width], e8[:, :, 0:2], ALU.add)).wait()
                st(nc.vector.scalar_tensor_tensor(z, z, SLOPE, z, ALU.mult, ALU.max)).wait()
                st(nc.vector.tensor_tensor(z, z, e8[:, :, 2:4], ALU.subtract)).wait()
                nc.vector.tensor_scalar(z, z, 0.0, None, ALU.min).then_inc(m.scored.sem, 1)
                if after(i, h):
                    hot(*after(i, h))
                dve.wait_ge(m.powered.sem, q + (m.powered.n + 1))
                nc.vector.tensor_tensor(
                    s.wt[:, :, 0:D].rearrange("p j (a u) -> p j a u", a=HEADS),
                    c.rows[:, h, :, 0:D].rearrange("p j (a u) -> p j a u", a=HEADS),
                    s.wt[:, :, D:width].unsqueeze(3).broadcast_to([P, G8, HEADS, CH]),
                    ALU.mult).then_inc(m.weighted.sem, 1)
                for j in range(G8):
                    bank = 3 + j % 5
                    add_chunk(c, dve, q, j, bins[j], width, c.ps[:, bank:bank + 1, 0:width])
            hot(0, 0)
            groups(dve, NG, reduce, ahead=1)
            st.end(NG // 2)

        @block.tensor
        def _(pe):
            def look_up(i, h):
                q = 2 * i + h
                bins = load_bins(c, mybir.EngineType.PE, "dst", q)
                pe.wait_ge(c.hot_ready.sem, q + (c.hot_ready.n + 1))
                for j in range(G8):
                    last = pe.transpose(c.ps[:, j // 4, (j % 4) * P:(j % 4 + 1) * P], c.hot[:, h, j, :], c.ident[:, :])
                    if j % 4 == 3:
                        last.then_inc(m.turned.sem, 1)
                for b in range(2):
                    pe.wait_ge(m.back.sem, q * 2 + (m.back.n + b + 1))
                    for j in range(4 * b, 4 * b + 4):
                        last = pe.matmul(c.ps[:, 2, 4 * j:4 * j + 4], s.hot_t[:, j, :],
                                         s.nt[:, bass.ds(bins[j], 1), :].rearrange("p a b -> p (a b)"),
                                         start=True, stop=True)
                last.then_inc(m.looked.sem, 1)

            def product(i, h):
                q = 2 * i + h
                pe.wait_ge(m.weighted.sem, q + (m.weighted.n + 1))
                for j in range(G8):
                    before = j - 5 if j >= 5 else j - 3 if j < 3 else j - G8
                    if not (first(i) and h == 0 and before < 0):
                        pe.wait_ge(c.added.sem, q * G8 + (c.added.n + before + 1))
                    pe.matmul(c.ps[:, 3 + j % 5, 0:width], c.hot[:, h, j, :], s.wt[:, j, :],
                              start=True, stop=True).then_inc(c.mm.sem, 1)
                if after(i, h):
                    look_up(*after(i, h))
            look_up(0, 0)
            groups(pe, NG, product, ahead=1)
    end_pass(c)
    m.turned.n += 2 * NG
    m.back.n += 2 * NG
    for x in (m.looked, m.scored, m.powered, m.weighted):
        x.n += NG


def prepare_weights(c, s):
    nc = c.nc
    v = nc.vector
    with nc.Block() as block:

        @block.scalar
        def _(act):
            nc.scalar.activation(s.sig[:, :], s.sig[:, :], ACT.Exp, scale=-1.0).then_inc(s.m.rooted.sem, 1)

        @block.vector
        def _(dve):
            st = Steps(dve, c.dve)
            st(v.tensor_scalar(s.lin1[:, :], s.lin1[:, :], MUL ** -0.5, None, ALU.mult))
            st(v.tensor_scalar(s.fc1[:, :], s.fc1[:, :], 8 ** -0.5, None, ALU.mult))
            st(v.tensor_scalar(s.fc2[:, :], s.fc2[:, :], SILU_NORM * 64 ** -0.5, None, ALU.mult))
            scale = 0.25 * (2 * MUL) ** -0.5
            st(v.tensor_scalar(s.lin2s[0:MUL, :], s.lin2s[0:MUL, :], scale * 3 ** -0.5, None, ALU.mult))
            st(v.tensor_scalar(s.lin2s[MUL:2 * MUL, :], s.lin2s[MUL:2 * MUL, :], scale, None, ALU.mult))
            st(v.tensor_scalar(s.lin2v[:, :], s.lin2v[:, :], scale, None, ALU.mult))
            st(v.tensor_tensor(s.attw[:, 0, :], s.wg[:, 0:D], s.att[:, 0, :], ALU.mult))
            st(v.tensor_tensor(s.attw[:, 1, :], s.wdst[:, :], s.att[:, 1, :], ALU.mult)).wait()
            st(v.tensor_reduce(s.wg[:, D:D + 4], s.attw[:, :, :].rearrange("p a (h u) -> p (a h) u", h=HEADS),
                               AX.X, ALU.add))
            dve.wait_ge(s.m.rooted.sem, s.m.rooted.n + 1)
            st(v.tensor_scalar(s.sig[:, :], s.sig[:, :], 1.0, None, ALU.add)).wait()
            st(v.reciprocal(s.sig[:, :], s.sig[:, :])).wait()
            for l in range(3):
                w, a = s.w[l][:, :], s.sig[:, l:l + 1]
                st(v.tensor_scalar(w, w, a, None, ALU.mult))
                st(v.tensor_scalar(s.b[l][:, :], s.b[l][:, :], a, None, ALU.mult))
    s.m.rooted.n += 1


def degrees(c, s):
    root(c, s, c.dinv[:, :], c.acc[:, :, 2 * MUL], c.ones[:, 0:1])


class Scratch:
    pass


def gnn(nc, A, out, upto=None):
    with ExitStack() as ctx:
        c = Chip(nc, ctx)
        s = Scratch()
        sb = c.sb
        flat = c.acc[:, :, :].rearrange("p n w -> p (n w)")
        at_ = [0]

        def lay(width, dt=F32):
            a = flat[:, at_[0]:at_[0] + width]
            at_[0] += width
            return a if dt is F32 else a.bitcast(dt)
        s.key = {k: lay(TC, I32) for k in ("dst", "src")}
        s.lof = {k: lay(TC) for k in ("dst", "src")}
        s.pos = {k: lay(TC) for k in ("dst", "src")}
        s.binf, s.mask, s.run, s.one_row = (lay(TC) for _ in range(4))
        s.ki, s.kl, s.kh = (lay(TC, I32) for _ in range(3))
        s.fsrc = lay(2 * TC).rearrange("p (t w) -> p t w", w=2)
        s.fld = sb("fld", [P, TC, 6])
        s.attr = s.fld[:, :, 0:4]
        s.pay4 = s.fld[:, :, :].rearrange("p t w -> p (t w)")[:, 0:4 * G8 * PW].rearrange(
            "p (r j w) -> p r j w", r=4, j=G8)
        s.cnt, s.nch, s.inc, s.exc = (sb(n, [P, NB]) for n in ("bin_count", "bin_chunks", "bin_end", "bin_start"))
        s.ci, s.cj = (sb(n, [P, NB], I32) for n in ("bin_count_i", "bin_chunks_i"))
        s.base = {k: sb(f"base_{k}", [P, NB]) for k in ("dst", "src")}
        s.end_t = sb("end_t", [64, 1])
        s.past = c.hot[0:64, 1, :, :].rearrange("p j n -> p (j n)")[:, 0:NCH]
        s.small = sb("small", [P, 2, G8, 2])
        s.hot_v = sb("hot_v", [P, G8, 3, P])
        s.prod = sb("prod", [P, G8, 4, 2 * MUL + 1])
        s.ex = s.hot_v[:, :, :, :].rearrange("p j a n -> p (j a n)")[:, 0:2 * SEGT * HID].rearrange(
            "p (g n w) -> p g n w", g=2, n=SEGT)
        s.hot_t = s.prod[:, :, :, :].rearrange("p j a n -> p (j a n)")[:, 0:G8 * P].rearrange("p (j n) -> p j n", j=G8)
        s.ea8 = s.hot_v[0:8, :, :, :].rearrange("p j a n -> p (j a n)")[:, 0:2 * G8 * P].rearrange(
            "p (h n) -> p h n", h=2)
        s.hid = s.prod[0:64, :, :, :].rearrange("p j a n -> p (j a n)")[:, 0:1024].rearrange("p (b n) -> p b n", b=2)
        s.wt = c.pay[:, 0, :, 0:D + HEADS]
        s.z = c.pay[:, 1, :, 0:HEADS]
        s.u = s.hid_u = sb("u", [P, 2, HID])
        s.dot = s.u[:, :, :].rearrange("p a n -> p (a n)")[:, 0:4 * 3 * MUL].rearrange(
            "p (j a u) -> p j a u", j=4, a=3)
        s.wev = s.hot_v[:, :, :, :].rearrange("p j a n -> p (j a n)").rearrange(
            "p (h j a t u) -> p h j a t u", h=2, j=G8, a=3, t=2)
        s.ut = sb("ut", [P, 2, 4 * P])
        s.st6 = sb("st6", [P, NB, 6])
        s.mx = sb("mx", [P, NB, HEADS])
        s.mx8 = sb("mx8", [P, G8, HEADS])
        s.nt = sb("nt", [P, NB, 4])
        s.rcnt = sb("rcnt", [P, NB])
        s.has = sb("has", [P, NB])
        s.lin1 = sb("lin1", [P, P])
        s.fc1 = sb("fc1", [8, 64])
        s.fc2 = sb("fc2", [64, P])
        s.lin2s = sb("lin2s", [2 * MUL, MUL])
        s.lin2v = sb("lin2v", [2 * MUL, MUL])
        s.w = [sb("w0", [P, HID]), sb("w1", [P, 2 * HID]), sb("w2", [P, 2 * HID])]
        s.w3 = sb("w3", [P, 2 * D])
        s.b = [sb(f"b{l}", [P, HID]) for l in range(3)]
        s.gain = [sb(f"gain{l}", [P, HID]) for l in range(3)]
        s.shift = [sb(f"shift{l}", [P, HID]) for l in range(3)]
        s.b3 = sb("b3", [P, D])
        s.sig = sb("sig", [P, 3])
        s.wself, s.wneigh = sb("wself", [P, D]), sb("wneigh", [P, D])
        s.bself, s.bneigh = sb("bself", [P, D]), sb("bneigh", [P, D])
        s.wg, s.wdst = sb("wg", [P, D + 4]), sb("wdst", [P, D])
        s.att, s.attw = sb("att", [P, 2, D]), sb("attw", [P, 2, D])
        s.bias, s.prelu = sb("bias", [P, D]), sb("prelu", [P, D])
        two = lambda ap: ap.rearrange("(a p) n -> p a n", p=P)
        each = lambda ap: ap.partition_broadcast(P)
        halves = lambda t: t[:, :].rearrange("p (a n) -> p a n", a=2)
        s.weights = [(s.lin1[0:MUL, 0:MUL], A["L0_gnn_w_lin1_s"]),
                     (s.fc1[:, :], A["L0_gnn_fc_w1"]), (s.fc2[:, :], A["L0_gnn_fc_w2"]),
                     (s.lin2s[0:MUL, :], A["L0_gnn_w_lin2_s"][MUL:2 * MUL, :]),
                     (s.lin2s[MUL:2 * MUL, :], A["L0_gnn_w_lin2_s"][0:MUL, :]),
                     (s.lin2v[:, :], A["L0_gnn_w_lin2_v"]),
                     (s.w[0][:, :], A["L1_gnn_W0"]), (halves(s.w[1]), two(A["L1_gnn_W1"])),
                     (halves(s.w[2]), two(A["L1_gnn_W2"])), (halves(s.w3), two(A["L1_gnn_W3"])),
                     (s.b3[:, :], each(A["L1_gnn_b3"])),
                     (s.wself[:, :], A["WsT"]), (s.wneigh[:, :], A["WnT"]),
                     (s.bself[:, :], each(A["L2_gnn_b_self"])), (s.bneigh[:, :], each(A["L2_gnn_b_neigh"])),
                     (s.wg[:, 0:D], A["L3_gnn_W_src"]), (s.wdst[:, :], A["L3_gnn_W_dst"]),
                     (s.att[:, 0, :], each(A["L3_gnn_att_src"].rearrange("h u -> (h u)"))),
                     (s.att[:, 1, :], each(A["L3_gnn_att_dst"].rearrange("h u -> (h u)"))),
                     (s.bias[:, :], each(A["L3_gnn_bias"])), (s.prelu[:, :], each(A["L3_gnn_prelu_w"]))]
        for i in range(3):
            s.weights += [(s.lin1[MUL + i:P:3, MUL * (i + 1):MUL * (i + 2)], A["L0_gnn_w_lin1_v"]),
                          (s.b[i][:, :], each(A[f"L1_gnn_b{i}"])), (s.gain[i][:, :], each(A[f"L1_gnn_g{i}"])),
                          (s.shift[i][:, :], each(A[f"L1_gnn_beta{i}"])), (s.sig[:, i:i + 1], each(A[f"L1_gnn_a{i}"]))]
        dram = lambda name, shape: nc.dram_tensor(name, shape, F32, kind="Internal").ap()
        s.dst_rows = dram("dst_rows", (NCH * P, PW))
        s.src_rows = dram("src_rows", (NCH * P, 2))
        t0, t1 = dram("table_lin1", (NB * P, D)), dram("table_gcn0", (NB * P, D))
        t2, t3 = dram("table_gcn1", (NB * P, HID)), dram("table_gcn2", (NB * P, HID))
        t4, t5 = dram("table_gcn3", (NB * P, D)), dram("table_mean", (NB * P, D))
        t6, t7 = dram("table_gat", (NB * P, D + HEADS)), dram("table_score", (NB * P, HEADS))
        s.prefilled = c.sem("rows_prefilled")
        s.counted, s.summed, s.ended = c.sem("bins_counted"), c.sem("bins_summed"), c.sem("bins_ended")
        s.turned, s.passed, s.binned = c.sem("ends_turned"), c.sem("ends_passed"), c.sem("chunks_binned")
        m = s.m = Scratch()
        m.h_mm = c.sem("mlp_hidden_multiplied")
        m.silu = c.sem("mlp_hidden_ready")
        m.w_mm = c.sem("mlp_weights_multiplied")
        m.copied = c.sem("payload_ready")
        m.dotted = c.sem("vectors_multiplied")
        m.small = c.sem("small_rows_ready")
        m.kept = c.sem("small_fields_kept")
        m.prod = c.sem("tensor_products_ready")
        m.scaled = c.sem("scaled_one_hots_ready")
        m.fed = c.sem("tile_fed")
        m.turned = c.sem("tile_turned")
        m.back = c.sem("turned_tile_back")
        m.multiplied = c.sem("tile_multiplied")
        m.taken = c.sem("tile_taken")
        m.rooted = c.sem("root_taken")
        m.moments = c.sem("moments_ready")
        m.part = c.sem("segment_ready")
        m.centred = c.sem("segment_centred")
        m.shifted = c.sem("segment_shifted")
        m.cut = c.sem("segment_cut")
        m.powered = c.sem("exponential_taken")
        m.reduced = c.sem("scores_reduced")
        m.looked = c.sem("node_scores_looked_up")
        m.scored = c.sem("edge_scores_ready")
        m.weighted = c.sem("rows_weighted")
        m.ea = [c.sem(f"edge_scalars_loaded_{h}") for h in range(2)]
        m.sc = [c.sem(f"rows_scattered_{h}") for h in range(2)]
        m.ss = [c.sem(f"small_rows_scattered_{h}") for h in range(2)]
        m.pay = [c.sem(f"payload_loaded_{r}") for r in range(4)]
        run(c, A, s, out, (t0, t1, t2, t3, t4, t5, t6, t7), upto)


def run(c, A, s, out, tables, upto):
    nc = c.nc
    t0, t1, t2, t3, t4, t5, t6, t7 = tables
    ps, acc, x = c.ps, c.acc, c.x
    v = nc.vector

    def flat(ap):
        return ap.rearrange("p a b -> p (a b)")

    def dump():
        with nc.Block() as block:
            @block.sync
            def _(sp):
                sp.dma_start(tiles(out[0:(NT - 1) * P, :], 0, 0), x[:, 0:NT - 1, :]).then_inc(c.store.sem, 16)
                sp.dma_start(out[(NT - 1) * P:N, :], x[0:LASTN, NT - 1, :]).then_inc(c.store.sem, 16)
                sp.wait_ge(c.store.sem, c.store.n + 32)

    setup(c, A, s)
    prepare_weights(c, s)
    sort_key(c, s, "dst")
    sort_key(c, s, "src")
    fields(c, s)
    scatter_dst(c, A, s)
    scatter_src(c, s)

    def feed_x(k, slot):
        return nc.scalar.activation(s.u[:, slot, 0:D], flat(x[:, one(k), :]), ACT.Copy)

    def take_rows(st, k, bank):
        return v.tensor_copy(flat(acc[:, one(k), 0:D]), ps[:, bank, 0:D])
    node_product(c, s, feed_x, 1, P, [(0, s.lin1[:, :], 0, D, True, True)], 0, take_rows)
    write_table(c, acc[:, :, 0:D], t0, D)
    with nc.Block() as block:
        @block.vector
        def _(dve):
            v.memset(acc[:, :, :], 0.0)
            Steps(dve, c.dve)(v.memset(s.prod[:, :, :, :], 1.0))
    messages(c, s, t0)
    degrees(c, s)

    def feed_msg(k, slot):
        return nc.scalar.activation(s.u[:, slot, :].rearrange("p (g w) -> p g w", g=4),
                                    flat(acc[:, one(k), :]).rearrange("p (g w) -> p g w", g=4)[:, :, 0:2 * MUL], ACT.Copy)

    def take_msg(st, k, bank):
        xs = flat(x[:, one(k), 0:MUL])
        xv = flat(x[:, one(k), MUL:D]).rearrange("p (u i) -> p i u", i=3)
        st(v.tensor_tensor(xs, xs, ps[:, bank, 0:MUL], ALU.add))
        st(v.tensor_tensor(xv, xv, ps[:, bank, MUL:D].rearrange("p (i u) -> p i u", i=3), ALU.add))
        return stats(c, s, st, k, flat(x[:, one(k), :]))
    node_product(c, s, feed_msg, 4, 2 * MUL,
                 [(g, (s.lin2v if g else s.lin2s)[:, :], MUL * g, MUL * g + MUL, True, True) for g in range(4)],
                 2, take_msg)
    normalise(c, s, self_term=True, table=t1)
    if upto == 0:
        return dump()

    def feed_scaled(width):
        def feed(k, slot):
            return nc.scalar.activation(s.u[:, slot, 0:width], flat(acc[:, one(k), 0:width]), ACT.Copy,
                                        scale=c.dinv[:, one(k)])
        return feed

    def take_conv(l):
        def take(st, k, bank):
            y = flat(acc[:, one(k), 0:HID])
            st(v.tensor_tensor(y, ps[:, bank, 0:HID], s.b[l][:, :], ALU.add))
            return stats(c, s, st, k, y)
        return take
    aggregate(c, "dst", t1, D, D)
    node_product(c, s, feed_scaled(D), 1, P, [(0, s.w[0][:, :], 0, HID, True, True)], 1, take_conv(0))
    conv_norm(c, s, 0, t2)
    for l, tin, tout in ((1, t2, t3), (2, t3, None)):
        aggregate(c, "dst", tin, HID, HID)
        node_product(c, s, feed_scaled(HID), 2, P,
                     [(a, s.w[l][:, a * HID:(a + 1) * HID], 0, HID, a == 0, a == 1) for a in range(2)], 1, take_conv(l))
        conv_norm(c, s, l, tout)

    def feed_acc(k, slot):
        return nc.scalar.activation(s.u[:, slot, :], flat(acc[:, one(k), 0:HID]), ACT.Copy)
    node_product(c, s, feed_acc, 2, P, [(a, s.w3[:, a * D:(a + 1) * D], 0, D, a == 0, a == 1) for a in range(2)],
                 0, take_rows)
    write_table(c, acc[:, :, 0:D], t4, D)
    aggregate(c, "dst", t4, D, D)
    add_gcn(c, s)
    normalise(c, s, table=t5, clear=True)
    if upto == 1:
        return dump()

    with nc.Block() as block:
        @block.vector
        def _(dve):
            Steps(dve, c.dve)(v.memset(c.rows[:, :, :, D:D + 1], 1.0))
    aggregate(c, "src", t5, D, D + 1)
    with nc.Block() as block:
        @block.vector
        def _(dve):
            st = Steps(dve, c.dve)
            st(v.tensor_scalar(s.has[:, :], acc[:, :, D], 0.0, None, ALU.is_gt))
            st(v.tensor_scalar(s.rcnt[:, :], acc[:, :, D], 1.0, None, ALU.max)).wait()
            st(v.reciprocal(s.rcnt[:, :], s.rcnt[:, :]))

    def feed_mean(k, slot):
        nc.scalar.activation(s.u[:, slot, 0:D], flat(acc[:, one(k), 0:D]), ACT.Copy, scale=s.rcnt[:, one(k)])
        return nc.scalar.activation(s.u[:, slot, D:2 * D], flat(x[:, one(k), :]), ACT.Copy)

    def take_mean(st, k, bank):
        t, y = s.ex[:, 0, 0, 0:D], flat(x[:, one(k), :])
        st(v.scalar_tensor_tensor(t, s.bneigh[:, :], s.has[:, one(k)], ps[:, bank, 0:D], ALU.mult, ALU.add)).wait()
        st(v.tensor_tensor(t, t, s.bself[:, :], ALU.add)).wait()
        st(v.scalar_tensor_tensor(y, t, 0.0, y, ALU.max, ALU.add))
        return stats(c, s, st, k, y)
    node_product(c, s, feed_mean, 2, P, [(0, s.wneigh[:, :], 0, D, True, False), (1, s.wself[:, :], 0, D, False, True)],
                 3, take_mean)
    normalise(c, s, table=t5)
    if upto == 2:
        return dump()

    def take_gat(st, k, bank):
        st(v.tensor_copy(flat(acc[:, one(k), 0:D + HEADS]), ps[:, bank, 0:D + HEADS]))
        return v.tensor_copy(flat(s.nt[:, one(k), 0:HEADS]), ps[:, bank, D + HEADS:D + 2 * HEADS])
    node_product(c, s, feed_x, 1, P, [(0, s.wg[:, :], 0, D + 4, True, True)], 1, take_gat)
    write_table(c, acc[:, :, 0:D + HEADS], t6, D + HEADS)
    write_table(c, acc[:, :, D:D + HEADS], t7, HEADS)
    with nc.Block() as block:
        @block.vector
        def _(dve):
            Steps(dve, c.dve)(v.memset(s.mx[:, :, :], NEG))
    scores_max(c, s, t7)
    node_max(c, s)
    attend(c, s, t6)
    add_gat(c, s)
    normalise(c, s, out=out)


_PLAIN = ["x", "L0_gnn_w_lin1_s", "L0_gnn_w_lin1_v", "L0_gnn_fc_w1", "L0_gnn_fc_w2", "L0_gnn_w_lin2_s",
          "L0_gnn_w_lin2_v", "L1_gnn_W0", "L1_gnn_b0", "L1_gnn_W1", "L1_gnn_b1", "L1_gnn_W2", "L1_gnn_b2",
          "L1_gnn_W3", "L1_gnn_b3", "L1_gnn_a0", "L1_gnn_a1", "L1_gnn_a2", "L1_gnn_g0", "L1_gnn_beta0",
          "L1_gnn_g1", "L1_gnn_beta1", "L1_gnn_g2", "L1_gnn_beta2", "L2_gnn_b_self", "L2_gnn_b_neigh",
          "L3_gnn_W_src", "L3_gnn_W_dst", "L3_gnn_att_src", "L3_gnn_att_dst", "L3_gnn_bias", "L3_gnn_prelu_w"]
UPTO = None


def kernel(**inputs):
    import concourse.bacc as _bacc
    from concourse.bass_utils import run_bass_kernel_spmd as _run

    whole = (TC - 1) * P
    arrays = {n: np.ascontiguousarray(inputs[n]) for n in _PLAIN}
    for k in ("dst", "src"):
        e = np.ascontiguousarray(inputs[k])
        arrays[k + "_main"] = np.ascontiguousarray(e[:whole].reshape(TC - 1, P).T)
        arrays[k + "_tail"] = np.ascontiguousarray(e[whole:].reshape(TAIL, 1))
    a = np.ascontiguousarray(inputs["edge_attr_4"])
    arrays["ea4_main"] = np.ascontiguousarray(a[:whole].reshape(TC - 1, P, 4).transpose(1, 0, 2))
    arrays["ea4_tail"] = np.ascontiguousarray(a[whole:])
    arrays["ea8"] = np.ascontiguousarray(np.ascontiguousarray(inputs["edge_attr_8"]).T)
    arrays["WsT"] = np.ascontiguousarray(np.ascontiguousarray(inputs["L2_gnn_W_self"]).T)
    arrays["WnT"] = np.ascontiguousarray(np.ascontiguousarray(inputs["L2_gnn_W_neigh"]).T)
    nc = _bacc.Bacc("TRN2", target_bir_lowering=False, num_devices=1)
    aps = {n: nc.dram_tensor("in_" + n, a.shape, mybir.dt.from_np(a.dtype), kind="ExternalInput").ap()
           for n, a in arrays.items()}
    out = nc.dram_tensor("out_x", (N, D), F32, kind="ExternalOutput").ap()
    gnn(nc, aps, out, UPTO)
    r = _run(nc, [{"in_" + n: a for n, a in arrays.items()}], core_ids=[0])
    return r.results[0]["out_x"]
```

```python
import numpy as np
import concourse.bass as bass
from concourse import mybir
from contextlib import ExitStack

F32 = mybir.dt.float32
I32 = mybir.dt.int32
U32 = mybir.dt.uint32
ALU = mybir.AluOpType
ACT = mybir.ActivationFunctionType
AX = mybir.AxisListType

P = 128
N = 6250
E = 100000
D = 128
HID = 256
MUL = 32
NT = -(-N // P)
NB = NT + 1
LASTN = N - (NT - 1) * P
TC = -(-E // P)
TAIL = E - (TC - 1) * P
PADKEY = NT * P
G8 = 8
NG = 104
RING = 4
NCH = NG * G8
assert NCH >= (TC * P + NB * (P - 1)) // P
SCG = TC // G8
REST = TC - SCG * G8
PW = 136
EV, SRC, LO = 128, 131, 132
AW = 260
GW = 260
EPS = 1e-5
SILU_NORM = 1.6791767923989418
NEG = -1.0e38
SEGT = 5
NSEG = NB // SEGT
HEADS, CH = 2, 64
SLOPE = 0.2


class Count:

    def __init__(self, sem):
        self.sem, self.n = sem, 0


class Steps:

    def __init__(self, eng, count):
        self.eng, self.c, self.turn, self.per, self.k = eng, count, None, 0, 0

    def loop(self, turn, per):
        self.turn, self.per, self.k = turn, per, 0

    def end(self, turns):
        assert self.k == self.per, (self.k, self.per)
        self.c.n += turns * self.per
        self.turn = None

    def __call__(self, ins):
        ins.then_inc(self.c.sem, 1)
        if self.turn is None:
            self.c.n += 1
        else:
            self.k += 1
        return self

    def reached(self):
        return self.c.n if self.turn is None else self.turn * self.per + (self.c.n + self.k)

    def wait(self, but=0):
        self.eng.wait_ge(self.c.sem, self.reached() - but)


class Chip:

    def __init__(self, nc, ctx):
        self.nc, self.ctx = nc, ctx
        sb = self.sb
        self.ps = ctx.enter_context(nc.psum_tensor("ps", [P, 8, 512], F32))
        self.ident = sb("ident", [P, P])
        self.ones = sb("ones", [P, P])
        self.upper = sb("upper", [P, P])
        self.iota = sb("iota", [P, P])
        self.iota_b = sb("iota_b", [P, NB])
        self.eps = sb("eps", [P, 1])
        self.x = sb("x", [P, NB, D])
        self.acc = sb("acc", [P, NB, AW])
        self.mv = sb("mv", [P, NB, 2])
        self.rstd = sb("rstd", [P, NB])
        self.dinv = sb("dinv", [P, NB])
        self.meta = {k: sb(f"meta_{k}", [P, NCH, 2]) for k in ("dst", "src")}
        self.bin_of = {k: sb(f"bin_of_{k}", [1, NCH], I32) for k in ("dst", "src")}
        self.idx = sb("idx", [P, 4, G8], I32)
        self.rows = sb("rows", [P, 2, G8, GW])
        self.hot = sb("hot", [P, 2, G8, P])
        self.pay = sb("pay", [P, 2, G8, PW])
        self.iota_c = self.hot[0:64, 0, :, :].rearrange("p j n -> p (j n)")[:, 0:NCH]
        sem = self.sem
        self.ready = sem("constants_ready")
        self.held = sem("held")
        self.dve = sem("dve_step")
        self.pool = sem("pool_step")
        self.act = sem("act_step")
        self.load = sem("load_done")
        self.store = sem("store_done")
        self.idx_ready = sem("indices_ready")
        self.gathered = [sem(f"gathered_{h}") for h in range(4)]
        self.scattered = [sem(f"scattered_{h}") for h in range(2)]
        self.hot_ready = sem("one_hot_ready")
        self.mm = sem("chunk_multiplied")
        self.added = sem("chunk_added")

    def sb(self, name, shape, dt=F32):
        return self.ctx.enter_context(self.nc.sbuf_tensor(name, shape, dt))

    def sem(self, name):
        return Count(self.ctx.enter_context(self.nc.semaphore(name)))

    def hold(self, eng, count, value):
        eng.wait_ge(count.sem, value)
        eng.sem_inc(self.held.sem, 1)


def tiles(ap, n, width):
    return ap.rearrange("(n p) f -> p n f", p=P)


def setup(c, A, s):
    nc = c.nc
    with nc.Block() as block:

        @block.gpsimd
        def _(pool):
            st = Steps(pool, c.pool)
            st(pool.memset(c.ident[:, :], 0.0))
            st(pool.memset(c.ones[:, :], 1.0))
            st(pool.memset(c.upper[:, :], 0.0))
            st.wait()
            pool.affine_select(out=c.ident[:, :], in_=c.ident[:, :], compare_op=ALU.not_equal, fill=1.0,
                               base=0, pattern=[[-1, P]], channel_multiplier=1)
            pool.affine_select(out=c.upper[:, :], in_=c.upper[:, :], compare_op=ALU.is_ge, fill=1.0,
                               base=0, pattern=[[-1, P]], channel_multiplier=1)
            pool.iota(c.iota[:, :], pattern=[[1, P]], base=0, channel_multiplier=0,
                      allow_small_or_imprecise_dtypes=True)
            pool.iota(c.iota_b[:, :], pattern=[[1, NB]], base=0, channel_multiplier=0,
                      allow_small_or_imprecise_dtypes=True)
            pool.iota(c.iota_c[:, :], pattern=[[1, NCH]], base=0, channel_multiplier=0,
                      allow_small_or_imprecise_dtypes=True)
            pool.memset(c.eps[:, :], EPS).then_inc(c.ready.sem, 1)

        @block.vector
        def _(dve):
            st = Steps(dve, c.dve)
            st(dve.memset(s.key["dst"][:, :], PADKEY))
            st(dve.memset(s.key["src"][:, :], PADKEY))
            st(dve.memset(s.attr[:, :, :], 0.0))
            st(dve.memset(c.x[:, NT - 1:NB, :], 0.0))
            st(dve.memset(s.lin1[:, :], 0.0))
            st(dve.memset(s.one_row[:, :], 1.0))
            st(dve.memset(s.pos["dst"][:, :], 0.0))
            st(dve.memset(s.pos["src"][:, :], 0.0))
            st(dve.memset(c.pay[:, :, :, :], 0.0))
            for k in ("dst", "src"):
                st(dve.memset(c.meta[k][:, :, 0], 0.0))
                st(dve.memset(c.meta[k][:, :, 1], -1.0))
            st(dve.memset(c.rows[:, :, :, :], 1.0))
            st.wait()
            st(dve.memset(c.pay[:, :, :, LO], -1.0))

        @block.sync
        def _(sp):
            sp.wait_ge(c.dve.sem, 2)
            for k in ("dst", "src"):
                sp.dma_start(s.key[k][:, 0:TC - 1], A[k + "_main"]).then_inc(s.keys_loaded.sem, 16)
                sp.dma_start(s.key[k][0:TAIL, TC - 1:TC], A[k + "_tail"]).then_inc(s.keys_loaded.sem, 16)
            sp.wait_ge(s.keys_loaded.sem, 64)
    c.ready.n = 1
    c.pool.n = 3


def sort_dve(c, s, dve, k, banks):
    key, binf, lof, pos, base = s.key[k], s.binf, s.lof[k], s.pos[k], s.base[k]
    masks, runs = (s.mask, s.mask2), (s.run, s.run2)
    st = Steps(dve, c.dve)
    st(dve.tensor_scalar(s.ki[:, :], key[:, :], 7, None, ALU.arith_shift_right))
    st(dve.tensor_scalar(s.kl[:, :], key[:, :], P - 1, None, ALU.bitwise_and)).wait()
    st(dve.tensor_copy(binf[:, :], s.ki[:, :]))
    st(dve.tensor_copy(lof, s.kl[:, :])).wait()
    with dve.Fori(0, NB // 2) as b:
        st.loop(b, 4)
        for i in range(2):
            st.wait(but=1)
            st(dve.tensor_scalar(masks[i], binf[:, :], c.iota_b[:, bass.ds(b * 2 + i, 1)], None, ALU.is_equal))
        for i in range(2):
            st.wait(but=1)
            st(dve.tensor_reduce(s.cnt[:, bass.ds(b * 2 + i, 1)], masks[i], AX.X, ALU.add))
    st.end(NB // 2)
    st.wait()
    dve.sem_inc(s.counted.sem, 1)
    dve.wait_ge(s.summed.sem, s.summed.n + 1)
    st(dve.tensor_scalar(s.ci[:, :], c.ps[:, banks[0], 0:NB], float(P - 1), None, ALU.add)).wait()
    st(dve.tensor_scalar(s.cj[:, :], s.ci[:, :], 7, None, ALU.arith_shift_right)).wait()
    st(dve.tensor_copy(s.nch[:, :], s.cj[:, :])).wait()
    st(dve.tensor_tensor_scan(s.inc[:, :], c.ones[:, 0:NB], s.nch[:, :], 0.0, ALU.mult, ALU.add)).wait()
    st(dve.tensor_tensor(s.exc[:, :], s.inc[:, :], s.nch[:, :], ALU.subtract)).wait()
    dve.sem_inc(s.ended.sem, 1)
    st(dve.tensor_scalar(s.exc[:, :], s.exc[:, :], float(P), -1.0, ALU.mult, ALU.add)).wait()
    st(dve.tensor_tensor(base[:, :], s.exc[:, :], c.ps[:, banks[1], 0:NB], ALU.add)).wait()
    dve.wait_ge(s.turned.sem, s.turned.n + 1)
    st(dve.tensor_copy(s.end_t[0:NB, :], c.ps[0:NB, banks[2], 0:1])).wait()
    st(dve.tensor_scalar(s.past[0:NT, :], c.iota_c[0:NT, :], s.end_t[0:NT, 0:1], None, ALU.is_ge)).wait()
    dve.sem_inc(s.passed.sem, 1)
    dve.wait_ge(s.binned.sem, s.binned.n + 1)
    half = NCH // 2
    for i, bank in enumerate((banks[3], banks[0])):
        st(dve.tensor_copy(c.bin_of[k][0:1, i * half:(i + 1) * half], c.ps[0:1, bank, 0:half]))
    with dve.Fori(0, NB // 2) as b:
        st.loop(b, 6)
        for i in range(2):
            st.wait(but=1)
            st(dve.tensor_scalar(masks[i], binf[:, :], c.iota_b[:, bass.ds(b * 2 + i, 1)], None, ALU.is_equal))
        for i in range(2):
            st.wait(but=1)
            st(dve.tensor_tensor_scan(runs[i], s.one_row[:, :], masks[i], base[:, bass.ds(b * 2 + i, 1)],
                                      ALU.mult, ALU.add))
        for i in range(2):
            c.hold(dve, c.dve, st.reached() - (1 - i))
            st(dve.copy_predicated(pos[:, :], masks[i].bitcast(U32), runs[i]))
    st.end(NB // 2)
    st.wait()
    st(dve.tensor_copy(s.ki[:, :], pos[:, :])).wait()
    st(dve.tensor_scalar(s.kl[:, :], s.ki[:, :], P - 1, None, ALU.bitwise_and))
    st(dve.tensor_scalar(s.kh[:, :], s.ki[:, :], 7, None, ALU.arith_shift_right)).wait()
    st(dve.tensor_copy(s.run[:, :], s.kl[:, :]))
    st(dve.tensor_copy(s.mask[:, :], s.kh[:, :])).wait()
    st(dve.scalar_tensor_tensor(pos[:, :], s.run[:, :], float(NCH), s.mask[:, :], ALU.mult, ALU.add)).wait()


def sort_pe(c, s, pe, banks):
    pe.wait_ge(s.counted.sem, s.counted.n + 1)
    pe.matmul(c.ps[:, banks[0], 0:NB], c.ones[:, :], s.cnt[:, :], start=True, stop=True)
    pe.matmul(c.ps[:, banks[1], 0:NB], c.upper[:, :], s.cnt[:, :], start=True, stop=True).then_inc(s.summed.sem, 1)
    pe.wait_ge(s.ended.sem, s.ended.n + 1)
    pe.transpose(c.ps[0:NB, banks[2], 0:P], s.inc[:, :], c.ident[:, :]).then_inc(s.turned.sem, 1)
    pe.wait_ge(s.passed.sem, s.passed.n + 1)
    half = NCH // 2
    for i, bank in enumerate((banks[3], banks[0])):
        last = pe.matmul(c.ps[0:1, bank, 0:half], c.ones[0:NT, 0:1], s.past[0:NT, i * half:(i + 1) * half],
                         start=True, stop=True)
    last.then_inc(s.binned.sem, 1)


def end_sort(s):
    for x in (s.counted, s.summed, s.ended, s.turned, s.passed, s.binned):
        x.n += 1


def fields(c, s, dve, index, place, of_index, of_place):
    st = Steps(dve, c.dve)
    st(dve.tensor_copy(s.run[:, :], s.key[index][:, :])).wait()
    st(dve.scalar_tensor_tensor(of_index, s.run[:, :], float(PADKEY), s.run[:, :], ALU.is_lt, ALU.mult))
    st(dve.tensor_copy(of_place, s.lof[place])).wait()


def sort_dst(c, A, s):
    nc = c.nc
    with nc.Block() as block:

        @block.vector
        def _(dve):
            sort_dve(c, s, dve, "dst", (4, 5, 6, 7))
            fields(c, s, dve, "src", "dst", s.fld[:, :, 4], s.fld[:, :, 5])

        @block.tensor
        def _(pe):
            sort_pe(c, s, pe, (4, 5, 6, 7))

        @block.sync
        def _(sp):
            sp.dma_start(s.attr[:, 0:TC - 1, :], A["ea4_main"]).then_inc(s.attr_loaded.sem, 16)
            sp.dma_start(s.attr[0:TAIL, TC - 1, :], A["ea4_tail"]).then_inc(s.attr_loaded.sem, 16)
            for dst, src in s.weights:
                sp.dma_start(dst, src).then_inc(c.load.sem, 16)
            sp.dma_start(c.x[:, 0:NT - 1, :], tiles(A["x"][0:(NT - 1) * P, :], NT - 1, D)).then_inc(c.load.sem, 16)
            sp.dma_start(c.x[0:LASTN, NT - 1, :], A["x"][(NT - 1) * P:N, :]).then_inc(c.load.sem, 16)
            sp.dma_start(s.src_rows.rearrange("(p j) w -> p j w", p=P), c.meta["src"][:, :, :]).then_inc(c.store.sem, 16)

        @block.scalar
        def _(act):
            width = 2 * G8 * PW
            view = s.dst_rows.rearrange("(p j) w -> p (j w)", p=P)
            src = c.pay[:, :, :, :].rearrange("p h g w -> p (h g w)")
            with act.Fori(0, NG // 2) as i:
                act.dma_start(view[:, bass.ds(i * width, width)], src).then_inc(s.prefilled.sem, 16)
    end_sort(s)
    c.load.n += 16 * (len(s.weights) + 2)
    c.store.n += 16
    s.prefilled.n += 16 * (NG // 2)
    s.attr_loaded.n += 32


def groups(eng, total, body, ahead=0, per=2):
    turns = total // per
    for h in range(per):
        body(0, h)
    with eng.Fori(1, turns - (ahead > 0)) as i:
        for h in range(per):
            body(i, h)
    if ahead:
        for h in range(per):
            body(turns - 1, h)


def after(i, h, by=1, per=2):
    if h + by < per:
        return i, h + by
    return None if isinstance(i, int) and i == NG // per - 1 else (i + 1, h + by - per)


def first(i):
    return isinstance(i, int) and i == 0


def at(q, per, start, n):
    if isinstance(q, int):
        return slice(q * per + start, q * per + start + n)
    return bass.ds(q * per + start, n)


def scatter_dst(c, A, s):
    nc = c.nc
    m = s.m
    n0 = SCG // 2

    def all_groups(eng, body):
        groups(eng, SCG, lambda i, h: body(i, h, G8))
        body(n0, 0, G8)
        body(n0, 1, REST)

    with nc.Block() as block:

        @block.sync
        def _(sp):
            def load(i, h, n):
                q = 2 * i + h
                width = G8 * P if n == G8 else E - SCG * G8 * P
                if not first(i):
                    sp.wait_ge(m.h_mm.sem, q * 2 - 2 + m.h_mm.n)
                sp.dma_start(s.ea8[:, h, 0:width], A["ea8"][:, at(q, G8 * P, 0, width)]).then_inc(m.ea[h].sem, 16)
            all_groups(sp, load)

        @block.tensor
        def _(pe):
            def mlp(i, h, n):
                q = 2 * i + h
                pe.wait_ge(m.ea[h].sem, i * 16 + (m.ea[h].n + 16))
                for b in range(2):
                    w = min(512, n * P - 512 * b)
                    if not (first(i) and h == 0):
                        pe.wait_ge(m.silu.sem, q * 2 + (m.silu.n + b - 1))
                    pe.matmul(c.ps[0:64, b, 0:w], s.fc1[:, :], s.ea8[:, h, 512 * b:512 * b + w],
                              start=True, stop=True).then_inc(m.h_mm.sem, 1)
                for b in range(2):
                    pe.wait_ge(m.silu.sem, q * 2 + (m.silu.n + b + 1))
                    if not (first(i) and h == 0):
                        pe.wait_ge(m.copied.sem, q * 2 + (m.copied.n + b - 1))
                    for j in range(min(4, n - 4 * b)):
                        last = pe.matmul(c.ps[:, 2 + b, j * P:(j + 1) * P], s.hid[:, b, j * P:(j + 1) * P],
                                         s.fc2[:, :], start=True, stop=True)
                    last.then_inc(m.w_mm.sem, 1)
            groups(pe, SCG // 2, lambda i, h: mlp(i, h, G8))
            sort_pe(c, s, pe, (4, 5, 6, 7))
            with pe.Fori(SCG // 4, n0) as i:
                mlp(i, 0, G8)
                mlp(i, 1, G8)
            mlp(n0, 0, G8)
            mlp(n0, 1, REST)

        @block.vector
        def _(dve):
            sort_dve(c, s, dve, "src", (4, 5, 6, 7))
            fields(c, s, dve, "dst", "src", s.fsrc[:, :, 0], s.fsrc[:, :, 1])

        @block.scalar
        def _(act):
            def payload(i, h, n):
                q = 2 * i + h
                for b in range(2):
                    w = min(512, n * P - 512 * b)
                    act.wait_ge(m.h_mm.sem, q * 2 + (m.h_mm.n + b + 1))
                    if not (first(i) and h == 0):
                        act.wait_ge(m.w_mm.sem, q * 2 + (m.w_mm.n + b - 1))
                    nc.scalar.activation(s.hid[:, b, 0:w], c.ps[0:64, b, 0:w], ACT.Silu).then_inc(m.silu.sem, 1)
                if not first(i):
                    act.wait_ge(m.sc[h].sem, i * (16 * G8) + m.sc[h].n)
                nc.scalar.activation(c.idx[:, h, 0:n], s.pos["dst"][:, at(q, G8, 0, n)], ACT.Copy)
                nc.scalar.activation(c.pay[:, h, 0:n, EV:EV + 5], s.fld[:, at(q, G8, 0, n), 1:6], ACT.Copy)
                for b in range(2):
                    k = min(4, n - 4 * b)
                    act.wait_ge(m.w_mm.sem, q * 2 + (m.w_mm.n + b + 1))
                    w4 = c.ps[:, 2 + b, :].rearrange("p (j a t u) -> p j a t u", j=4, a=2, t=2)
                    to = c.pay[:, h, 4 * b:4 * b + k, 0:P].rearrange("p j (a t u) -> p j a t u", a=2, t=2)
                    nc.scalar.activation(to[:, :, :, 1, :], w4[:, 0:k, :, 1, :], ACT.Copy)
                    for j in range(k):
                        last = nc.scalar.activation(to[:, j, :, 0, :], w4[:, j, :, 0, :], ACT.Copy,
                                                    scale=s.attr[:, at(q, G8, 4 * b + j, 1), 0])
                    last.then_inc(m.copied.sem, 1)
            act.wait_ge(s.prefilled.sem, s.prefilled.n)
            act.wait_ge(s.attr_loaded.sem, s.attr_loaded.n)
            all_groups(act, payload)

        @block.gpsimd
        def _(pool):
            pool.wait_ge(s.prefilled.sem, s.prefilled.n)
            def send(i, h, n):
                c.hold(pool, m.copied, i * 4 + (h * 2 + m.copied.n + 2))
                for j in range(n):
                    pool.indirect_dma_start(s.dst_rows, bass.IndirectOffsetOnAxis(ap=c.idx[:, h, j:j + 1], axis=0),
                                            c.pay[:, h, j, :], None).then_inc(m.sc[h].sem, 16)
            all_groups(pool, send)
            pool.wait_ge(m.sc[0].sem, m.sc[0].n + 16 * G8 * (n0 + 1))
            pool.wait_ge(m.sc[1].sem, m.sc[1].n + 16 * (G8 * n0 + REST))
    for x in (m.h_mm, m.silu, m.w_mm, m.copied):
        x.n += 2 * (SCG + 1)
    m.ea[0].n += 16 * (n0 + 1)
    m.ea[1].n += 16 * (n0 + 1)
    end_sort(s)
    m.sc[0].n += 16 * G8 * (n0 + 1)
    m.sc[1].n += 16 * (G8 * n0 + REST)


def scatter_src(c, s):
    nc = c.nc
    m = s.m
    n0 = SCG // 2

    def all_groups(eng, body):
        groups(eng, SCG, lambda i, h: body(i, h, G8))
        body(n0, 0, G8)
        body(n0, 1, REST)

    with nc.Block() as block:

        @block.scalar
        def _(act):
            def payload(i, h, n):
                q = 2 * i + h
                if not first(i):
                    act.wait_ge(m.ss[h].sem, i * (16 * G8) + m.ss[h].n)
                nc.scalar.activation(c.idx[:, h, 0:n], s.pos["src"][:, at(q, G8, 0, n)], ACT.Copy)
                nc.scalar.activation(s.small[:, h, 0:n, :], s.fsrc[:, at(q, G8, 0, n), :],
                                     ACT.Copy).then_inc(m.small.sem, 1)
            all_groups(act, payload)

        @block.gpsimd
        def _(pool):
            def send(i, h, n):
                c.hold(pool, m.small, i * 2 + (h + m.small.n + 1))
                for j in range(n):
                    pool.indirect_dma_start(s.src_rows, bass.IndirectOffsetOnAxis(ap=c.idx[:, h, j:j + 1], axis=0),
                                            s.small[:, h, j, :], None).then_inc(m.ss[h].sem, 16)
            all_groups(pool, send)

        @block.sync
        def _(sp):
            sp.wait_ge(m.ss[0].sem, m.ss[0].n + 16 * G8 * (n0 + 1))
            sp.wait_ge(m.ss[1].sem, m.ss[1].n + 16 * (G8 * n0 + REST))
            sp.dma_start(c.meta["src"][:, :, :], s.src_rows.rearrange("(p j) w -> p j w", p=P)).then_inc(c.load.sem, 16)
            sp.wait_ge(c.load.sem, c.load.n + 16)
    m.small.n += SCG + 1
    m.ss[0].n += 16 * G8 * (n0 + 1)
    m.ss[1].n += 16 * (G8 * n0 + REST)
    c.load.n += 16


def load_bins(c, eng, k, q):
    _, vals = c.nc.values_load_multi_w_load_instructions(
        c.bin_of[k][0:1, at(q, G8, 0, G8)], engines=[eng], min_val=0, max_val=NB - 1,
        skip_runtime_bounds_check_because="the sort makes them from 0 to NB - 1")
    return vals


def one_hot(c, h, places):
    c.nc.vector.tensor_tensor(c.hot[:, h, :, :], c.iota[:, :].unsqueeze(1).broadcast_to([P, G8, P]),
                              places.broadcast_to([P, G8, P]), ALU.is_equal).then_inc(c.hot_ready.sem, 1)


def add_chunk(c, dve, q, j, bin_, width, product):
    dve.wait_ge(c.mm.sem, q * G8 + (c.mm.n + j + 1))
    if not (first(q) and j == 0):
        dve.wait_ge(c.added.sem, q * G8 + (c.added.n + j))
    to = c.acc[:, bass.ds(bin_, 1), 0:width]
    c.nc.vector.tensor_tensor(to, to, product, ALU.add).then_inc(c.added.sem, 1)


def end_pass(c, per=2):
    c.mm.n += NCH
    c.added.n += NCH
    c.hot_ready.n += NG
    c.idx_ready.n += NG
    for g in c.gathered[0:per]:
        g.n += 16 * G8 * (NG // per)


def messages(c, s, table):
    nc = c.nc
    m = s.m
    rows3 = s.dst_rows.rearrange("(p j) w -> p j w", p=P)
    rows_of = lambda r: ring_rows(c, r, D)

    with nc.Block() as block:

        @block.sync
        def _(sp):
            def load(i, r):
                q = RING * i + r
                if not first(i):
                    c.hold(sp, c.mm, q * G8 + (c.mm.n - (RING - 1) * G8))
                    sp.wait_ge(m.kept.sem, q + (m.kept.n - RING + 1))
                sp.dma_start(s.pay4[:, r, :, :], rows3[:, at(q, G8, 0, G8), :]).then_inc(m.pay[r].sem, 16)
            groups(sp, NG, load, per=RING)

        @block.scalar
        def _(act):
            def indices(i, r):
                q = RING * i + r
                act.wait_ge(m.pay[r].sem, i * 16 + (m.pay[r].n + 16))
                if not first(i):
                    act.wait_ge(m.prod.sem, q * 2 + (m.prod.n - 2 * (RING - 1)))
                nc.scalar.activation(c.idx[:, r, :], s.pay4[:, r, :, SRC], ACT.Copy).then_inc(c.idx_ready.sem, 1)
                nc.scalar.activation(c.meta["dst"][:, at(q, G8, 0, G8), :], s.pay4[:, r, :, SRC:SRC + 2],
                                     ACT.Copy).then_inc(m.kept.sem, 1)

            def scaled(i, r):
                q = RING * i + r
                if after(i, r, 2, RING):
                    indices(*after(i, r, 2, RING))
                act.wait_ge(m.pay[r].sem, i * 16 + (m.pay[r].n + 16))
                if not (first(i) and r < 2):
                    act.wait_ge(m.prod.sem, q * 2 + (m.prod.n - 2))
                for j in range(G8):
                    w13 = s.pay4[:, r, j, 0:P].rearrange("p (t u) -> p t u", t=4)[:, 1:4:2, :]
                    for a in range(3):
                        last = nc.scalar.activation(s.wev[:, r % 2, j, a, :, :], w13, ACT.Copy,
                                                    scale=s.pay4[:, r, j, EV + a:EV + a + 1])
                    if j % 4 == 3:
                        last.then_inc(m.scaled.sem, 1)
            indices(0, 0)
            indices(0, 1)
            groups(act, NG, scaled, ahead=2, per=RING)

        @block.gpsimd
        def _(pool):
            groups(pool, NG, ring_gather(c, pool, table, D), per=RING)

        @block.vector
        def _(dve):
            def hot(i, r):
                q = RING * i + r
                dve.wait_ge(m.pay[r].sem, i * 16 + (m.pay[r].n + 16))
                if not (first(i) and r < 2):
                    dve.wait_ge(c.mm.sem, q * G8 + (c.mm.n - G8))
                one_hot(c, r % 2, s.pay4[:, r, :, LO:LO + 1])

            def products(i, r, b, step):
                q = RING * i + r
                js = slice(4 * b, 4 * b + 4)
                w = s.pay4[:, r, js, 0:P].rearrange("p j (t u) -> p j t u", t=4)
                wev = s.wev[:, r % 2, js, :, :, :]
                g = rows_of(r)[:, js, :].rearrange("p j (t u) -> p j t u", t=4)
                if step == 0:
                    if b == 0:
                        dve.wait_ge(c.gathered[r].sem, i * (16 * G8) + (c.gathered[r].n + 16 * G8))
                    if not (first(i) and r == 0):
                        dve.wait_ge(c.mm.sem, q * G8 + (c.mm.n + 4 * b + 4 - G8))
                    dve.wait_ge(m.scaled.sem, q * 2 + (m.scaled.n + b + 1))
                    if not (first(q) and b == 0):
                        dve.wait_ge(m.prod.sem, q * 2 + (m.prod.n + b))
                    nc.vector.tensor_tensor(s.dot, wev[:, :, :, 1, :], g[:, :, 1:4, :],
                                            ALU.mult).then_inc(m.dotted.sem, 1)
                elif step == 1:
                    nc.vector.tensor_tensor(s.prod[:, js, 0, MUL:2 * MUL], w[:, :, 0, :], g[:, :, 0, :], ALU.mult)
                elif step == 2:
                    nc.vector.tensor_tensor(s.prod[:, js, 1:4, 0:MUL], wev[:, :, :, 0, :],
                                            g[:, :, 0:1, :].broadcast_to([P, 4, 3, MUL]), ALU.mult)
                elif step == 3:
                    nc.vector.tensor_tensor(s.prod[:, js, 1:4, MUL:2 * MUL],
                                            w[:, :, 2:3, :].broadcast_to([P, 4, 3, MUL]), g[:, :, 1:4, :], ALU.mult)
                else:
                    dve.wait_ge(m.dotted.sem, q * 2 + (m.dotted.n + b + 1))
                    nc.vector.tensor_reduce(s.prod[:, js, 0, 0:MUL], s.dot.rearrange("p j a u -> p j u a"),
                                            AX.X, ALU.add).then_inc(m.prod.sem, 1)

            def reduce(i, r):
                q = RING * i + r
                bins = load_bins(c, mybir.EngineType.DVE, "dst", q)
                products(i, r, 1, 0)
                for j in range(4):
                    add_chunk(c, dve, q, j, bins[j], AW, c.ps[:, j:j + 1, 0:AW])
                    products(i, r, 1, j + 1)
                if after(i, r, 1, RING):
                    hot(*after(i, r, 1, RING))
                    products(*after(i, r, 1, RING), 0, 0)
                for j in range(4, G8):
                    add_chunk(c, dve, q, j, bins[j], AW, c.ps[:, j:j + 1, 0:AW])
                    if after(i, r, 1, RING):
                        products(*after(i, r, 1, RING), 0, j - 3)
            hot(0, 0)
            for step in range(5):
                products(0, 0, 0, step)
            groups(dve, NG, reduce, ahead=1, per=RING)

        @block.tensor
        def _(pe):
            def product(i, r):
                q = RING * i + r
                pe.wait_ge(c.hot_ready.sem, q + (c.hot_ready.n + 1))
                for j in range(G8):
                    if j % 4 == 0:
                        pe.wait_ge(m.prod.sem, q * 2 + (m.prod.n + j // 4 + 1))
                    if not (first(i) and r == 0):
                        pe.wait_ge(c.added.sem, q * G8 + (c.added.n + j - G8 + 1))
                    pe.matmul(c.ps[:, j, 0:AW], c.hot[:, r % 2, j, :],
                              s.prod[:, j, :, :].rearrange("p g u -> p (g u)"),
                              start=True, stop=True).then_inc(c.mm.sem, 1)
            groups(pe, NG, product, per=RING)
    end_pass(c, RING)
    for p in m.pay:
        p.n += 16 * (NG // RING)
    m.kept.n += NG
    for x in (m.prod, m.scaled, m.dotted):
        x.n += 2 * NG


def ring_rows(c, r, width):
    return c.rows[:, r % 2, :, (r // 2) * width:(r // 2 + 1) * width]


def ring_indices(c, act, k, used, per):
    def body(i, r):
        q = RING * i + r
        if not first(i):
            act.wait_ge(used.sem, q * per + (used.n - (RING - 1) * per))
        c.nc.scalar.activation(c.idx[:, r, :], c.meta[k][:, at(q, G8, 0, G8), 0], ACT.Copy).then_inc(c.idx_ready.sem, 1)
    return body


def ring_gather(c, pool, table, width):
    def body(i, r):
        c.hold(pool, c.idx_ready, i * RING + (r + c.idx_ready.n + 1))
        for j in range(G8):
            pool.indirect_dma_start(ring_rows(c, r, width)[:, j, :], None, table,
                                    bass.IndirectOffsetOnAxis(ap=c.idx[:, r, j:j + 1], axis=0)
                                    ).then_inc(c.gathered[r].sem, 16)
    return body


def copy_indices(c, act, k):
    def body(i, h):
        q = 2 * i + h
        if not first(i):
            act.wait_ge(c.mm.sem, q * G8 + (c.mm.n - G8))
        c.nc.scalar.activation(c.idx[:, h, :], c.meta[k][:, at(q, G8, 0, G8), 0], ACT.Copy).then_inc(c.idx_ready.sem, 1)
    return body


def gather_rows(c, pool, table, to):
    def body(i, h):
        c.hold(pool, c.idx_ready, i * 2 + (h + c.idx_ready.n + 1))
        for j in range(G8):
            pool.indirect_dma_start(to(h, j), None, table,
                                    bass.IndirectOffsetOnAxis(ap=c.idx[:, h, j:j + 1], axis=0)
                                    ).then_inc(c.gathered[h].sem, 16)
    return body


def aggregate(c, k, table, width, used):
    nc = c.nc
    with nc.Block() as block:

        @block.scalar
        def _(act):
            groups(act, NG, copy_indices(c, act, k))

        @block.gpsimd
        def _(pool):
            groups(pool, NG, gather_rows(c, pool, table, lambda h, j: c.rows[:, h, j, 0:width]))

        @block.vector
        def _(dve):
            def reduce(i, h):
                q = 2 * i + h
                if not first(i):
                    dve.wait_ge(c.mm.sem, q * G8 + (c.mm.n - G8))
                one_hot(c, h, c.meta[k][:, at(q, G8, 0, G8), 1:2])
                bins = load_bins(c, mybir.EngineType.DVE, k, q)
                for j in range(G8):
                    add_chunk(c, dve, q, j, bins[j], used, c.ps[:, j:j + 1, 0:used])
            groups(dve, NG, reduce)

        @block.tensor
        def _(pe):
            def product(i, h):
                q = 2 * i + h
                pe.wait_ge(c.gathered[h].sem, i * (16 * G8) + (c.gathered[h].n + 16 * G8))
                pe.wait_ge(c.hot_ready.sem, q + (c.hot_ready.n + 1))
                for j in range(G8):
                    if not (first(i) and h == 0):
                        pe.wait_ge(c.added.sem, q * G8 + (c.added.n + j - G8 + 1))
                    pe.matmul(c.ps[:, j, 0:used], c.hot[:, h, j, :], c.rows[:, h, j, 0:used],
                              start=True, stop=True).then_inc(c.mm.sem, 1)
            groups(pe, NG, product)
    end_pass(c)


def node_product(c, s, feed, parts, part_width, products, steps, take):
    nc = c.nc
    m = s.m

    def tiles_of(eng, body):
        body(0)
        with eng.Fori(1, NB // 2 - 1) as i:
            body(i)
        body(NB // 2 - 1)

    last_ = lambda i: isinstance(i, int) and i == NB // 2 - 1

    with nc.Block() as block:

        @block.scalar
        def _(act):
            def fill(k, slot, free):
                if free:
                    act.wait_ge(m.turned.sem, k + (m.turned.n - 1))
                feed(k, slot).then_inc(m.fed.sem, 1)

            def body(i):
                if first(i):
                    fill(0, 0, False)
                    fill(1, 1, False)
                for slot in range(2):
                    k = 2 * i + slot
                    act.wait_ge(m.turned.sem, k + (m.turned.n + 1))
                    if not first(i):
                        act.wait_ge(m.multiplied.sem, k + (m.multiplied.n - 1))
                    nc.scalar.activation(s.ut[0:part_width, slot, 0:parts * P], c.ps[0:part_width, slot, 0:parts * P],
                                         ACT.Copy).then_inc(m.back.sem, 1)
                    if not last_(i):
                        fill(k + 2, slot, True)
            tiles_of(act, body)

        @block.tensor
        def _(pe):
            def turn(k, slot, free):
                if free:
                    pe.wait_ge(m.back.sem, k + (m.back.n - 1))
                c.hold(pe, m.fed, k + (m.fed.n + 1))
                for a in range(parts):
                    last = pe.transpose(c.ps[0:part_width, slot, a * P:(a + 1) * P],
                                        s.u[:, slot, a * part_width:(a + 1) * part_width], c.ident[:, :])
                last.then_inc(m.turned.sem, 1)

            def body(i):
                if first(i):
                    turn(0, 0, False)
                for slot in range(2):
                    k = 2 * i + slot
                    if not (last_(i) and slot == 1):
                        turn(k + 1, 1 - slot, not (first(i) and slot == 0))
                    pe.wait_ge(m.back.sem, k + (m.back.n + 1))
                    if not first(i):
                        pe.wait_ge(m.taken.sem, k + (m.taken.n - 1))
                    for a, w, lo, hi, start, stop in products:
                        last = pe.matmul(c.ps[:, 4 + slot, lo:hi], s.ut[0:part_width, slot, a * P:(a + 1) * P], w,
                                         start=start, stop=stop)
                    last.then_inc(m.multiplied.sem, 1)
            tiles_of(pe, body)

        @block.vector
        def _(dve):
            st = Steps(dve, c.dve)

            def body(i):
                st.loop(i, 2 * steps)
                for slot in range(2):
                    k = 2 * i + slot
                    dve.wait_ge(m.multiplied.sem, k + (m.multiplied.n + 1))
                    take(st, k, 4 + slot).then_inc(m.taken.sem, 1)
                assert st.k == st.per, (st.k, st.per)
            tiles_of(dve, body)
            st.end(NB // 2)
    for x in (m.fed, m.turned, m.back, m.multiplied, m.taken):
        x.n += NB


def one(k):
    return slice(k, k + 1) if isinstance(k, int) else bass.ds(k, 1)


def stats(c, s, st, k, ap):
    c.hold(st.eng, st.c, st.reached())
    return c.nc.vector.bn_stats(s.st6[:, one(k), :].rearrange("p a b -> p (a b)"), ap)


def moments(c, s, dve, width):
    v, st = c.nc.vector, Steps(dve, c.dve)
    me, ve, mo, vo = (s.st6[:, :, i] for i in (1, 2, 4, 5))
    mean, var = c.mv[:, :, 0], c.mv[:, :, 1]
    st(v.tensor_tensor(mean, me, mo, ALU.add))
    st(v.tensor_tensor(mo, me, mo, ALU.subtract))
    st(v.tensor_tensor(var, ve, vo, ALU.add)).wait()
    st(v.tensor_scalar(mean, mean, 0.5, None, ALU.mult))
    st(v.tensor_tensor(mo, mo, mo, ALU.mult))
    st(v.tensor_scalar(var, var, 1.0 / width, None, ALU.mult)).wait()
    st(v.scalar_tensor_tensor(var, mo, 0.25, var, ALU.mult, ALU.add))


def seg(ap, g):
    return ap[:, g * SEGT:(g + 1) * SEGT]


def spread(col, width):
    return col.unsqueeze(2).broadcast_to([P, col.shape[1], width])


def over(row, n):
    return row.unsqueeze(1).broadcast_to([P, n, row.shape[1]])


def root(c, s, to, src, bias, width=None):
    nc = c.nc
    m = s.m
    with nc.Block() as block:

        @block.scalar
        def _(act):
            if width:
                act.wait_ge(m.moments.sem, m.moments.n + 1)
            nc.scalar.activation(to, src, ACT.Sqrt, bias=bias).then_inc(m.rooted.sem, 1)

        @block.vector
        def _(dve):
            if width:
                moments(c, s, dve, width)
                dve.wait_ge(c.dve.sem, c.dve.n)
                dve.sem_inc(m.moments.sem, 1)
            dve.wait_ge(m.rooted.sem, m.rooted.n + 1)
            Steps(dve, c.dve)(nc.vector.reciprocal(to, to))
    m.rooted.n += 1
    m.moments.n += bool(width)


def normalise(c, s, self_term=False, clear=False, table=None, out=None):
    nc = c.nc
    root(c, s, c.rstd[:, :], c.mv[:, :, 1], c.eps[:, 0:1], D)
    with nc.Block() as block:

        @block.vector
        def _(dve):
            st = Steps(dve, c.dve)
            for g in range(NSEG):
                x = seg(c.x, g)
                st(nc.vector.tensor_tensor(x, x, spread(seg(c.mv, g)[:, :, 0], D), ALU.subtract)).wait()
                last = nc.vector.tensor_tensor(x, x, spread(seg(c.rstd, g), D), ALU.mult)
                if self_term:
                    st(last).wait()
                    last = nc.vector.tensor_tensor(seg(c.acc, g)[:, :, 0:D], x, spread(seg(c.dinv, g), D), ALU.mult)
                last.then_inc(s.m.part.sem, 1)
            if clear:
                nc.vector.memset(c.acc[:, :, :], 0.0)

        @block.sync
        def _(sp):
            for g in range(NSEG):
                sp.wait_ge(s.m.part.sem, s.m.part.n + g + 1)
                src = seg(c.acc, g)[:, :, 0:D] if self_term else seg(c.x, g)
                if out is None:
                    sp.dma_start(tiles(table, NB, D)[:, g * SEGT:(g + 1) * SEGT, :], src).then_inc(c.store.sem, 16)
                elif g < NSEG - 1:
                    sp.dma_start(tiles(out[0:(NSEG - 1) * SEGT * P, :], 0, 0)[:, g * SEGT:(g + 1) * SEGT, :], src
                                 ).then_inc(c.store.sem, 16)
                else:
                    full = NT - 1 - g * SEGT
                    sp.dma_start(tiles(out[g * SEGT * P:(NT - 1) * P, :], 0, 0), src[:, 0:full, :]).then_inc(c.store.sem, 16)
                    sp.dma_start(out[(NT - 1) * P:N, :], c.x[0:LASTN, NT - 1, :]).then_inc(c.store.sem, 16)
            sp.wait_ge(c.store.sem, c.store.n + 16 * (NSEG + (out is not None)))
    s.m.part.n += NSEG
    c.store.n += 16 * (NSEG + (out is not None))


def write_table(c, src, table, width):
    nc = c.nc
    with nc.Block() as block:

        @block.sync
        def _(sp):
            for g in range(NSEG):
                sp.dma_start(tiles(table, NB, width)[:, g * SEGT:(g + 1) * SEGT, :], seg(src, g)).then_inc(c.store.sem, 16)
            sp.wait_ge(c.store.sem, c.store.n + 16 * NSEG)
    c.store.n += 16 * NSEG


def clear_acc(c, value=0.0):
    nc = c.nc
    with nc.Block() as block:

        @block.vector
        def _(dve):
            Steps(dve, c.dve)(nc.vector.memset(c.acc[:, :, :], value))


def conv_norm(c, s, l, table):
    nc = c.nc
    root(c, s, c.rstd[:, :], c.mv[:, :, 1], c.eps[:, 0:1], HID)
    m = s.m
    gain, shift = s.gain[l], s.shift[l]
    with nc.Block() as block:

        @block.vector
        def _(dve):
            st = Steps(dve, c.dve)

            def finish(g):
                a = seg(c.acc, g)[:, :, 0:HID]
                dve.wait_ge(m.powered.sem, m.powered.n + g + 1)
                st(nc.vector.scalar_tensor_tensor(a, a, 0.0, s.ex[:, g % 2, :, :], ALU.max, ALU.add)).wait()
                nc.vector.scalar_tensor_tensor(a, a, -1.0, spread(seg(c.dinv, g), HID), ALU.add,
                                               ALU.mult).then_inc(m.part.sem, 1)

            for g in range(NSEG):
                a = seg(c.acc, g)[:, :, 0:HID]
                st(nc.vector.tensor_tensor(a, a, spread(seg(c.mv, g)[:, :, 0], HID), ALU.subtract)).wait()
                nc.vector.tensor_tensor(a, a, spread(seg(c.rstd, g), HID), ALU.mult).then_inc(m.centred.sem, 1)
                if g:
                    dve.wait_ge(m.shifted.sem, m.shifted.n + g)
                    b = seg(c.acc, g - 1)[:, :, 0:HID]
                    nc.vector.tensor_scalar(s.ex[:, (g - 1) % 2, :, :], b, 0.0, None, ALU.min).then_inc(m.cut.sem, 1)
                if g >= 2:
                    finish(g - 2)
            dve.wait_ge(m.shifted.sem, m.shifted.n + NSEG)
            b = seg(c.acc, NSEG - 1)[:, :, 0:HID]
            nc.vector.tensor_scalar(s.ex[:, (NSEG - 1) % 2, :, :], b, 0.0, None, ALU.min).then_inc(m.cut.sem, 1)
            finish(NSEG - 2)
            finish(NSEG - 1)

        @block.gpsimd
        def _(pool):
            for g in range(NSEG):
                a = seg(c.acc, g)[:, :, 0:HID]
                pool.wait_ge(m.centred.sem, m.centred.n + g + 1)
                pool.tensor_tensor(a, a, over(gain[:, :], SEGT), ALU.mult).then_inc(c.pool.sem, 1)
                pool.wait_ge(c.pool.sem, c.pool.n + g + 1)
                pool.tensor_tensor(a, a, over(shift[:, :], SEGT), ALU.add).then_inc(m.shifted.sem, 1)

        @block.scalar
        def _(act):
            for g in range(NSEG):
                act.wait_ge(m.cut.sem, m.cut.n + g + 1)
                e = s.ex[:, g % 2, :, :]
                nc.scalar.activation(e, e, ACT.Exp).then_inc(m.powered.sem, 1)

        @block.sync
        def _(sp):
            if table is not None:
                for g in range(NSEG):
                    sp.wait_ge(m.part.sem, m.part.n + g + 1)
                    sp.dma_start(tiles(table, NB, HID)[:, g * SEGT:(g + 1) * SEGT, :],
                                 seg(c.acc, g)[:, :, 0:HID]).then_inc(c.store.sem, 16)
                sp.wait_ge(c.store.sem, c.store.n + 16 * NSEG)
    if table is not None:
        c.store.n += 16 * NSEG
    for x in (m.centred, m.shifted, m.cut, m.powered, m.part):
        x.n += NSEG
    c.pool.n += NSEG


def tile_stats(c, s, dve, st):
    with dve.Fori(0, NB) as k:
        st.loop(k, 1)
        st(c.nc.vector.bn_stats(s.st6[:, one(k), :].rearrange("p a b -> p (a b)"),
                                c.x[:, one(k), :].rearrange("p a b -> p (a b)")))
    st.end(NB)
    st.wait()


def add_gcn(c, s):
    nc = c.nc
    with nc.Block() as block:

        @block.vector
        def _(dve):
            st = Steps(dve, c.dve)
            for g in range(NSEG):
                a, x = seg(c.acc, g)[:, :, 0:D], seg(c.x, g)
                st(nc.vector.tensor_tensor(a, a, spread(seg(c.dinv, g), D), ALU.mult))
                st(nc.vector.tensor_tensor(x, x, over(s.b3[:, :], SEGT), ALU.add)).wait()
                st(nc.vector.tensor_tensor(x, x, a, ALU.add))
            st.wait()
            tile_stats(c, s, dve, st)


def add_gat(c, s):
    nc = c.nc
    with nc.Block() as block:

        @block.vector
        def _(dve):
            st = Steps(dve, c.dve)
            two = lambda ap: ap.rearrange("p n (h u) -> p n h u", h=HEADS)
            sums = two(c.acc[:, :, 0:D + HEADS])
            den = sums[:, :, :, CH]
            st(nc.vector.tensor_scalar(den, den, 1e-16, None, ALU.add)).wait()
            st(nc.vector.reciprocal(den, den)).wait()
            for g in range(0, NSEG, 2):
                one_of = lambda k: (seg(c.x, g + k), s.ex[:, k, :, 0:D], s.ex[:, k, :, D:2 * D])
                for k in range(2):
                    x, a, t = one_of(k)
                    st.wait(but=1)
                    st(nc.vector.tensor_tensor(two(a), seg(sums, g + k)[:, :, :, 0:CH],
                                               seg(sums, g + k)[:, :, :, CH:CH + 1].broadcast_to([P, SEGT, HEADS, CH]),
                                               ALU.mult))
                for k in range(2):
                    x, a, t = one_of(k)
                    st.wait(but=1)
                    st(nc.vector.tensor_tensor(a, a, over(s.bias[:, :], SEGT), ALU.add))
                for k in range(2):
                    x, a, t = one_of(k)
                    st.wait(but=1)
                    st(nc.vector.scalar_tensor_tensor(t, a, 0.0, over(s.prelu[:, :], SEGT), ALU.min, ALU.mult))
                for k in range(2):
                    x, a, t = one_of(k)
                    st.wait(but=1)
                    st(nc.vector.scalar_tensor_tensor(a, a, 0.0, t, ALU.max, ALU.add))
                for k in range(2):
                    x, a, t = one_of(k)
                    st.wait(but=1)
                    st(nc.vector.tensor_tensor(x, x, a, ALU.add))
            st.wait()
            tile_stats(c, s, dve, st)


def bin_starts(c, s):
    nc = c.nc
    half = NCH // 2
    with nc.Block() as block:

        @block.vector
        def _(dve):
            st = Steps(dve, c.dve)
            st(nc.vector.tensor_copy(s.bin_row[0:1, :], c.bin_of["dst"][:, :])).wait()
            dve.sem_inc(s.m.fed.sem, 1)
            dve.wait_ge(s.m.turned.sem, s.m.turned.n + 1)
            for i in range(2):
                st(nc.vector.tensor_copy(s.bin_all[:, i * half:(i + 1) * half], c.ps[:, i, 0:half]))
            st(nc.vector.memset(s.new_bin[:, :], 1.0)).wait()
            st(nc.vector.tensor_tensor(s.new_bin[:, 1:NCH], s.bin_all[:, 1:NCH], s.bin_all[:, 0:NCH - 1],
                                       ALU.not_equal)).wait()
            st(nc.vector.tensor_scalar(s.new_bin[:, :], s.new_bin[:, :], NEG, None, ALU.mult))
            nc.vector.memset(s.top[:, :, :, :], NEG)
            nc.vector.memset(c.acc[:, :, :], 0.0)

        @block.tensor
        def _(pe):
            pe.wait_ge(s.m.fed.sem, s.m.fed.n + 1)
            for i in range(2):
                last = pe.matmul(c.ps[:, i, 0:half], c.ones[0:1, :], s.bin_row[0:1, i * half:(i + 1) * half],
                                 start=True, stop=True)
            last.then_inc(s.m.turned.sem, 1)
    s.m.fed.n += 1
    s.m.turned.n += 1


def attend(c, s, table):
    nc = c.nc
    m = s.m
    HW = CH + 1
    width = HEADS * HW
    nxt = lambda i, r, by=1: after(i, r, by, RING)
    hot_of = lambda r: c.hot[:, r, :, :] if r < 2 else s.hot_more[:, r - 2, :, :]
    heads = lambda ap: ap.rearrange("p j (h u) -> p j h u", h=HEADS)
    with nc.Block() as block:

        @block.scalar
        def _(act):
            copy = ring_indices(c, act, "dst", m.weighted, 1)

            def masked(i, r, b):
                q = RING * i + r
                if b == 0:
                    act.wait_ge(c.hot_ready.sem, q + (c.hot_ready.n + 1))
                    nc.scalar.activation(s.mask8[:, :, :], hot_of(r), ACT.Copy, scale=-1.0,
                                         bias=1.0).then_inc(m.masked.sem, 1)
                    act.wait_ge(m.masked.sem, q + (m.masked.n + 1))
                    act.wait_ge(c.gathered[r].sem, i * (16 * G8) + (c.gathered[r].n + 16 * G8))
                if not first(q):
                    act.wait_ge(m.flipped.sem, q * 4 + (m.flipped.n + b - 3))
                rows = heads(ring_rows(c, r, width))
                for j in (2 * b, 2 * b + 1):
                    for a in range(HEADS):
                        last = nc.scalar.activation(s.hot_v[:, j, a, :], s.mask8[:, j, :], ACT.Identity,
                                                    bias=rows[:, j, a, CH:HW], scale=NEG)
                last.then_inc(m.scaled.sem, 1)

            def turned(i, r):
                q = RING * i + r
                for b in range(2):
                    act.wait_ge(m.turned.sem, q * 2 + (m.turned.n + b + 1))
                    nc.scalar.activation(s.hot_t[:, 4 * b:4 * b + 4, :].rearrange("p j n -> p (j n)"),
                                         c.ps[:, 2 + b, :], ACT.Copy).then_inc(m.back.sem, 1)

            def factor(i, r):
                q = RING * i + r
                act.wait_ge(m.maxed.sem, q + (m.maxed.n + 1))
                nc.scalar.activation(s.factor[:, r % 2, :, :], s.drop[:, :, :], ACT.Exp).then_inc(m.factored.sem, 1)

            def body(i, r):
                q = RING * i + r
                if nxt(i, r, 2):
                    copy(*nxt(i, r, 2))
                if nxt(i, r):
                    for b in range(3):
                        masked(*nxt(i, r), b)
                act.wait_ge(m.scored.sem, q + (m.scored.n + 1))
                nc.scalar.activation(heads(s.wt)[:, :, :, CH], s.z[:, :, :], ACT.Exp).then_inc(m.powered.sem, 1)
                if nxt(i, r):
                    masked(*nxt(i, r), 3)
                    turned(*nxt(i, r))
                    factor(*nxt(i, r))
            copy(0, 0)
            copy(0, 1)
            for b in range(4):
                masked(0, 0, b)
            turned(0, 0)
            factor(0, 0)
            groups(act, NG, body, ahead=2, per=RING)

        @block.gpsimd
        def _(pool):
            groups(pool, NG, ring_gather(c, pool, table, width), per=RING)

        @block.vector
        def _(dve):
            st = Steps(dve, c.dve)
            def hot(i, r):
                q = RING * i + r
                if not first(i):
                    dve.wait_ge(c.mm.sem, q * G8 + (c.mm.n - (RING - 1) * G8))
                nc.vector.tensor_tensor(hot_of(r), c.iota[:, :].unsqueeze(1).broadcast_to([P, G8, P]),
                                        c.meta["dst"][:, at(q, G8, 0, G8), 1:2].broadcast_to([P, G8, P]),
                                        ALU.is_equal).then_inc(c.hot_ready.sem, 1)

            def chunk_max(i, r, b):
                q = RING * i + r
                dve.wait_ge(m.flipped.sem, q * 4 + (m.flipped.n + b + 1))
                nc.vector.tensor_reduce(s.mx8[:, 2 * b:2 * b + 2, :].rearrange("p j a -> p (j a)"),
                                        c.ps[:, b % 2, :].rearrange("p (k e) -> p k e", e=P),
                                        AX.X, ALU.max).then_inc(m.reduced.sem, 1)

            def node_scores(i, r):
                q = RING * i + r
                bins = load_bins(c, mybir.EngineType.DVE, "dst", q)
                for j in range(G8):
                    nc.vector.tensor_copy(s.nt8[:, j:j + 1, 0:2], s.nt[:, bass.ds(bins[j], 1), :])
                st(nc.vector.tensor_copy(s.top[:, r % 2, 0, :], s.top[:, 1 - r % 2, G8, :]))

            def running_max(i, r, step):
                q = RING * i + r
                top, ou, ad = s.top[:, r % 2, :, :], s.ou[:, :, :, :], s.nt8[:, :, 0:2]
                pen = s.new_bin[:, at(q, G8, 0, G8)]
                st.wait()
                if step == 0:
                    dve.wait_ge(m.reduced.sem, q * 4 + (m.reduced.n + 4))
                    for a in range(HEADS):
                        st(nc.vector.tensor_tensor_scan(top[:, 1:G8 + 1, a], pen, s.mx8[:, :, a], top[:, 0, a:a + 1],
                                                        ALU.add, ALU.max))
                elif step == 1:
                    st(nc.vector.tensor_tensor(ou[:, 0], top[:, 0:G8, :], pen.unsqueeze(2).broadcast_to([P, G8, HEADS]),
                                               ALU.add))
                    st(nc.vector.tensor_tensor(ou[:, 1], top[:, 1:G8 + 1, :], ad, ALU.add))
                elif step == 2:
                    st(nc.vector.tensor_tensor(ou[:, 0], ou[:, 0], ad, ALU.add))
                elif step == 3:
                    st(nc.vector.scalar_tensor_tensor(ou, ou, SLOPE, ou, ALU.mult, ALU.max))
                else:
                    st(nc.vector.tensor_copy(s.nt8[:, :, 2:4], ou[:, 1]))
                    if not first(q):
                        dve.wait_ge(m.factored.sem, q + m.factored.n)
                    nc.vector.tensor_tensor(s.drop[:, :, :], ou[:, 0], ou[:, 1], ALU.subtract).then_inc(m.maxed.sem, 1)

            def weigh(i, r):
                q = RING * i + r
                dve.wait_ge(c.gathered[r].sem, i * (16 * G8) + (c.gathered[r].n + 16 * G8))
                dve.wait_ge(m.looked.sem, q + (m.looked.n + 1))
                e8 = c.ps[:, 4, 0:4 * G8].rearrange("p (j k) -> p j k", j=G8)
                z, rows = s.z[:, :, :], heads(ring_rows(c, r, width))
                st(nc.vector.tensor_tensor(z, rows[:, :, :, CH], e8[:, :, 0:2], ALU.add)).wait()
                st(nc.vector.scalar_tensor_tensor(z, z, SLOPE, z, ALU.mult, ALU.max)).wait()
                st(nc.vector.tensor_tensor(z, z, e8[:, :, 2:4], ALU.subtract)).wait()
                nc.vector.tensor_scalar(z, z, 0.0, None, ALU.min).then_inc(m.scored.sem, 1)
                if nxt(i, r):
                    chunk_max(*nxt(i, r), 0)
                dve.wait_ge(m.powered.sem, q + (m.powered.n + 1))
                wt = heads(s.wt)
                nc.vector.tensor_tensor(wt[:, :, :, 0:CH], rows[:, :, :, 0:CH],
                                        wt[:, :, :, CH:HW].broadcast_to([P, G8, HEADS, CH]),
                                        ALU.mult).then_inc(m.weighted.sem, 1)

            def add(q, r, j, bin_):
                if j == 0:
                    dve.wait_ge(m.factored.sem, q + (m.factored.n + 1))
                dve.wait_ge(c.mm.sem, q * G8 + (c.mm.n + j + 1))
                for a in range(HEADS):
                    if not (first(q) and j == 0):
                        dve.wait_ge(c.added.sem, q * 2 * G8 + (c.added.n + 2 * j + a - 1))
                    to = c.acc[:, bass.ds(bin_, 1), a * HW:(a + 1) * HW].rearrange("p n u -> p (n u)")
                    nc.vector.scalar_tensor_tensor(to, to, s.factor[:, r % 2, j, a:a + 1],
                                                   c.ps[:, 5 + j % 3, a * HW:(a + 1) * HW],
                                                   ALU.mult, ALU.add).then_inc(c.added.sem, 1)

            def body(i, r):
                q = RING * i + r
                if r == 0:
                    st.loop(i, 11 * RING)
                if nxt(i, r, 2):
                    hot(*nxt(i, r, 2))
                weigh(i, r)
                if nxt(i, r):
                    chunk_max(*nxt(i, r), 1)
                    node_scores(*nxt(i, r))
                    chunk_max(*nxt(i, r), 2)
                    chunk_max(*nxt(i, r), 3)
                bins = load_bins(c, mybir.EngineType.DVE, "dst", q)
                for j in range(G8):
                    if nxt(i, r) and j < 5:
                        running_max(*nxt(i, r), j)
                    add(q, r, j, bins[j])
            hot(0, 0)
            node_scores(0, 0)
            for b in range(4):
                chunk_max(0, 0, b)
            for step in range(5):
                running_max(0, 0, step)
            hot(0, 1)
            groups(dve, NG, body, ahead=2, per=RING)
            assert st.k == 11 * RING - 8
            st.c.n += (NG // RING) * 11 * RING - 8

        @block.tensor
        def _(pe):
            def turn(i, r, j):
                q = RING * i + r
                if j == 0:
                    pe.wait_ge(c.hot_ready.sem, q + (c.hot_ready.n + 1))
                    if not first(q):
                        pe.wait_ge(m.back.sem, q * 2 + m.back.n)
                last = pe.transpose(c.ps[:, 2 + j // 4, (j % 4) * P:(j % 4 + 1) * P], hot_of(r)[:, j, :],
                                    c.ident[:, :])
                if j % 4 == 3:
                    last.then_inc(m.turned.sem, 1)

            def flip(i, r):
                q = RING * i + r
                for b in range(4):
                    pe.wait_ge(m.scaled.sem, q * 4 + (m.scaled.n + b + 1))
                    if not (first(q) and b < 2):
                        pe.wait_ge(m.reduced.sem, q * 4 + (m.reduced.n + b - 1))
                    for k in range(2 * HEADS):
                        last = pe.transpose(c.ps[:, b % 2, k * P:(k + 1) * P], s.hot_v[:, 2 * b + k // 2, k % 2, :],
                                            c.ident[:, :])
                    last.then_inc(m.flipped.sem, 1)

            def look_up(i, r):
                q = RING * i + r
                pe.wait_ge(m.maxed.sem, q + (m.maxed.n + 1))
                for b in range(2):
                    pe.wait_ge(m.back.sem, q * 2 + (m.back.n + b + 1))
                    for j in range(4 * b, 4 * b + 4):
                        last = pe.matmul(c.ps[:, 4, 4 * j:4 * j + 4], s.hot_t[:, j, :], s.nt8[:, j, :],
                                         start=True, stop=True)
                last.then_inc(m.looked.sem, 1)

            def product(i, r):
                q = RING * i + r
                if nxt(i, r):
                    flip(*nxt(i, r))
                pe.wait_ge(m.weighted.sem, q + (m.weighted.n + 1))
                for j in range(G8):
                    before = j - 3 if j >= 3 else (-2, -1, -3)[j]
                    if not (first(q) and before < 0):
                        pe.wait_ge(c.added.sem, q * 2 * G8 + (c.added.n + 2 * before + 2))
                    pe.matmul(c.ps[:, 5 + j % 3, 0:width], hot_of(r)[:, j, :], s.wt[:, j, :],
                              start=True, stop=True).then_inc(c.mm.sem, 1)
                    if nxt(i, r, 2):
                        turn(*nxt(i, r, 2), j)
                if nxt(i, r):
                    look_up(*nxt(i, r))
            for j in range(G8):
                turn(0, 0, j)
            flip(0, 0)
            look_up(0, 0)
            for j in range(G8):
                turn(0, 1, j)
            groups(pe, NG, product, ahead=2, per=RING)
    end_pass(c, RING)
    c.added.n += NCH
    for x in (m.turned, m.back):
        x.n += 2 * NG
    for x in (m.scaled, m.flipped, m.reduced):
        x.n += 4 * NG
    for x in (m.looked, m.scored, m.powered, m.weighted, m.masked, m.maxed, m.factored):
        x.n += NG


def prepare_weights(c, s):
    nc = c.nc
    v = nc.vector
    with nc.Block() as block:

        @block.sync
        def _(sp):
            sp.wait_ge(c.store.sem, c.store.n)

        @block.scalar
        def _(act):
            act.wait_ge(c.load.sem, c.load.n)
            nc.scalar.activation(s.sig[:, :], s.sig[:, :], ACT.Exp, scale=-1.0).then_inc(s.m.rooted.sem, 1)

        @block.vector
        def _(dve):
            st = Steps(dve, c.dve)
            dve.wait_ge(c.load.sem, c.load.n)
            st(v.tensor_scalar(s.lin1[:, :], s.lin1[:, :], MUL ** -0.5, None, ALU.mult))
            st(v.tensor_scalar(s.fc1[:, :], s.fc1[:, :], 8 ** -0.5, None, ALU.mult))
            st(v.tensor_scalar(s.fc2[:, :], s.fc2[:, :], SILU_NORM * 64 ** -0.5, None, ALU.mult))
            scale = 0.25 * (2 * MUL) ** -0.5
            st(v.tensor_scalar(s.lin2s[0:MUL, :], s.lin2s[0:MUL, :], scale * 3 ** -0.5, None, ALU.mult))
            st(v.tensor_scalar(s.lin2s[MUL:2 * MUL, :], s.lin2s[MUL:2 * MUL, :], scale, None, ALU.mult))
            st(v.tensor_scalar(s.lin2v[:, :], s.lin2v[:, :], scale, None, ALU.mult))
            st(v.tensor_tensor(s.attw[:, 0, :], s.wg[:, 0:D], s.att[:, 0, :], ALU.mult))
            st(v.tensor_tensor(s.attw[:, 1, :], s.wdst[:, :], s.att[:, 1, :], ALU.mult)).wait()
            st(v.tensor_reduce(s.wg[:, D:D + 4], s.attw[:, :, :].rearrange("p a (h u) -> p (a h) u", h=HEADS),
                               AX.X, ALU.add))
            dve.wait_ge(s.m.rooted.sem, s.m.rooted.n + 1)
            st(v.tensor_scalar(s.sig[:, :], s.sig[:, :], 1.0, None, ALU.add)).wait()
            st(v.reciprocal(s.sig[:, :], s.sig[:, :])).wait()
            for l in range(3):
                w, a = s.w[l][:, :], s.sig[:, l:l + 1]
                st(v.tensor_scalar(w, w, a, None, ALU.mult))
                st(v.tensor_scalar(s.b[l][:, :], s.b[l][:, :], a, None, ALU.mult))
    s.m.rooted.n += 1


def degrees(c, s):
    root(c, s, c.dinv[:, :], c.acc[:, :, 2 * MUL], c.ones[:, 0:1])


class Scratch:
    pass


def gnn(nc, A, out, upto=None):
    with ExitStack() as ctx:
        c = Chip(nc, ctx)
        s = Scratch()
        sb = c.sb
        flat = c.acc[:, :, :].rearrange("p n w -> p (n w)")
        at_ = [0]

        def lay(width, dt=F32):
            a = flat[:, at_[0]:at_[0] + width]
            at_[0] += width
            return a if dt is F32 else a.bitcast(dt)
        s.key = {k: lay(TC, I32) for k in ("dst", "src")}
        s.lof = {k: lay(TC) for k in ("dst", "src")}
        s.pos = {k: lay(TC) for k in ("dst", "src")}
        s.binf, s.mask, s.run, s.one_row = (lay(TC) for _ in range(4))
        s.ki = lay(TC, I32)
        s.mask2, s.run2 = lay(TC), lay(TC)
        s.kl, s.kh = s.mask2.bitcast(I32), s.run2.bitcast(I32)
        s.fsrc = lay(2 * TC).rearrange("p (t w) -> p t w", w=2)
        s.fld = sb("fld", [P, TC, 6])
        s.attr = s.fld[:, :, 0:4]
        s.pay4 = s.fld[:, :, :].rearrange("p t w -> p (t w)")[:, 0:4 * G8 * PW].rearrange(
            "p (r j w) -> p r j w", r=4, j=G8)
        s.cnt, s.nch, s.inc, s.exc = (sb(n, [P, NB]) for n in ("bin_count", "bin_chunks", "bin_end", "bin_start"))
        s.ci, s.cj = (sb(n, [P, NB], I32) for n in ("bin_count_i", "bin_chunks_i"))
        s.base = {k: sb(f"base_{k}", [P, NB]) for k in ("dst", "src")}
        s.end_t = sb("end_t", [64, 1])
        s.past = c.hot[0:64, 1, :, :].rearrange("p j n -> p (j n)")[:, 0:NCH]
        s.small = sb("small", [P, 2, G8, 2])
        s.hot_v = sb("hot_v", [P, G8, 3, P])
        s.prod = sb("prod", [P, G8, 4, 2 * MUL + 1])
        s.ex = s.hot_v[:, :, :, :].rearrange("p j a n -> p (j a n)")[:, 0:2 * SEGT * HID].rearrange(
            "p (g n w) -> p g n w", g=2, n=SEGT)
        s.hot_t = s.prod[:, :, :, :].rearrange("p j a n -> p (j a n)")[:, 0:G8 * P].rearrange("p (j n) -> p j n", j=G8)
        s.ea8 = s.hot_v[0:8, :, :, :].rearrange("p j a n -> p (j a n)")[:, 0:2 * G8 * P].rearrange(
            "p (h n) -> p h n", h=2)
        s.hid = s.prod[0:64, :, :, :].rearrange("p j a n -> p (j a n)")[:, 0:1024].rearrange("p (b n) -> p b n", b=2)
        s.wt = c.pay[:, 0, :, 0:D + HEADS]
        s.z = c.pay[:, 1, :, 0:HEADS]
        s.u = sb("u", [P, 2, HID])
        s.dot = s.u[:, :, :].rearrange("p a n -> p (a n)")[:, 0:4 * 3 * MUL].rearrange(
            "p (j a u) -> p j a u", j=4, a=3)
        s.wev = s.hot_v[:, :, :, :].rearrange("p j a n -> p (j a n)").rearrange(
            "p (h j a t u) -> p h j a t u", h=2, j=G8, a=3, t=2)
        s.ut = sb("ut", [P, 2, 4 * P])
        s.st6 = sb("st6", [P, NB, 6])
        fld = s.fld[:, :, :].rearrange("p t w -> p (t w)")
        s.new_bin, s.bin_all, s.bin_row = (fld[:, i * NCH:(i + 1) * NCH] for i in range(3))
        s.hot_more = fld[:, NCH:NCH + 2 * G8 * P].rearrange("p (h j n) -> p h j n", h=2, j=G8)
        s.top = sb("top", [P, 2, G8 + 1, HEADS])
        s.ou = sb("ou", [P, 2, G8, HEADS])
        s.drop = sb("drop", [P, G8, HEADS])
        s.factor = sb("factor", [P, 2, G8, HEADS])
        s.nt8 = sb("nt8", [P, G8, 2 * HEADS])
        s.mask8 = s.prod[:, :, :, :].rearrange("p j a n -> p (j a n)")[:, G8 * P:2 * G8 * P].rearrange(
            "p (j n) -> p j n", j=G8)
        s.mx8 = sb("mx8", [P, G8, HEADS])
        s.nt = sb("nt", [P, NB, HEADS])
        s.rcnt = sb("rcnt", [P, NB])
        s.has = sb("has", [P, NB])
        s.lin1 = sb("lin1", [P, P])
        s.fc1 = sb("fc1", [8, 64])
        s.fc2 = sb("fc2", [64, P])
        s.lin2s = sb("lin2s", [2 * MUL, MUL])
        s.lin2v = sb("lin2v", [2 * MUL, MUL])
        s.w = [sb("w0", [P, HID]), sb("w1", [P, 2 * HID]), sb("w2", [P, 2 * HID])]
        s.w3 = sb("w3", [P, 2 * D])
        s.b = [sb(f"b{l}", [P, HID]) for l in range(3)]
        s.gain = [sb(f"gain{l}", [P, HID]) for l in range(3)]
        s.shift = [sb(f"shift{l}", [P, HID]) for l in range(3)]
        s.b3 = sb("b3", [P, D])
        s.sig = sb("sig", [P, 3])
        s.wself, s.wneigh = sb("wself", [P, D]), sb("wneigh", [P, D])
        s.bself, s.bneigh = sb("bself", [P, D]), sb("bneigh", [P, D])
        s.wg, s.wdst = sb("wg", [P, D + 4]), sb("wdst", [P, D])
        s.att, s.attw = sb("att", [P, 2, D]), sb("attw", [P, 2, D])
        s.bias, s.prelu = sb("bias", [P, D]), sb("prelu", [P, D])
        two = lambda ap: ap.rearrange("(a p) n -> p a n", p=P)
        each = lambda ap: ap.partition_broadcast(P)
        halves = lambda t: t[:, :].rearrange("p (a n) -> p a n", a=2)
        s.weights = [(s.lin1[0:MUL, 0:MUL], A["L0_gnn_w_lin1_s"]),
                     (s.fc1[:, :], A["L0_gnn_fc_w1"]), (s.fc2[:, :], A["L0_gnn_fc_w2"]),
                     (s.lin2s[0:MUL, :], A["L0_gnn_w_lin2_s"][MUL:2 * MUL, :]),
                     (s.lin2s[MUL:2 * MUL, :], A["L0_gnn_w_lin2_s"][0:MUL, :]),
                     (s.lin2v[:, :], A["L0_gnn_w_lin2_v"]),
                     (s.w[0][:, :], A["L1_gnn_W0"]), (halves(s.w[1]), two(A["L1_gnn_W1"])),
                     (halves(s.w[2]), two(A["L1_gnn_W2"])), (halves(s.w3), two(A["L1_gnn_W3"])),
                     (s.b3[:, :], each(A["L1_gnn_b3"])),
                     (s.wself[:, :], A["WsT"]), (s.wneigh[:, :], A["WnT"]),
                     (s.bself[:, :], each(A["L2_gnn_b_self"])), (s.bneigh[:, :], each(A["L2_gnn_b_neigh"])),
                     (s.wg[:, 0:D], A["L3_gnn_W_src"]), (s.wdst[:, :], A["L3_gnn_W_dst"]),
                     (s.att[:, 0, :], each(A["L3_gnn_att_src"].rearrange("h u -> (h u)"))),
                     (s.att[:, 1, :], each(A["L3_gnn_att_dst"].rearrange("h u -> (h u)"))),
                     (s.bias[:, :], each(A["L3_gnn_bias"])), (s.prelu[:, :], each(A["L3_gnn_prelu_w"]))]
        for i in range(3):
            s.weights += [(s.lin1[MUL + i:P:3, MUL * (i + 1):MUL * (i + 2)], A["L0_gnn_w_lin1_v"]),
                          (s.b[i][:, :], each(A[f"L1_gnn_b{i}"])), (s.gain[i][:, :], each(A[f"L1_gnn_g{i}"])),
                          (s.shift[i][:, :], each(A[f"L1_gnn_beta{i}"])), (s.sig[:, i:i + 1], each(A[f"L1_gnn_a{i}"]))]
        dram = lambda name, shape: nc.dram_tensor(name, shape, F32, kind="Internal").ap()
        s.dst_rows = dram("dst_rows", (NCH * P, PW))
        s.src_rows = dram("src_rows", (NCH * P, 2))
        t0, t1 = dram("table_lin1", (NB * P, D)), dram("table_gcn0", (NB * P, D))
        t2, t3 = dram("table_gcn1", (NB * P, HID)), dram("table_gcn2", (NB * P, HID))
        t4, t5 = dram("table_gcn3", (NB * P, D)), dram("table_mean", (NB * P, D))
        t6 = dram("table_gat", (NB * P, D + HEADS))
        s.prefilled = c.sem("rows_prefilled")
        s.attr_loaded = c.sem("edge_vectors_loaded")
        s.keys_loaded = c.sem("keys_loaded")
        s.counted, s.summed, s.ended = c.sem("bins_counted"), c.sem("bins_summed"), c.sem("bins_ended")
        s.turned, s.passed, s.binned = c.sem("ends_turned"), c.sem("ends_passed"), c.sem("chunks_binned")
        m = s.m = Scratch()
        m.h_mm = c.sem("mlp_hidden_multiplied")
        m.silu = c.sem("mlp_hidden_ready")
        m.w_mm = c.sem("mlp_weights_multiplied")
        m.copied = c.sem("payload_ready")
        m.masked = c.sem("masks_ready")
        m.flipped = c.sem("masked_scores_turned")
        m.maxed = c.sem("running_maxima_ready")
        m.factored = c.sem("factors_ready")
        m.dotted = c.sem("vectors_multiplied")
        m.small = c.sem("small_rows_ready")
        m.kept = c.sem("small_fields_kept")
        m.prod = c.sem("tensor_products_ready")
        m.scaled = c.sem("scaled_ready")
        m.fed = c.sem("tile_fed")
        m.turned = c.sem("tile_turned")
        m.back = c.sem("turned_tile_back")
        m.multiplied = c.sem("tile_multiplied")
        m.taken = c.sem("tile_taken")
        m.rooted = c.sem("root_taken")
        m.moments = c.sem("moments_ready")
        m.part = c.sem("segment_ready")
        m.centred = c.sem("segment_centred")
        m.shifted = c.sem("segment_shifted")
        m.cut = c.sem("segment_cut")
        m.powered = c.sem("exponential_taken")
        m.reduced = c.sem("scores_reduced")
        m.looked = c.sem("node_scores_looked_up")
        m.scored = c.sem("edge_scores_ready")
        m.weighted = c.sem("rows_weighted")
        m.ea = [c.sem(f"edge_scalars_loaded_{h}") for h in range(2)]
        m.sc = [c.sem(f"rows_scattered_{h}") for h in range(2)]
        m.ss = [c.sem(f"small_rows_scattered_{h}") for h in range(2)]
        m.pay = [c.sem(f"payload_loaded_{r}") for r in range(4)]
        run(c, A, s, out, (t0, t1, t2, t3, t4, t5, t6), upto)


def run(c, A, s, out, tables, upto):
    nc = c.nc
    t0, t1, t2, t3, t4, t5, t6 = tables
    ps, acc, x = c.ps, c.acc, c.x
    v = nc.vector

    def flat(ap):
        return ap.rearrange("p a b -> p (a b)")

    def dump():
        with nc.Block() as block:
            @block.sync
            def _(sp):
                sp.dma_start(tiles(out[0:(NT - 1) * P, :], 0, 0), x[:, 0:NT - 1, :]).then_inc(c.store.sem, 16)
                sp.dma_start(out[(NT - 1) * P:N, :], x[0:LASTN, NT - 1, :]).then_inc(c.store.sem, 16)
                sp.wait_ge(c.store.sem, c.store.n + 32)

    setup(c, A, s)
    sort_dst(c, A, s)
    prepare_weights(c, s)
    scatter_dst(c, A, s)
    scatter_src(c, s)

    def feed_x(k, slot):
        return nc.scalar.activation(s.u[:, slot, 0:D], flat(x[:, one(k), :]), ACT.Copy)

    def take_rows(st, k, bank):
        return v.tensor_copy(flat(acc[:, one(k), 0:D]), ps[:, bank, 0:D])
    node_product(c, s, feed_x, 1, P, [(0, s.lin1[:, :], 0, D, True, True)], 0, take_rows)
    write_table(c, acc[:, :, 0:D], t0, D)
    with nc.Block() as block:
        @block.vector
        def _(dve):
            v.memset(acc[:, :, :], 0.0)
            Steps(dve, c.dve)(v.memset(s.prod[:, :, :, :], 1.0))
    messages(c, s, t0)
    degrees(c, s)

    def feed_msg(k, slot):
        return nc.scalar.activation(s.u[:, slot, :].rearrange("p (g w) -> p g w", g=4),
                                    flat(acc[:, one(k), :]).rearrange("p (g w) -> p g w", g=4)[:, :, 0:2 * MUL], ACT.Copy)

    def take_msg(st, k, bank):
        xs = flat(x[:, one(k), 0:MUL])
        xv = flat(x[:, one(k), MUL:D]).rearrange("p (u i) -> p i u", i=3)
        st(v.tensor_tensor(xs, xs, ps[:, bank, 0:MUL], ALU.add))
        st(v.tensor_tensor(xv, xv, ps[:, bank, MUL:D].rearrange("p (i u) -> p i u", i=3), ALU.add))
        return stats(c, s, st, k, flat(x[:, one(k), :]))
    node_product(c, s, feed_msg, 4, 2 * MUL,
                 [(g, (s.lin2v if g else s.lin2s)[:, :], MUL * g, MUL * g + MUL, True, True) for g in range(4)],
                 2, take_msg)
    normalise(c, s, self_term=True, table=t1)
    if upto == 0:
        return dump()

    def feed_scaled(width):
        def feed(k, slot):
            return nc.scalar.activation(s.u[:, slot, 0:width], flat(acc[:, one(k), 0:width]), ACT.Copy,
                                        scale=c.dinv[:, one(k)])
        return feed

    def take_conv(l):
        def take(st, k, bank):
            y = flat(acc[:, one(k), 0:HID])
            st(v.tensor_tensor(y, ps[:, bank, 0:HID], s.b[l][:, :], ALU.add))
            return stats(c, s, st, k, y)
        return take
    aggregate(c, "dst", t1, D, D)
    node_product(c, s, feed_scaled(D), 1, P, [(0, s.w[0][:, :], 0, HID, True, True)], 1, take_conv(0))
    conv_norm(c, s, 0, t2)
    for l, tin, tout in ((1, t2, t3), (2, t3, None)):
        aggregate(c, "dst", tin, HID, HID)
        node_product(c, s, feed_scaled(HID), 2, P,
                     [(a, s.w[l][:, a * HID:(a + 1) * HID], 0, HID, a == 0, a == 1) for a in range(2)], 1, take_conv(l))
        conv_norm(c, s, l, tout)

    def feed_acc(k, slot):
        return nc.scalar.activation(s.u[:, slot, :], flat(acc[:, one(k), 0:HID]), ACT.Copy)
    node_product(c, s, feed_acc, 2, P, [(a, s.w3[:, a * D:(a + 1) * D], 0, D, a == 0, a == 1) for a in range(2)],
                 0, take_rows)
    write_table(c, acc[:, :, 0:D], t4, D)
    aggregate(c, "dst", t4, D, D)
    add_gcn(c, s)
    normalise(c, s, table=t5, clear=True)
    if upto == 1:
        return dump()

    with nc.Block() as block:
        @block.vector
        def _(dve):
            Steps(dve, c.dve)(v.memset(c.rows[:, :, :, D:D + 1], 1.0))
    aggregate(c, "src", t5, D, D + 1)
    with nc.Block() as block:
        @block.vector
        def _(dve):
            st = Steps(dve, c.dve)
            st(v.tensor_scalar(s.has[:, :], acc[:, :, D], 0.0, None, ALU.is_gt))
            st(v.tensor_scalar(s.rcnt[:, :], acc[:, :, D], 1.0, None, ALU.max)).wait()
            st(v.reciprocal(s.rcnt[:, :], s.rcnt[:, :]))

    def feed_mean(k, slot):
        nc.scalar.activation(s.u[:, slot, 0:D], flat(acc[:, one(k), 0:D]), ACT.Copy, scale=s.rcnt[:, one(k)])
        return nc.scalar.activation(s.u[:, slot, D:2 * D], flat(x[:, one(k), :]), ACT.Copy)

    def take_mean(st, k, bank):
        t, y = s.ex[:, 0, 0, 0:D], flat(x[:, one(k), :])
        st(v.scalar_tensor_tensor(t, s.bneigh[:, :], s.has[:, one(k)], ps[:, bank, 0:D], ALU.mult, ALU.add)).wait()
        st(v.tensor_tensor(t, t, s.bself[:, :], ALU.add)).wait()
        st(v.scalar_tensor_tensor(y, t, 0.0, y, ALU.max, ALU.add))
        return stats(c, s, st, k, y)
    node_product(c, s, feed_mean, 2, P, [(0, s.wneigh[:, :], 0, D, True, False), (1, s.wself[:, :], 0, D, False, True)],
                 3, take_mean)
    normalise(c, s, table=t5)
    if upto == 2:
        return dump()

    def take_gat(st, k, bank):
        to = flat(acc[:, one(k), 0:D + HEADS]).rearrange("p (h u) -> p h u", h=HEADS)
        st(v.tensor_copy(to[:, :, 0:CH], ps[:, bank, 0:D].rearrange("p (h u) -> p h u", h=HEADS)))
        st(v.tensor_copy(to[:, :, CH], ps[:, bank, D:D + HEADS]))
        return v.tensor_copy(flat(s.nt[:, one(k), :]), ps[:, bank, D + HEADS:D + 2 * HEADS])
    node_product(c, s, feed_x, 1, P, [(0, s.wg[:, :], 0, D + 4, True, True)], 2, take_gat)
    write_table(c, acc[:, :, 0:D + HEADS], t6, D + HEADS)
    bin_starts(c, s)
    attend(c, s, t6)
    add_gat(c, s)
    normalise(c, s, out=out)


_PLAIN = ["x", "L0_gnn_w_lin1_s", "L0_gnn_w_lin1_v", "L0_gnn_fc_w1", "L0_gnn_fc_w2", "L0_gnn_w_lin2_s",
          "L0_gnn_w_lin2_v", "L1_gnn_W0", "L1_gnn_b0", "L1_gnn_W1", "L1_gnn_b1", "L1_gnn_W2", "L1_gnn_b2",
          "L1_gnn_W3", "L1_gnn_b3", "L1_gnn_a0", "L1_gnn_a1", "L1_gnn_a2", "L1_gnn_g0", "L1_gnn_beta0",
          "L1_gnn_g1", "L1_gnn_beta1", "L1_gnn_g2", "L1_gnn_beta2", "L2_gnn_b_self", "L2_gnn_b_neigh",
          "L3_gnn_W_src", "L3_gnn_W_dst", "L3_gnn_att_src", "L3_gnn_att_dst", "L3_gnn_bias", "L3_gnn_prelu_w"]
UPTO = None


def kernel(**inputs):
    import concourse.bacc as _bacc
    from concourse.bass_utils import run_bass_kernel_spmd as _run

    whole = (TC - 1) * P
    arrays = {n: np.ascontiguousarray(inputs[n]) for n in _PLAIN}
    for k in ("dst", "src"):
        e = np.ascontiguousarray(inputs[k])
        arrays[k + "_main"] = np.ascontiguousarray(e[:whole].reshape(TC - 1, P).T)
        arrays[k + "_tail"] = np.ascontiguousarray(e[whole:].reshape(TAIL, 1))
    a = np.ascontiguousarray(inputs["edge_attr_4"])
    arrays["ea4_main"] = np.ascontiguousarray(a[:whole].reshape(TC - 1, P, 4).transpose(1, 0, 2))
    arrays["ea4_tail"] = np.ascontiguousarray(a[whole:])
    arrays["ea8"] = np.ascontiguousarray(np.ascontiguousarray(inputs["edge_attr_8"]).T)
    arrays["WsT"] = np.ascontiguousarray(np.ascontiguousarray(inputs["L2_gnn_W_self"]).T)
    arrays["WnT"] = np.ascontiguousarray(np.ascontiguousarray(inputs["L2_gnn_W_neigh"]).T)
    nc = _bacc.Bacc("TRN2", target_bir_lowering=False, num_devices=1)
    aps = {n: nc.dram_tensor("in_" + n, a.shape, mybir.dt.from_np(a.dtype), kind="ExternalInput").ap()
           for n, a in arrays.items()}
    out = nc.dram_tensor("out_x", (N, D), F32, kind="ExternalOutput").ap()
    gnn(nc, aps, out, UPTO)
    r = _run(nc, [{"in_" + n: a for n, a in arrays.items()}], core_ids=[0])
    return r.results[0]["out_x"]
```
